# Optimizing a Trainium2 kernel written in Bass

```python
import numpy as np
import jax
import jax.numpy as jnp

def _softmax(x, axis=-1):
    return jax.nn.softmax(x, axis=axis)
def _gelu(x):
    return jax.nn.gelu(x, approximate=True)
def _silu(x):
    return jax.nn.silu(x)
def _sigmoid(x):
    return jax.nn.sigmoid(x)
def _layernorm(x, axis=-1, eps=1e-5):
    m = jnp.mean(x, axis=axis, keepdims=True)
    v = jnp.var(x, axis=axis, keepdims=True)
    return (x - m) / jnp.sqrt(v + eps)
def _scatter_add(tgt, idx, src, axis=0):
    return tgt.at[idx].add(src)
def _segment_sum(src, seg, n):
    return jax.ops.segment_sum(src, seg, n)

kernel_name = 'mk_metaformer_d4_conv_nhwc128_41fd95'

def setup_inputs(seed: int = 0):
    np.random.seed(seed)
    _w = jnp.asarray
    def _rec_inputs():
        import jax
        import jax.numpy as jnp
        _gk = jax.random.key(seed)
        x = 7.22e-05 + 1 * jax.random.normal(jax.random.fold_in(_gk, 1), (1, 256, 256, 128), jnp.float32)
        return x
    x = _rec_inputs()
    def _L0_conv_setup():
        import jax, jax.numpy as jnp
        import numpy as np
        C_Z = 128
        C_HIDDEN = 32
        N_HEAD = 4
        HC = N_HEAD * C_HIDDEN
        LN_EPS = 1e-05
        key = jax.random.key(seed)
        ks = jax.random.split(key, 8)
        b, n = (1, 256)
        s = 1.0 / np.sqrt(C_Z)
        return {'z_ij': jax.random.normal(ks[0], (b, n, n, C_Z), dtype=jnp.float32), 'ln_gamma': jnp.ones((C_Z,), dtype=jnp.float32), 'ln_beta': jnp.zeros((C_Z,), dtype=jnp.float32), 'Wq': jax.random.normal(ks[1], (C_Z, HC), dtype=jnp.float32) * s, 'Wk': jax.random.normal(ks[2], (C_Z, HC), dtype=jnp.float32) * s, 'Wv': jax.random.normal(ks[3], (C_Z, HC), dtype=jnp.float32) * s, 'Wb': jax.random.normal(ks[4], (C_Z, N_HEAD), dtype=jnp.float32) * s, 'Wg': jax.random.normal(ks[5], (C_Z, HC), dtype=jnp.float32) * s, 'Wout': jax.random.normal(ks[6], (HC, C_Z), dtype=jnp.float32) * (1.0 / np.sqrt(HC))}
    _L0_conv_all = _L0_conv_setup()
    _L0_conv_in = {k: v for k, v in _L0_conv_all.items() if k in ('ln_gamma', 'ln_beta', 'Wq', 'Wk', 'Wv', 'Wb', 'Wg', 'Wout', )}
    del _L0_conv_all

    def _L0_ffn_setup():
        import jax, jax.numpy as jnp
        import numpy as np
        B, S, D, E, H, O, K = (512, 2048, 128, 64, 512, 128, 8)
        key = jax.random.key(seed)
        k0, k1, k2, k3 = jax.random.split(key, 4)
        x = jax.random.normal(k0, (B, S, D), dtype=jnp.float32)
        gate_w = jax.random.normal(k1, (E, D), dtype=jnp.float32) * (1.0 / np.sqrt(D))
        gate_b = jnp.zeros((E,), dtype=jnp.float32)
        weight1 = jax.random.uniform(k2, (E, D + 1, H), dtype=jnp.float32, minval=-1.0, maxval=1.0) * (1.0 / np.sqrt(D + 1))
        weight2 = jax.random.uniform(k3, (E, H + 1, O), dtype=jnp.float32, minval=-1.0, maxval=1.0) * (1.0 / np.sqrt(H + 1))
        return {'x': x, 'gate_w': gate_w, 'gate_b': gate_b, 'weight1': weight1, 'weight2': weight2}
    _L0_ffn_all = _L0_ffn_setup()
    _L0_ffn_in = {k: v for k, v in _L0_ffn_all.items() if k in ('gate_w', 'gate_b', 'weight1', 'weight2', )}
    del _L0_ffn_all

    def _L1_conv_setup():
        import jax, jax.numpy as jnp
        import numpy as np
        from jax import lax
        H = 128

        def _ema_scan(x):
            xt = jnp.moveaxis(x, 1, 0)

            def step(s, xi):
                s = s * 0.9 + xi * 0.1
                return (s, s)
            _, ys = lax.scan(step, jnp.zeros_like(xt[0]), xt)
            return jnp.moveaxis(ys, 0, 1)
        key = jax.random.key(seed)
        k1, k2, k3, k4, k5 = jax.random.split(key, 5)
        B, T, N = (4, 96, 512)
        x = jax.random.normal(k1, (B, T, N, H), dtype=jnp.float32)
        s = 1.0 / np.sqrt(H)
        W_exp = jax.random.uniform(k2, (2 * H, H), jnp.float32, -s, s)
        b_exp = jax.random.uniform(k3, (2 * H,), jnp.float32, -s, s)
        W_con = jax.random.uniform(k4, (H, H), jnp.float32, -s, s)
        b_con = jax.random.uniform(k5, (H,), jnp.float32, -s, s)
        return {'spatial_temporal_representation': x, 'W_exp': W_exp, 'b_exp': b_exp, 'W_con': W_con, 'b_con': b_con}
    _L1_conv_all = _L1_conv_setup()
    _L1_conv_in = {k: v for k, v in _L1_conv_all.items() if k in ('W_exp', 'b_exp', 'W_con', 'b_con', )}
    del _L1_conv_all

    def _L1_ffn_setup():
        import jax, jax.numpy as jnp
        import numpy as np
        BN_EPS = 1e-05
        key = jax.random.key(seed)
        k1, k2, k3 = jax.random.split(key, 3)
        B, T, I, H = (64, 2048, 128, 128)
        x = jax.random.normal(k1, (B, T, I), dtype=jnp.float32)
        W = jax.random.normal(k2, (H, I), dtype=jnp.float32) * (1.0 / np.sqrt(I))
        V = jnp.linalg.qr(jax.random.normal(k3, (H, H), dtype=jnp.float32))[0]
        gamma = jnp.ones((H,), dtype=jnp.float32)
        beta = jnp.zeros((H,), dtype=jnp.float32)
        return {'x': x, 'W': W, 'V': V, 'gamma': gamma, 'beta': beta}
    _L1_ffn_all = _L1_ffn_setup()
    _L1_ffn_in = {k: v for k, v in _L1_ffn_all.items() if k in ('W', 'V', 'gamma', 'beta', )}
    del _L1_ffn_all

    def _L2_conv_setup():
        import jax, jax.numpy as jnp
        import numpy as np
        B, H, W, C = (16, 96, 96, 128)
        FOCAL_LEVEL = 3
        FOCAL_WINDOW = 3
        FOCAL_FACTOR = 2
        LN_EPS = 0.001

        def dwconv_same(x, k):
            return jax.lax.conv_general_dilated(x, k, window_strides=(1, 1), padding='SAME', dimension_numbers=('NHWC', 'HWIO', 'NHWC'), feature_group_count=x.shape[-1])
        key = jax.random.key(seed)
        ks = jax.random.split(key, 12)
        s = 0.02
        out_f = 2 * C + (FOCAL_LEVEL + 1)
        inp = {'x': jax.random.normal(ks[0], (B, H, W, C), dtype=jnp.float32), 'Wf': jax.random.normal(ks[1], (C, out_f), dtype=jnp.float32) * s, 'bf': jnp.zeros((out_f,), dtype=jnp.float32), 'Wh': jax.random.normal(ks[2], (C, C), dtype=jnp.float32) * s, 'bh': jnp.zeros((C,), dtype=jnp.float32), 'gamma': jnp.ones((C,), dtype=jnp.float32), 'beta': jnp.zeros((C,), dtype=jnp.float32), 'Wp': jax.random.normal(ks[3], (C, C), dtype=jnp.float32) * s, 'bp': jnp.zeros((C,), dtype=jnp.float32)}
        for l in range(FOCAL_LEVEL):
            kk = FOCAL_FACTOR * l + FOCAL_WINDOW
            inp[f'k{l}'] = jax.random.normal(ks[4 + l], (kk, kk, 1, C), dtype=jnp.float32) * s
        return inp
    _L2_conv_all = _L2_conv_setup()
    _L2_conv_in = {k: v for k, v in _L2_conv_all.items() if k in ('Wf', 'bf', 'k0', 'k1', 'k2', 'Wh', 'bh', 'gamma', 'beta', 'Wp', 'bp', )}
    del _L2_conv_all

    def _L2_ffn_setup():
        import jax, jax.numpy as jnp
        import numpy as np
        B, S, D, E, H, O, K = (512, 2048, 128, 64, 512, 128, 8)
        key = jax.random.key(seed)
        k0, k1, k2, k3 = jax.random.split(key, 4)
        x = jax.random.normal(k0, (B, S, D), dtype=jnp.float32)
        gate_w = jax.random.normal(k1, (E, D), dtype=jnp.float32) * (1.0 / np.sqrt(D))
        gate_b = jnp.zeros((E,), dtype=jnp.float32)
        weight1 = jax.random.uniform(k2, (E, D + 1, H), dtype=jnp.float32, minval=-1.0, maxval=1.0) * (1.0 / np.sqrt(D + 1))
        weight2 = jax.random.uniform(k3, (E, H + 1, O), dtype=jnp.float32, minval=-1.0, maxval=1.0) * (1.0 / np.sqrt(H + 1))
        return {'x': x, 'gate_w': gate_w, 'gate_b': gate_b, 'weight1': weight1, 'weight2': weight2}
    _L2_ffn_all = _L2_ffn_setup()
    _L2_ffn_in = {k: v for k, v in _L2_ffn_all.items() if k in ('gate_w', 'gate_b', 'weight1', 'weight2', )}
    del _L2_ffn_all

    def _L3_conv_setup():
        import jax, jax.numpy as jnp
        import numpy as np
        from jax import lax
        KH, KW = (3, 3)
        KK = KH * KW
        PAD = 1

        def _deform_conv(x, kernel, bias, offset_w, offset_b):
            B, H, W, C = x.shape
            F = kernel.shape[-1]
            offsets = lax.conv_general_dilated(x, offset_w, window_strides=(1, 1), padding='SAME', dimension_numbers=('NHWC', 'HWIO', 'NHWC')) + offset_b
            offsets = offsets.reshape(B, H, W, KK, 2)
            dy, dx = (offsets[..., 0], offsets[..., 1])
            ky = jnp.repeat(jnp.arange(KH, dtype=jnp.float32) - PAD, KW)
            kx = jnp.tile(jnp.arange(KW, dtype=jnp.float32) - PAD, KH)
            py = jnp.arange(H, dtype=jnp.float32)[None, :, None, None] + ky + dy
            px = jnp.arange(W, dtype=jnp.float32)[None, None, :, None] + kx + dx
            y0 = jnp.floor(py)
            x0 = jnp.floor(px)
            wy = py - y0
            wx = px - x0
            y0i = y0.astype(jnp.int32)
            x0i = x0.astype(jnp.int32)
            b_idx = jnp.arange(B)[:, None, None, None]

            def gather(yi, xi):
                valid = (yi >= 0) & (yi < H) & (xi >= 0) & (xi < W)
                yc = jnp.clip(yi, 0, H - 1)
                xc = jnp.clip(xi, 0, W - 1)
                v = x[b_idx, yc, xc]
                return v * valid[..., None].astype(x.dtype)
            val = gather(y0i, x0i) * ((1 - wy) * (1 - wx))[..., None] + gather(y0i, x0i + 1) * ((1 - wy) * wx)[..., None] + gather(y0i + 1, x0i) * (wy * (1 - wx))[..., None] + gather(y0i + 1, x0i + 1) * (wy * wx)[..., None]
            out = jnp.einsum('bhwkc,kcf->bhwf', val, kernel.reshape(KK, C, F))
            return out + bias
        key = jax.random.key(seed)
        k1, k2, k3 = jax.random.split(key, 3)
        B, H, W, C, F = (8, 64, 64, 128, 128)
        x = jax.random.normal(k1, (B, H, W, C), dtype=jnp.float32)
        kernel = jax.random.normal(k2, (KH, KW, C, F), dtype=jnp.float32) * 0.05
        bias = jnp.zeros((F,), dtype=jnp.float32)
        offset_w = jax.random.normal(k3, (KH, KW, C, 2 * KK), dtype=jnp.float32) * 0.01
        offset_b = jnp.zeros((2 * KK,), dtype=jnp.float32)
        return {'x': x, 'kernel': kernel, 'bias': bias, 'offset_w': offset_w, 'offset_b': offset_b}
    _L3_conv_all = _L3_conv_setup()
    _L3_conv_in = {k: v for k, v in _L3_conv_all.items() if k in ('kernel', 'bias', 'offset_w', 'offset_b', )}
    del _L3_conv_all

    def _L3_ffn_setup():
        import jax, jax.numpy as jnp
        import numpy as np
        B, S, D, E, H, O, K = (512, 2048, 128, 64, 512, 128, 8)
        key = jax.random.key(seed)
        k0, k1, k2, k3 = jax.random.split(key, 4)
        x = jax.random.normal(k0, (B, S, D), dtype=jnp.float32)
        gate_w = jax.random.normal(k1, (E, D), dtype=jnp.float32) * (1.0 / np.sqrt(D))
        gate_b = jnp.zeros((E,), dtype=jnp.float32)
        weight1 = jax.random.uniform(k2, (E, D + 1, H), dtype=jnp.float32, minval=-1.0, maxval=1.0) * (1.0 / np.sqrt(D + 1))
        weight2 = jax.random.uniform(k3, (E, H + 1, O), dtype=jnp.float32, minval=-1.0, maxval=1.0) * (1.0 / np.sqrt(H + 1))
        return {'x': x, 'gate_w': gate_w, 'gate_b': gate_b, 'weight1': weight1, 'weight2': weight2}
    _L3_ffn_all = _L3_ffn_setup()
    _L3_ffn_in = {k: v for k, v in _L3_ffn_all.items() if k in ('gate_w', 'gate_b', 'weight1', 'weight2', )}
    del _L3_ffn_all

    return {
        "x": x,
        "L0_conv_ln_gamma": _L0_conv_in["ln_gamma"],
        "L0_conv_ln_beta": _L0_conv_in["ln_beta"],
        "L0_conv_Wq": _L0_conv_in["Wq"],
        "L0_conv_Wk": _L0_conv_in["Wk"],
        "L0_conv_Wv": _L0_conv_in["Wv"],
        "L0_conv_Wb": _L0_conv_in["Wb"],
        "L0_conv_Wg": _L0_conv_in["Wg"],
        "L0_conv_Wout": _L0_conv_in["Wout"],
        "L0_ffn_gate_w": _L0_ffn_in["gate_w"],
        "L0_ffn_gate_b": _L0_ffn_in["gate_b"],
        "L0_ffn_weight1": _L0_ffn_in["weight1"],
        "L0_ffn_weight2": _L0_ffn_in["weight2"],
        "L1_conv_W_exp": _L1_conv_in["W_exp"],
        "L1_conv_b_exp": _L1_conv_in["b_exp"],
        "L1_conv_W_con": _L1_conv_in["W_con"],
        "L1_conv_b_con": _L1_conv_in["b_con"],
        "L1_ffn_W": _L1_ffn_in["W"],
        "L1_ffn_V": _L1_ffn_in["V"],
        "L1_ffn_gamma": _L1_ffn_in["gamma"],
        "L1_ffn_beta": _L1_ffn_in["beta"],
        "L2_conv_Wf": _L2_conv_in["Wf"],
        "L2_conv_bf": _L2_conv_in["bf"],
        "L2_conv_k0": _L2_conv_in["k0"],
        "L2_conv_k1": _L2_conv_in["k1"],
        "L2_conv_k2": _L2_conv_in["k2"],
        "L2_conv_Wh": _L2_conv_in["Wh"],
        "L2_conv_bh": _L2_conv_in["bh"],
        "L2_conv_gamma": _L2_conv_in["gamma"],
        "L2_conv_beta": _L2_conv_in["beta"],
        "L2_conv_Wp": _L2_conv_in["Wp"],
        "L2_conv_bp": _L2_conv_in["bp"],
        "L2_ffn_gate_w": _L2_ffn_in["gate_w"],
        "L2_ffn_gate_b": _L2_ffn_in["gate_b"],
        "L2_ffn_weight1": _L2_ffn_in["weight1"],
        "L2_ffn_weight2": _L2_ffn_in["weight2"],
        "L3_conv_kernel": _L3_conv_in["kernel"],
        "L3_conv_bias": _L3_conv_in["bias"],
        "L3_conv_offset_w": _L3_conv_in["offset_w"],
        "L3_conv_offset_b": _L3_conv_in["offset_b"],
        "L3_ffn_gate_w": _L3_ffn_in["gate_w"],
        "L3_ffn_gate_b": _L3_ffn_in["gate_b"],
        "L3_ffn_weight1": _L3_ffn_in["weight1"],
        "L3_ffn_weight2": _L3_ffn_in["weight2"],
    }

def reference(x, L0_conv_ln_gamma, L0_conv_ln_beta, L0_conv_Wq, L0_conv_Wk, L0_conv_Wv, L0_conv_Wb, L0_conv_Wg, L0_conv_Wout, L0_ffn_gate_w, L0_ffn_gate_b, L0_ffn_weight1, L0_ffn_weight2, L1_conv_W_exp, L1_conv_b_exp, L1_conv_W_con, L1_conv_b_con, L1_ffn_W, L1_ffn_V, L1_ffn_gamma, L1_ffn_beta, L2_conv_Wf, L2_conv_bf, L2_conv_k0, L2_conv_k1, L2_conv_k2, L2_conv_Wh, L2_conv_bh, L2_conv_gamma, L2_conv_beta, L2_conv_Wp, L2_conv_bp, L2_ffn_gate_w, L2_ffn_gate_b, L2_ffn_weight1, L2_ffn_weight2, L3_conv_kernel, L3_conv_bias, L3_conv_offset_w, L3_conv_offset_b, L3_ffn_gate_w, L3_ffn_gate_b, L3_ffn_weight1, L3_ffn_weight2):
    import jax
    import jax.numpy as jnp
    def _L0_conv_ref(z_ij, ln_gamma, ln_beta, Wq, Wk, Wv, Wb, Wg, Wout):
        import jax, jax.numpy as jnp
        import numpy as np
        C_Z = 128
        C_HIDDEN = 32
        N_HEAD = 4
        HC = N_HEAD * C_HIDDEN
        LN_EPS = 1e-05
        b, n, _, _ = z_ij.shape
        mu = jnp.mean(z_ij, axis=-1, keepdims=True)
        var = jnp.var(z_ij, axis=-1, keepdims=True)
        z = (z_ij - mu) * jax.lax.rsqrt(var + LN_EPS) * ln_gamma + ln_beta

        def heads(x):
            return x.reshape(b, n, n, N_HEAD, C_HIDDEN)
        q = heads(z @ Wq)
        k = heads(z @ Wk)
        v = heads(z @ Wv)
        bias = z @ Wb
        g = jax.nn.sigmoid(heads(z @ Wg))
        scores = jnp.einsum('bijhd,bikhd->bijkh', q, k) / np.sqrt(C_HIDDEN)
        scores = scores + bias[:, None]
        a = jax.nn.softmax(scores, axis=-2)
        o = jnp.einsum('bijkh,bikhd->bijhd', a, v)
        o = (g * o).reshape(b, n, n, HC)
        return o @ Wout

    def _L0_ffn_ref(x, gate_w, gate_b, weight1, weight2):
        import jax, jax.numpy as jnp
        import numpy as np
        B, S, D, E, H, O, K = (512, 2048, 128, 64, 512, 128, 8)
        Bn, Sn, Dn = x.shape
        logits = jnp.einsum('bsd,ed->bse', x, gate_w) + gate_b
        probs = jax.nn.softmax(logits, axis=1)
        vals, idx = jax.lax.top_k(probs.transpose(0, 2, 1), K)
        topv = vals.transpose(0, 2, 1)
        topi = idx.transpose(0, 2, 1)
        flat_idx = topi.reshape(Bn, K * E)
        gathered = jnp.take_along_axis(x, flat_idx[:, :, None], axis=1)
        gathered = gathered.reshape(Bn, K, E, Dn)
        pooled = jnp.einsum('bked,bke->bed', gathered, topv)
        ones = jnp.ones((E, Bn, 1), dtype=x.dtype)
        h = jnp.concatenate([pooled.transpose(1, 0, 2), ones], axis=-1)
        h = jax.nn.gelu(jnp.einsum('ebd,edh->ebh', h, weight1), approximate=False)
        h = jnp.concatenate([h, ones], axis=-1)
        out = jnp.einsum('ebh,eho->ebo', h, weight2)
        out = out.transpose(1, 0, 2)
        weighted = jnp.einsum('beo,bke->bkeo', out, topv).reshape(Bn, K * E, O)
        outputs = jnp.zeros((Bn, Sn, O), dtype=x.dtype)
        outputs = outputs.at[jnp.arange(Bn)[:, None], flat_idx].add(weighted)
        return outputs

    def _L1_conv_ref(spatial_temporal_representation, W_exp, b_exp, W_con, b_con):
        import jax, jax.numpy as jnp
        import numpy as np
        from jax import lax
        H = 128

        def _ema_scan(x):
            xt = jnp.moveaxis(x, 1, 0)

            def step(s, xi):
                s = s * 0.9 + xi * 0.1
                return (s, s)
            _, ys = lax.scan(step, jnp.zeros_like(xt[0]), xt)
            return jnp.moveaxis(ys, 0, 1)
        x = spatial_temporal_representation
        expanded = jnp.einsum('btnh,oh->btno', x, W_exp) + b_exp
        state_primary, state_gating = jnp.split(expanded, 2, axis=-1)
        gated_activation = jax.nn.sigmoid(_ema_scan(state_gating))
        out = jnp.einsum('btnh,oh->btno', state_primary * gated_activation, W_con) + b_con
        return out

    def _L1_ffn_ref(x, W, V, gamma, beta):
        import jax, jax.numpy as jnp
        import numpy as np
        BN_EPS = 1e-05
        B, T, H = (x.shape[0], x.shape[1], W.shape[0])
        Wx = jnp.einsum('bti,hi->bth', x, W)
        flat = Wx.reshape(B * T, H)
        mean = jnp.mean(flat, axis=0)
        var = jnp.var(flat, axis=0)
        Wx = ((flat - mean) * jax.lax.rsqrt(var + BN_EPS) * gamma + beta).reshape(B, T, H)
        Vt = V.T

        def step(yt, wx_t):
            yt = jax.nn.sigmoid(wx_t + yt @ Vt)
            return (yt, yt)
        y0 = jnp.zeros((B, H), dtype=Wx.dtype)
        _, ys = jax.lax.scan(step, y0, jnp.swapaxes(Wx, 0, 1))
        return jnp.swapaxes(ys, 0, 1)

    def _L2_conv_ref(x, Wf, bf, k0, k1, k2, Wh, bh, gamma, beta, Wp, bp):
        import jax, jax.numpy as jnp
        import numpy as np
        B, H, W, C = (16, 96, 96, 128)
        FOCAL_LEVEL = 3
        FOCAL_WINDOW = 3
        FOCAL_FACTOR = 2
        LN_EPS = 0.001

        def dwconv_same(x, k):
            return jax.lax.conv_general_dilated(x, k, window_strides=(1, 1), padding='SAME', dimension_numbers=('NHWC', 'HWIO', 'NHWC'), feature_group_count=x.shape[-1])
        gelu = lambda t: jax.nn.gelu(t, approximate=False)
        y = jnp.einsum('bhwc,cd->bhwd', x, Wf) + bf
        q = y[..., :C]
        ctx = y[..., C:2 * C]
        gates = y[..., 2 * C:]
        ctx_all = jnp.zeros_like(ctx)
        for l, k in enumerate((k0, k1, k2)):
            ctx = gelu(dwconv_same(ctx, k))
            ctx_all = ctx_all + ctx * gates[..., l:l + 1]
        ctx_global = gelu(jnp.mean(ctx, axis=(1, 2), keepdims=True))
        ctx_all = ctx_all + ctx_global * gates[..., FOCAL_LEVEL:]
        modulator = jnp.einsum('bhwc,cd->bhwd', ctx_all, Wh) + bh
        x_out = q * modulator
        mu = jnp.mean(x_out, axis=-1, keepdims=True)
        var = jnp.mean(jnp.square(x_out - mu), axis=-1, keepdims=True)
        x_out = (x_out - mu) * jax.lax.rsqrt(var + LN_EPS) * gamma + beta
        x_out = jnp.einsum('bhwc,cd->bhwd', x_out, Wp) + bp
        return x_out

    def _L2_ffn_ref(x, gate_w, gate_b, weight1, weight2):
        import jax, jax.numpy as jnp
        import numpy as np
        B, S, D, E, H, O, K = (512, 2048, 128, 64, 512, 128, 8)
        Bn, Sn, Dn = x.shape
        logits = jnp.einsum('bsd,ed->bse', x, gate_w) + gate_b
        probs = jax.nn.softmax(logits, axis=1)
        vals, idx = jax.lax.top_k(probs.transpose(0, 2, 1), K)
        topv = vals.transpose(0, 2, 1)
        topi = idx.transpose(0, 2, 1)
        flat_idx = topi.reshape(Bn, K * E)
        gathered = jnp.take_along_axis(x, flat_idx[:, :, None], axis=1)
        gathered = gathered.reshape(Bn, K, E, Dn)
        pooled = jnp.einsum('bked,bke->bed', gathered, topv)
        ones = jnp.ones((E, Bn, 1), dtype=x.dtype)
        h = jnp.concatenate([pooled.transpose(1, 0, 2), ones], axis=-1)
        h = jax.nn.gelu(jnp.einsum('ebd,edh->ebh', h, weight1), approximate=False)
        h = jnp.concatenate([h, ones], axis=-1)
        out = jnp.einsum('ebh,eho->ebo', h, weight2)
        out = out.transpose(1, 0, 2)
        weighted = jnp.einsum('beo,bke->bkeo', out, topv).reshape(Bn, K * E, O)
        outputs = jnp.zeros((Bn, Sn, O), dtype=x.dtype)
        outputs = outputs.at[jnp.arange(Bn)[:, None], flat_idx].add(weighted)
        return outputs

    def _L3_conv_ref(x, kernel, bias, offset_w, offset_b):
        import jax, jax.numpy as jnp
        import numpy as np
        from jax import lax
        KH, KW = (3, 3)
        KK = KH * KW
        PAD = 1

        def _deform_conv(x, kernel, bias, offset_w, offset_b):
            B, H, W, C = x.shape
            F = kernel.shape[-1]
            offsets = lax.conv_general_dilated(x, offset_w, window_strides=(1, 1), padding='SAME', dimension_numbers=('NHWC', 'HWIO', 'NHWC')) + offset_b
            offsets = offsets.reshape(B, H, W, KK, 2)
            dy, dx = (offsets[..., 0], offsets[..., 1])
            ky = jnp.repeat(jnp.arange(KH, dtype=jnp.float32) - PAD, KW)
            kx = jnp.tile(jnp.arange(KW, dtype=jnp.float32) - PAD, KH)
            py = jnp.arange(H, dtype=jnp.float32)[None, :, None, None] + ky + dy
            px = jnp.arange(W, dtype=jnp.float32)[None, None, :, None] + kx + dx
            y0 = jnp.floor(py)
            x0 = jnp.floor(px)
            wy = py - y0
            wx = px - x0
            y0i = y0.astype(jnp.int32)
            x0i = x0.astype(jnp.int32)
            b_idx = jnp.arange(B)[:, None, None, None]

            def gather(yi, xi):
                valid = (yi >= 0) & (yi < H) & (xi >= 0) & (xi < W)
                yc = jnp.clip(yi, 0, H - 1)
                xc = jnp.clip(xi, 0, W - 1)
                v = x[b_idx, yc, xc]
                return v * valid[..., None].astype(x.dtype)
            val = gather(y0i, x0i) * ((1 - wy) * (1 - wx))[..., None] + gather(y0i, x0i + 1) * ((1 - wy) * wx)[..., None] + gather(y0i + 1, x0i) * (wy * (1 - wx))[..., None] + gather(y0i + 1, x0i + 1) * (wy * wx)[..., None]
            out = jnp.einsum('bhwkc,kcf->bhwf', val, kernel.reshape(KK, C, F))
            return out + bias
        return _deform_conv(x, kernel, bias, offset_w, offset_b)

    def _L3_ffn_ref(x, gate_w, gate_b, weight1, weight2):
        import jax, jax.numpy as jnp
        import numpy as np
        B, S, D, E, H, O, K = (512, 2048, 128, 64, 512, 128, 8)
        Bn, Sn, Dn = x.shape
        logits = jnp.einsum('bsd,ed->bse', x, gate_w) + gate_b
        probs = jax.nn.softmax(logits, axis=1)
        vals, idx = jax.lax.top_k(probs.transpose(0, 2, 1), K)
        topv = vals.transpose(0, 2, 1)
        topi = idx.transpose(0, 2, 1)
        flat_idx = topi.reshape(Bn, K * E)
        gathered = jnp.take_along_axis(x, flat_idx[:, :, None], axis=1)
        gathered = gathered.reshape(Bn, K, E, Dn)
        pooled = jnp.einsum('bked,bke->bed', gathered, topv)
        ones = jnp.ones((E, Bn, 1), dtype=x.dtype)
        h = jnp.concatenate([pooled.transpose(1, 0, 2), ones], axis=-1)
        h = jax.nn.gelu(jnp.einsum('ebd,edh->ebh', h, weight1), approximate=False)
        h = jnp.concatenate([h, ones], axis=-1)
        out = jnp.einsum('ebh,eho->ebo', h, weight2)
        out = out.transpose(1, 0, 2)
        weighted = jnp.einsum('beo,bke->bkeo', out, topv).reshape(Bn, K * E, O)
        outputs = jnp.zeros((Bn, Sn, O), dtype=x.dtype)
        outputs = outputs.at[jnp.arange(Bn)[:, None], flat_idx].add(weighted)
        return outputs

    def _gn(v, G=32, eps=1e-5):
        B_, H_, W_, C_ = v.shape
        g = v.reshape(B_, H_, W_, G, C_ // G)
        m = jnp.mean(g, axis=(1, 2, 4), keepdims=True)
        s = jnp.var(g, axis=(1, 2, 4), keepdims=True)
        return ((g - m) / jnp.sqrt(s + eps)).reshape(v.shape)

    def _ln_c(v, eps=1e-6):
        m = jnp.mean(v, axis=-1, keepdims=True)
        s = jnp.var(v, axis=-1, keepdims=True)
        return (v - m) / jnp.sqrt(s + eps)

    def _ln_t(v, eps=1e-5):
        m = jnp.mean(v, axis=-1, keepdims=True)
        s = jnp.var(v, axis=-1, keepdims=True)
        return (v - m) / jnp.sqrt(s + eps)

    def _to_tokens(v):
        B_, H_, W_, C_ = v.shape
        return v.reshape(B_, H_ * W_, C_)
    def _from_tokens(t, like):
        return t.reshape(like.shape)

    x = x + _L0_conv_ref(_ln_c(x), L0_conv_ln_gamma, L0_conv_ln_beta, L0_conv_Wq, L0_conv_Wk, L0_conv_Wv, L0_conv_Wb, L0_conv_Wg, L0_conv_Wout)
    t = _to_tokens(x)
    t = t + _L0_ffn_ref(_ln_t(t), L0_ffn_gate_w, L0_ffn_gate_b, L0_ffn_weight1, L0_ffn_weight2)
    x = _from_tokens(t, x)
    x = x + _L1_conv_ref(_ln_c(x), L1_conv_W_exp, L1_conv_b_exp, L1_conv_W_con, L1_conv_b_con)
    t = _to_tokens(x)
    t = t + _L1_ffn_ref(_ln_t(t), L1_ffn_W, L1_ffn_V, L1_ffn_gamma, L1_ffn_beta)
    x = _from_tokens(t, x)
    x = x + _L2_conv_ref(_ln_c(x), L2_conv_Wf, L2_conv_bf, L2_conv_k0, L2_conv_k1, L2_conv_k2, L2_conv_Wh, L2_conv_bh, L2_conv_gamma, L2_conv_beta, L2_conv_Wp, L2_conv_bp)
    t = _to_tokens(x)
    t = t + _L2_ffn_ref(_ln_t(t), L2_ffn_gate_w, L2_ffn_gate_b, L2_ffn_weight1, L2_ffn_weight2)
    x = _from_tokens(t, x)
    x = x + _L3_conv_ref(_ln_c(x), L3_conv_kernel, L3_conv_bias, L3_conv_offset_w, L3_conv_offset_b)
    t = _to_tokens(x)
    t = t + _L3_ffn_ref(_ln_t(t), L3_ffn_gate_w, L3_ffn_gate_b, L3_ffn_weight1, L3_ffn_weight2)
    x = _from_tokens(t, x)
    return x


_drawn_inputs = setup_inputs


def setup_inputs(seed=0):
    import zlib

    import numpy as np

    out = dict(_drawn_inputs(seed))
    spreads = {'L0_conv_ln_gamma': (1.0, 0.2),
     'L0_conv_ln_beta': (0.0, 0.1),
     'L0_ffn_gate_b': (0.0, 0.8),
     'L1_ffn_gamma': (1.0, 0.2),
     'L1_ffn_beta': (0.0, 0.319),
     'L2_conv_bf': (0.0, 0.1),
     'L2_conv_bh': (0.0, 0.1),
     'L2_conv_gamma': (1.0, 0.6),
     'L2_conv_beta': (0.0, 0.273),
     'L2_conv_bp': (0.0, 0.1),
     'L2_ffn_gate_b': (0.0, 2.0),
     'L3_conv_bias': (0.0, 0.1),
     'L3_conv_offset_b': (0.0, 0.1),
     'L3_ffn_gate_b': (0.0, 0.8)}
    factors = {'L0_ffn_gate_w': 8.0,
     'L0_ffn_weight1': 8.0,
     'L0_ffn_weight2': 8.0,
     'L1_conv_b_exp': 2.823,
     'L2_conv_k0': 8.0,
     'L2_conv_k1': 8.0,
     'L2_conv_k2': 35.009,
     'L2_conv_Wh': 8.0,
     'L2_ffn_gate_w': 8.0,
     'L2_ffn_weight1': 8.0,
     'L2_ffn_weight2': 8.0,
     'L3_ffn_gate_w': 8.0,
     'L3_ffn_weight1': 8.0,
     'L3_ffn_weight2': 8.0}
    for name, (base, spread) in spreads.items():
        noise = np.random.default_rng([zlib.crc32(name.encode()), seed]).standard_normal(out[name].shape)
        drawn = base * np.exp(spread * noise) if base else spread * noise
        out[name] = jnp.asarray(drawn.astype(out[name].dtype))
    for name, factor in factors.items():
        out[name] = (out[name] * factor).astype(out[name].dtype)
    return out
```

```python
import numpy as np
import concourse.bass as bass
from concourse import mybir
from contextlib import ExitStack

fp32 = mybir.dt.float32
i32 = mybir.dt.int32
u32 = mybir.dt.uint32
ACT = mybir.ActivationFunctionType
ALU = mybir.AluOpType
AX = mybir.AxisListType

P = 128
C = 128
H = W = 256
N = H * W
TILES = 4
STEP = TILES * P
STEPS = N // STEP
BODY = 4
DMA = 16
PAD = 3
PW = W + 2 * PAD


class Namespace:
    pass


class Phase:

    def __init__(self, nc, ctx, name):
        self.nc, self.ctx, self.name, self.used = nc, ctx, name, []

    def sb(self, name, shape, dt=fp32):
        return self.ctx.enter_context(self.nc.sbuf_tensor(f"{self.name}_{name}", shape, dt))

    def banks(self, name, n=1):
        return self.ctx.enter_context(self.nc.psum_tensor(f"{self.name}_{name}", [P, n, 512], fp32))

    def sem(self, name):
        s = self.ctx.enter_context(self.nc.semaphore(f"{self.name}_{name}"))
        self.used.append(s)
        return s

    def block(self):
        self.ctx.callback(self.zero)
        return self.ctx.enter_context(self.nc.Block())

    def zero(self):
        with self.nc.Block() as block:
            @block.gpsimd
            def _(pool):
                for s in self.used:
                    pool.sem_clear(s)

    def sems(self, name, n):
        return [self.sem(f"{name}{i}") for i in range(n)]


def wait_alone(eng, sem, value, passed):
    eng.wait_ge(sem, value)
    eng.sem_inc(passed, 1)


class Chain:

    def __init__(self, eng, sem, before=0, passed=None):
        self.eng, self.sem, self.before, self.passed, self.n = eng, sem, before, passed, 0

    def link(self, ins):
        self.n += 1
        ins.then_inc(self.sem, 1)
        self.eng.wait_ge(self.sem, self.before + self.n)
        if self.passed is not None:
            self.eng.sem_inc(self.passed, 1)


def token_tiles(x, u):
    return x[bass.ds(u * STEP, STEP), :].rearrange("(j p) c -> p j c", p=P)


def column_stats(nc, chain, x4, stats, mv):
    for j in range(TILES):
        last = nc.vector.bn_stats(stats[:, j, :], x4[:, j, :])
    chain.link(last)
    for j in range(TILES):
        last = nc.vector.bn_aggr(mv[:, j, :], stats[:, j, :])
    return last


def normalize(nc, x4, mv, rstd, z4):
    for j in range(TILES):
        last = nc.vector.tensor_scalar(z4[:, j, :], x4[:, j, :], mv[:, j, 0:1], rstd[:, j:j + 1],
                                       ALU.subtract, ALU.mult)
    return last


def inverse_root(nc, pool, chain, mv, minus_half, rstd, scale, eps):
    chain.link(nc.gpsimd.tensor_scalar(rstd, mv[:, :, 1], scale, eps, ALU.mult, ALU.add))
    return nc.gpsimd.tensor_tensor(rstd, rstd, minus_half, ALU.pow)


def transpose_tiles(nc, bank, z4, ident):
    for j in range(TILES):
        last = nc.tensor.transpose(bank[:, j * P:(j + 1) * P], z4[:, j, :], ident[:, :])
    return last


def make_constants(nc, ident, minus_half):
    with ExitStack() as ctx:
        ph = Phase(nc, ctx, "const")
        done = ph.sem("done")
        block = ph.block()

        @block.gpsimd
        def _(pool):
            nc.gpsimd.memset(ident[:, :], 0.0).then_inc(done, 1)
            nc.gpsimd.memset(minus_half[:, :], -0.5).then_inc(done, 1)
            pool.wait_ge(done, 2)
            nc.gpsimd.affine_select(out=ident[:, :], in_=ident[:, :], compare_op=ALU.not_equal,
                                    fill=1.0, base=0, pattern=[[-1, P]],
                                    channel_multiplier=1).then_inc(done, 1)
            pool.wait_ge(done, 3)


def attention_front(nc, K, x, gamma, beta, wb, zt_out, bias_out):
    with ExitStack() as ctx:
        ph = Phase(nc, ctx, "l0f")
        xin = ph.sb("xin", [P, BODY, TILES, C])
        stats = ph.sb("stats", [P, BODY, TILES, 6])
        mv = ph.sb("mv", [P, BODY, TILES, 2])
        rstd = ph.sb("rstd", [P, BODY, TILES])
        z = ph.sb("z", [P, 2, TILES, C])
        zt = ph.sb("zt", [P, 2, STEP])
        bias = ph.sb("bias", [4, 2, STEP])
        gb = ph.sb("gb", [P, 2])
        wb_sb = ph.sb("wb", [P, 4])
        zt_ps = ph.banks("zt_ps", 2)
        bias_ps = ph.banks("bias_ps", 2)
        loaded = ph.sems("loaded", BODY)
        weights = ph.sem("weights")
        chain_d = ph.sem("chain_d")
        chain_p = ph.sem("chain_p")
        passed_d = ph.sem("passed_d")
        passed_p = ph.sem("passed_p")
        stats_ready = ph.sem("stats_ready")
        rstd_ready = ph.sem("rstd_ready")
        z_ready = ph.sem("z_ready")
        ztp_ready = ph.sem("ztp_ready")
        zt_ready = ph.sem("zt_ready")
        biasp_ready = ph.sem("biasp_ready")
        bias_ready = ph.sem("bias_ready")
        zt_stored = ph.sems("zt_stored", 2)
        bias_stored = ph.sems("bias_stored", 2)
        block = ph.block()

        @block.sync
        def _(sp):
            sp.dma_start(gb[:, 0:1], gamma.rearrange("(c a) -> c a", a=1)).then_inc(weights, DMA)
            sp.dma_start(gb[:, 1:2], beta.rearrange("(c a) -> c a", a=1)).then_inc(weights, DMA)
            sp.dma_start(wb_sb[:, :], wb).then_inc(weights, DMA)
            with sp.Fori(0, STEPS // BODY) as t:
                for b in range(BODY):
                    sp.wait_ge(z_ready, BODY * t + b + 1)
                    sp.dma_start(xin[:, b], token_tiles(x, BODY * t + b)).then_inc(loaded[b], DMA)

        @block.vector
        def _(dve):
            nc.vector.engine_nop().then_inc(z_ready, BODY)
            with dve.Fori(0, STEPS // BODY) as t:
                chain = Chain(dve, chain_d, BODY * t, passed_d)
                for b in range(BODY + 1):
                    if b < BODY:
                        dve.wait_ge(loaded[b], DMA * t + DMA)
                        column_stats(nc, chain, xin[:, b], stats[:, b], mv[:, b]).then_inc(stats_ready, 1)
                    if b:
                        u = BODY * t + b - 1
                        dve.wait_ge(rstd_ready, u + 1)
                        dve.wait_ge(ztp_ready, u + 1)
                        last = normalize(nc, xin[:, b - 1], mv[:, b - 1], rstd[:, b - 1], z[:, (b - 1) % 2])
                        last.then_inc(z_ready, 1)

        @block.gpsimd
        def _(pool):
            with pool.Fori(0, STEPS // BODY) as t:
                chain = Chain(pool, chain_p, BODY * t)
                for b in range(BODY):
                    wait_alone(pool, stats_ready, BODY * t + b + 1, passed_p)
                    inverse_root(nc, pool, chain, mv[:, b], K.minus_half[:, 0:TILES], rstd[:, b],
                                 1.0 + 1e-5, 1e-11).then_inc(rstd_ready, 1)

        @block.tensor
        def _(pe):
            nc.tensor.nop().then_inc(ztp_ready, 2)
            pe.wait_ge(weights, 3 * DMA)
            with pe.Fori(0, STEPS // BODY) as t:
                for b in range(BODY):
                    u = BODY * t + b
                    pe.wait_ge(z_ready, BODY + u + 1)
                    pe.wait_ge(zt_ready, u + 1)
                    transpose_tiles(nc, zt_ps[:, b % 2], z[:, b % 2], K.ident).then_inc(ztp_ready, 1)
                    pe.wait_ge(zt_ready, u + 3)
                    pe.wait_ge(bias_ready, u + 1)
                    nc.tensor.matmul(bias_ps[0:4, b % 2, :], wb_sb[:, :], zt[:, b % 2, :],
                                     start=True, stop=True).then_inc(biasp_ready, 1)

        @block.scalar
        def _(act):
            nc.scalar.nop().then_inc(zt_ready, 2)
            nc.scalar.nop().then_inc(bias_ready, 2)
            for i in range(2):
                nc.scalar.nop().then_inc(zt_stored[i], DMA)
                nc.scalar.nop().then_inc(bias_stored[i], DMA)
            act.wait_ge(weights, 3 * DMA)
            with act.Fori(0, STEPS // BODY) as t:
                for b in range(BODY):
                    u = BODY * t + b
                    act.wait_ge(ztp_ready, u + 3)
                    act.wait_ge(zt_stored[b % 2], DMA * (2 * t + b // 2 + 1))
                    nc.scalar.activation(zt[:, b % 2, :], zt_ps[:, b % 2, :], ACT.Identity,
                                         bias=gb[:, 1:2], scale=gb[:, 0:1]).then_inc(zt_ready, 1)
                    act.wait_ge(zt_ready, u + 3)
                    act.wait_ge(biasp_ready, u + 1)
                    act.dma_start(zt_out[:, bass.ds(u * STEP, STEP)], zt[:, b % 2, :])\
                        .then_inc(zt_stored[b % 2], DMA)
                    act.wait_ge(bias_stored[b % 2], DMA * (2 * t + b // 2 + 1))
                    nc.scalar.activation(bias[:, b % 2, :], bias_ps[0:4, b % 2, :], ACT.Copy)\
                        .then_inc(bias_ready, 1)
                    act.wait_ge(bias_ready, u + 3)
                    act.dma_start(bias_out[:, bass.ds(u * STEP, STEP)], bias[:, b % 2, :])\
                        .then_inc(bias_stored[b % 2], DMA)
            for i in range(2):
                act.wait_ge(zt_stored[i], DMA * (STEPS // 2 + 1))
                act.wait_ge(bias_stored[i], DMA * (STEPS // 2 + 1))


HEADS, HDIM = 4, 32
ROWS_BODY = 4


def spread(ap, n):
    return bass.AP(ap.tensor, ap.offset, [list(d) for d in ap.ap] + [[0, n]])


def attention(nc, K, x, zt, bias, wq, wk, wv, wg, wout, x_out):
    EV = 7
    CR = 4 * EV
    CB = 2 * EV
    with ExitStack() as ctx:
        ph = Phase(nc, ctx, "att")
        zrow = ph.sb("zrow", [P, ROWS_BODY, W])
        xrow = ph.sb("xrow", [P, ROWS_BODY, 2, C])
        w_qk = ph.sb("w_qk", [P, 2 * C])
        w_vg = ph.sb("w_vg", [P, 2 * C])
        w_out = ph.sb("w_out", [P, C])
        bias_sb = ph.sb("bias", [P, 2, HEADS, W])
        qk = ph.sb("qk", [P, 2, 2 * W])
        v = ph.sb("v", [P, 2, 2, C])
        gate = ph.sb("gate", [P, 2, 2, C])
        prob = ph.sb("prob", [P, 2, 2, HEADS, W])
        most = ph.sb("most", [P, 2, 8])
        neg = ph.sb("neg", [P, 2, 8])
        total = ph.sb("total", [P, 2, 8])
        inv = ph.sb("inv", [P, 8])
        probt = ph.sb("probt", [P, 4, HEADS * P])
        o = ph.sb("o", [P, 2 * C])
        ot = ph.sb("ot", [P, W])
        y = ph.sb("y", [P, ROWS_BODY, 2, C])
        qk_ps = ph.banks("qk_ps")
        vg_ps = ph.banks("vg_ps")
        s_ps = ph.banks("s_ps", HEADS)
        b_ps = ph.banks("b_ps", 2)
        loaded = ph.sems("loaded", ROWS_BODY)
        weights = ph.sem("weights")
        scaled = ph.sem("scaled")
        proj = ph.sem("proj")
        vg_free = ph.sem("vg_free")
        qk_ready = ph.sem("qk_ready")
        scores = ph.sem("scores")
        neg_ready = ph.sem("neg_ready")
        exp_ready = ph.sem("exp_ready")
        banked = ph.sem("banked")
        evac = ph.sem("evac")
        stored = ph.sems("stored", ROWS_BODY)
        chain_d = ph.sem("chain_d")
        passed_d = ph.sem("passed_d")
        block = ph.block()
        NW = 8 + 5

        @block.sync
        def _(sp):
            sp.dma_start(w_qk[:, 0:C], wq).then_inc(weights, DMA)
            sp.dma_start(w_qk[:, C:2 * C], wk).then_inc(weights, DMA)
            sp.dma_start(w_vg[:, 0:C], wv).then_inc(weights, DMA)
            sp.dma_start(w_vg[:, C:2 * C], wg).then_inc(weights, DMA)
            sp.dma_start(w_out[:, :], wout).then_inc(weights, DMA)
            for j in range(2):
                for h in range(HEADS):
                    sp.dma_start(bias_sb[:, j, h, :],
                                 bias[h, j * P * W:(j + 1) * P * W].rearrange("(p k) -> p k", k=W))\
                        .then_inc(weights, DMA)

            def load(t, b):
                i = ROWS_BODY * t + b
                sp.dma_start(zrow[:, b, :], zt[:, bass.ds(i * W, W)]).then_inc(loaded[b], DMA)
                sp.dma_start(xrow[:, b], x[bass.ds(i * W, W), :].rearrange("(j p) c -> p j c", p=P))\
                    .then_inc(loaded[b], DMA)

            def store(t, b):
                i = ROWS_BODY * t + b
                sp.wait_ge(evac, CR + EV * i + EV)
                sp.dma_start(x_out[bass.ds(i * W, W), :].rearrange("(j p) c -> p j c", p=P), y[:, b])\
                    .then_inc(stored[b], DMA)

            for b in range(ROWS_BODY):
                sp.nop().then_inc(stored[b], DMA)
                load(0, b)
            with sp.Fori(0, H // ROWS_BODY - 1) as t:
                for b in range(ROWS_BODY):
                    store(t, b)
                    load(t + 1, b)
            for b in range(ROWS_BODY):
                store(H // ROWS_BODY - 1, b)
            for b in range(ROWS_BODY):
                sp.wait_ge(stored[b], DMA * (H // ROWS_BODY + 1))

        @block.tensor
        def _(pe):
            nc.tensor.nop().then_inc(banked, CB)
            pe.wait_ge(weights, NW * DMA)
            pe.wait_ge(scaled, 1)

            def project(t, b):
                i = ROWS_BODY * t + b
                pe.wait_ge(loaded[b], 2 * DMA * t + 2 * DMA)
                pe.wait_ge(vg_free, i + 1)
                for a in range(2):
                    nc.tensor.matmul(qk_ps[:, 0, a * W:(a + 1) * W], w_qk[:, a * C:(a + 1) * C],
                                     zrow[:, b, :], start=True, stop=True)
                for j in range(2):
                    last = nc.tensor.matmul(vg_ps[:, 0, j * W:(j + 1) * W], zrow[:, b, j * P:(j + 1) * P],
                                            w_vg[:, :], start=True, stop=True)
                last.then_inc(proj, 1)

            def score(t, b):
                i = ROWS_BODY * t + b
                pe.wait_ge(qk_ready, i + 1)
                pe.wait_ge(neg_ready, i + 1)
                for j in range(2):
                    for h in range(HEADS):
                        part = slice(h * HDIM, (h + 1) * HDIM)
                        last = nc.tensor.matmul(s_ps[:, h, j * W:(j + 1) * W],
                                                qk[part, b % 2, j * P:(j + 1) * P],
                                                qk[part, b % 2, W:2 * W], start=True, stop=True)
                last.then_inc(scores, 1)

            def weigh(t, b):
                i = ROWS_BODY * t + b

                def bank(n):
                    return b_ps[:, (EV * b + n) % 2, :]

                for j in range(2):
                    pe.wait_ge(exp_ready, 2 * i + j + 1)
                    for k in range(2):
                        n = 2 * j + k
                        pe.wait_ge(evac, CR + EV * i + n - 1)
                        for h in range(HEADS):
                            last = nc.tensor.transpose(bank(n)[:, h * P:(h + 1) * P],
                                                       prob[:, b % 2, j, h, k * P:(k + 1) * P], K.ident[:, :])
                        last.then_inc(banked, 1)
                pe.wait_ge(evac, CR + EV * i + 4)
                for j in range(2):
                    for h in range(HEADS):
                        for k in range(2):
                            last = nc.tensor.matmul(bank(4)[:, j * C + h * HDIM:j * C + (h + 1) * HDIM],
                                                    probt[:, 2 * j + k, h * P:(h + 1) * P],
                                                    v[:, b % 2, k, h * HDIM:(h + 1) * HDIM],
                                                    start=(k == 0), stop=(k == 1))
                last.then_inc(banked, 1)
                pe.wait_ge(evac, CR + EV * i + 5)
                for j in range(2):
                    last = nc.tensor.transpose(bank(5)[:, j * P:(j + 1) * P], o[:, j * C:(j + 1) * C], K.ident[:, :])
                last.then_inc(banked, 1)
                pe.wait_ge(evac, CR + EV * i + 6)
                for j in range(2):
                    last = nc.tensor.matmul(bank(6)[:, j * C:(j + 1) * C], ot[:, j * P:(j + 1) * P],
                                            w_out[:, :], start=True, stop=True)
                last.then_inc(banked, 1)

            with pe.Fori(0, H // ROWS_BODY) as t:
                project(t, 0)
                for b in range(ROWS_BODY):
                    score(t, b)
                    if b + 1 < ROWS_BODY:
                        project(t, b + 1)
                    if b:
                        weigh(t, b - 1)
                weigh(t, ROWS_BODY - 1)

        @block.scalar
        def _(act):
            nc.scalar.nop().then_inc(vg_free, 1)

            def evacuate(t, b):
                i = ROWS_BODY * t + b
                act.wait_ge(proj, i + 1)
                act.wait_ge(neg_ready, i + 1)
                nc.scalar.activation(qk[:, b % 2, :], qk_ps[:, 0, :], ACT.Copy).then_inc(qk_ready, 1)
                act.wait_ge(evac, CR + EV * i - 2 * EV + 5)
                vg = vg_ps[:, 0, :].rearrange("p (j c) -> p j c", j=2)
                nc.scalar.activation(v[:, b % 2], vg[:, :, 0:C], ACT.Copy)
                nc.scalar.activation(gate[:, b % 2], vg[:, :, C:2 * C], ACT.Tanh, scale=0.5)\
                    .then_inc(vg_free, 1)

            with act.Fori(0, H // ROWS_BODY) as t:
                evacuate(t, 0)
                for b in range(ROWS_BODY):
                    i = ROWS_BODY * t + b
                    act.wait_ge(neg_ready, i + 2)
                    for j in range(2):
                        for h in range(HEADS):
                            m = j * HEADS + h
                            last = nc.scalar.activation(prob[:, b % 2, j, h, :], prob[:, b % 2, j, h, :], ACT.Exp,
                                                        bias=neg[:, b % 2, m:m + 1],
                                                        accum_out=total[:, b % 2, m:m + 1])
                        last.then_inc(exp_ready, 1)
                    if b + 1 < ROWS_BODY:
                        evacuate(t, b + 1)

        @block.vector
        def _(dve):
            nc.vector.engine_nop().then_inc(evac, CR)
            nc.vector.engine_nop().then_inc(neg_ready, 1)
            dve.wait_ge(weights, NW * DMA)
            nc.vector.tensor_scalar(w_qk[:, 0:C], w_qk[:, 0:C], float(HDIM) ** -0.5, None, ALU.mult)\
                .then_inc(scaled, 1)

            def maxima(t, b, chain):
                i = ROWS_BODY * t + b
                wait_alone(dve, banked, CB + EV * i - 2 * EV + 4, passed_d)
                wait_alone(dve, scores, i + 1, passed_d)
                for j in range(2):
                    for h in range(HEADS):
                        m = j * HEADS + h
                        last = nc.vector.tensor_tensor_reduce(
                            out=prob[:, b % 2, j, h, :], in0=s_ps[:, h, j * W:(j + 1) * W],
                            in1=bias_sb[:, j, h, :], scale=1.0, scalar=-3.0e38, op0=ALU.add, op1=ALU.max,
                            accum_out=most[:, b % 2, m:m + 1])
                chain.link(last)
                nc.vector.tensor_scalar(neg[:, b % 2, :], most[:, b % 2, :], -1.0, None, ALU.mult)\
                    .then_inc(neg_ready, 1)

            def finish(t, b, chain):
                i = ROWS_BODY * t + b

                def bank(n):
                    return b_ps[:, (EV * b + n) % 2, :]

                for n in range(4):
                    dve.wait_ge(banked, CB + EV * i + n + 1)
                    nc.vector.tensor_copy(probt[:, n, :], bank(n)).then_inc(evac, 1)
                dve.wait_ge(exp_ready, 2 * i + 2)
                chain.link(nc.vector.tensor_scalar(inv[:, :], total[:, b % 2, :], 2.0, None, ALU.mult))
                nc.vector.reciprocal(inv[:, :], inv[:, :])
                dve.wait_ge(banked, CB + EV * i + 5)
                dve.wait_ge(vg_free, i + 2)
                chain.link(nc.vector.scalar_tensor_tensor(
                    o[:, :], gate[:, b % 2].rearrange("p j c -> p (j c)"), 1.0, bank(4)[:, 0:2 * C],
                    ALU.add, ALU.mult))
                nc.vector.tensor_tensor(o[:, :].rearrange("p (m d) -> p m d", d=HDIM),
                                        o[:, :].rearrange("p (m d) -> p m d", d=HDIM),
                                        spread(inv[:, :], HDIM), ALU.mult).then_inc(evac, 1)
                dve.wait_ge(banked, CB + EV * i + 6)
                nc.vector.tensor_copy(ot[:, :], bank(5)[:, 0:W]).then_inc(evac, 1)
                dve.wait_ge(banked, CB + EV * i + 7)
                dve.wait_ge(stored[b], DMA * t + DMA)
                nc.vector.tensor_tensor(y[:, b].rearrange("p j c -> p (j c)"), bank(6)[:, 0:2 * C],
                                        xrow[:, b].rearrange("p j c -> p (j c)"), ALU.add).then_inc(evac, 1)

            with dve.Fori(0, H // ROWS_BODY) as t:
                chain = Chain(dve, chain_d, 3 * ROWS_BODY * t, passed_d)
                for b in range(ROWS_BODY + 1):
                    if b < ROWS_BODY:
                        maxima(t, b, chain)
                    if b:
                        finish(t, b - 1, chain)
                assert chain.n == 3 * ROWS_BODY


E_N = 64
TOP = 8
HID = 512
HB = HID // P
PAIRS = STEPS // 2
GROUP = 8
GROUPS = E_N // GROUP


def repeat_rows(ap, n):
    d = [list(x) for x in ap.ap]
    return bass.AP(ap.tensor, ap.offset, [d[0], [0, n]] + d[1:])


def moe(nc, K, name, x, gate_wt, gate_b, w1, w2):
    with ExitStack() as ctx:
        keep = Phase(nc, ctx, name)
        cand_v = keep.sb("cand_v", [E_N, PAIRS, 2, TOP])
        cand_i = keep.sb("cand_i", [E_N, PAIRS, 2, TOP])
        cand_s = keep.sb("cand_s", [E_N, 2, PAIRS])
        route(nc, K, name + "r", x, gate_wt, gate_b, cand_v, cand_i, cand_s)
        experts(nc, K, name + "e", x, w1, w2, cand_v, cand_i, cand_s)


def route(nc, K, name, x, gate_wt, gate_b, cand_v, cand_i, cand_s):
    with ExitStack() as ctx:
        ph = Phase(nc, ctx, name)
        xin = ph.sb("xin", [P, BODY, TILES, C])
        stats = ph.sb("stats", [P, BODY, TILES, 6])
        mv = ph.sb("mv", [P, BODY, TILES, 2])
        rstd = ph.sb("rstd", [P, BODY, TILES])
        z = ph.sb("z", [P, 2, TILES, C])
        zt = ph.sb("zt", [P, 2, STEP])
        gw = ph.sb("gw", [P, E_N])
        gb = ph.sb("gb", [P, 1])
        logit = ph.sb("logit", [P, 2, STEP])
        junk = ph.sb("junk", [P, STEP])
        best = ph.sb("best", [P, 2, TOP])
        place = ph.sb("place", [P, 2, TOP], u32)
        neg = ph.sb("neg", [P, 2, 1])
        all_v = ph.sb("all_v", [P, PAIRS, TOP])
        all_i = ph.sb("all_i", [P, PAIRS, TOP])
        all_s = ph.sb("all_s", [P, PAIRS])
        zt_ps = ph.banks("zt_ps", 2)
        lg_ps = ph.banks("lg_ps", 2)
        loaded = ph.sems("loaded", BODY)
        weights = ph.sem("weights")
        stats_ready = ph.sem("stats_ready")
        rstd_ready = ph.sem("rstd_ready")
        z_ready = ph.sem("z_ready")
        ztp_ready = ph.sem("ztp_ready")
        zt_ready = ph.sem("zt_ready")
        lgp_ready = ph.sem("lgp_ready")
        logit_ready = ph.sem("logit_ready")
        best_ready = ph.sem("best_ready")
        sum_ready = ph.sem("sum_ready")
        moved = ph.sem("moved")
        chain_d = ph.sem("chain_d")
        chain_p = ph.sem("chain_p")
        passed_d = ph.sem("passed_d")
        passed_p = ph.sem("passed_p")
        block = ph.block()

        @block.sync
        def _(sp):
            sp.dma_start(gw[:, :], gate_wt).then_inc(weights, DMA)
            for i in range(2):
                sp.dma_start(gb[i * E_N:(i + 1) * E_N, :], gate_b.rearrange("(c a) -> c a", a=1))\
                    .then_inc(weights, DMA)
            with sp.Fori(0, STEPS // BODY) as t:
                for b in range(BODY):
                    sp.wait_ge(z_ready, BODY * t + b + 1)
                    sp.dma_start(xin[:, b], token_tiles(x, BODY * t + b)).then_inc(loaded[b], DMA)
            sp.wait_ge(sum_ready, PAIRS + 2)
            sp.wait_ge(best_ready, PAIRS + 2)
            for i in range(2):
                part = slice(i * E_N, (i + 1) * E_N)
                sp.dma_start(cand_v[:, :, i, :], all_v[part]).then_inc(moved, DMA)
                sp.dma_start(cand_i[:, :, i, :], all_i[part]).then_inc(moved, DMA)
                sp.dma_start(cand_s[:, i, :], all_s[part, :]).then_inc(moved, DMA)
            sp.wait_ge(moved, 6 * DMA)

        @block.vector
        def _(dve):
            nc.vector.engine_nop().then_inc(z_ready, BODY)
            nc.vector.engine_nop().then_inc(best_ready, 2)

            def candidates(t, q):
                n = 2 * t + q
                wait_alone(dve, logit_ready, n + 3, passed_d)
                chain.link(nc.vector.max(best[:, q, :], logit[:, q, :]))
                nc.vector.max_index(place[:, q, :], best[:, q, :], logit[:, q, :])
                nc.vector.tensor_copy(all_v[:, bass.ds(n, 1), :], best[:, q:q + 1, :])
                wait_alone(dve, sum_ready, n + 1, passed_d)
                chain.link(nc.vector.tensor_scalar(neg[:, q, :], best[:, q, 0:1], -1.0, None, ALU.mult))
                nc.vector.tensor_copy(all_i[:, bass.ds(n, 1), :], place[:, q:q + 1, :]).then_inc(best_ready, 1)

            with dve.Fori(0, STEPS // BODY) as t:
                chain = Chain(dve, chain_d, (BODY + 4) * t, passed_d)
                for b in range(BODY + 1):
                    if b < BODY:
                        dve.wait_ge(loaded[b], DMA * t + DMA)
                        column_stats(nc, chain, xin[:, b], stats[:, b], mv[:, b]).then_inc(stats_ready, 1)
                    if b:
                        u = BODY * t + b - 1
                        dve.wait_ge(rstd_ready, u + 1)
                        dve.wait_ge(ztp_ready, u + 1)
                        normalize(nc, xin[:, b - 1], mv[:, b - 1], rstd[:, b - 1], z[:, (b - 1) % 2])\
                            .then_inc(z_ready, 1)
                    if b == 3:
                        candidates(t, 0)
                candidates(t, 1)
                assert chain.n == BODY + 4

        @block.gpsimd
        def _(pool):
            with pool.Fori(0, STEPS // BODY) as t:
                chain = Chain(pool, chain_p, BODY * t)
                for b in range(BODY):
                    wait_alone(pool, stats_ready, BODY * t + b + 1, passed_p)
                    inverse_root(nc, pool, chain, mv[:, b], K.minus_half[:, 0:TILES], rstd[:, b],
                                 1.0, 1e-5).then_inc(rstd_ready, 1)

        @block.tensor
        def _(pe):
            nc.tensor.nop().then_inc(ztp_ready, 2)
            pe.wait_ge(weights, 3 * DMA)
            with pe.Fori(0, STEPS // BODY) as t:
                for b in range(BODY):
                    u = BODY * t + b
                    pe.wait_ge(z_ready, BODY + u + 1)
                    pe.wait_ge(zt_ready, u + 1)
                    transpose_tiles(nc, zt_ps[:, b % 2], z[:, b % 2], K.ident).then_inc(ztp_ready, 1)
                    pe.wait_ge(zt_ready, u + 3)
                    if b % 2 == 0:
                        pe.wait_ge(logit_ready, 2 * t + b // 2 + 1)
                    half = (b % 2) * E_N
                    last = nc.tensor.matmul(lg_ps[half:half + E_N, b // 2, :], gw[:, :], zt[:, b % 2, :],
                                            start=True, stop=True)
                    last.then_inc(lgp_ready, 1)

        @block.scalar
        def _(act):
            nc.scalar.nop().then_inc(zt_ready, 2)
            nc.scalar.nop().then_inc(logit_ready, 2)
            nc.scalar.nop().then_inc(sum_ready, 2)
            act.wait_ge(weights, 3 * DMA)

            def exponentials(t, q):
                n = 2 * t + q
                act.wait_ge(best_ready, n + 3)
                act.wait_ge(sum_ready, n + 2)
                nc.scalar.activation(junk[:, :], logit[:, q, :], ACT.Exp, bias=neg[:, q, :],
                                     accum_out=all_s[:, bass.ds(n, 1)]).then_inc(sum_ready, 1)

            with act.Fori(0, STEPS // BODY) as t:
                for b in range(BODY):
                    u = BODY * t + b
                    act.wait_ge(ztp_ready, u + 3)
                    if b >= 2:
                        act.wait_ge(lgp_ready, BODY * t + b - 1)
                    nc.scalar.activation(zt[:, b % 2, :], zt_ps[:, b % 2, :], ACT.Copy).then_inc(zt_ready, 1)
                    if b % 2:
                        n = 2 * t + b // 2
                        act.wait_ge(lgp_ready, 2 * n + 2)
                        act.wait_ge(best_ready, n + 1)
                        act.wait_ge(sum_ready, n + 1)
                        nc.scalar.activation(logit[:, b // 2, :], lg_ps[:, b // 2, :], ACT.Identity,
                                             bias=gb[:, 0:1]).then_inc(logit_ready, 1)
                    if b == 3:
                        exponentials(t, 0)
                exponentials(t, 1)


def experts(nc, K, name, x, w1, w2, cand_v, cand_i, cand_s):
    NC = PAIRS * 2 * TOP
    FLAT = TOP * E_N
    with ExitStack() as ctx:
        ph = Phase(nc, ctx, name)
        w1_sb = ph.sb("w1", [P, 2, GROUP, HID])
        w2_sb = ph.sb("w2", [P, 2, GROUP, HB, C])
        b1_sb = ph.sb("b1", [E_N, HID])
        b1t = ph.sb("b1t", [P, HB, E_N])
        b2_sb = ph.sb("b2", [E_N, C])
        top = ph.sb("top", [E_N, TOP])
        place = ph.sb("place", [E_N, TOP], u32)
        placef = ph.sb("placef", [E_N, TOP])
        order_i = ph.sb("order_i", [E_N, NC], i32)
        order = ph.sb("order", [E_N, NC])
        base_i = ph.sb("base_i", [E_N, PAIRS * 2, TOP], i32)
        base = ph.sb("base", [E_N, PAIRS * 2, TOP])
        own_i = ph.sb("own_i", [E_N, TOP], i32)
        own = ph.sb("own", [E_N, TOP])
        junk = ph.sb("junk", [E_N, NC])
        idx = ph.sb("idx", [E_N, TOP])
        idx_u = ph.sb("idx_u", [E_N, TOP], u32)
        to = ph.sb("to", [E_N, TOP])
        to_u = ph.sb("to_u", [E_N, TOP], u32)
        neg = ph.sb("neg", [E_N, 1])
        scale = ph.sb("scale", [E_N, PAIRS * 2])
        total = ph.sb("total", [E_N, 1])
        prob = ph.sb("prob", [E_N, TOP])
        xg = ph.sb("xg", [E_N, TOP, C])
        zg = ph.sb("zg", [E_N, TOP, C])
        stats = ph.sb("stats", [E_N, TOP, 6])
        mv = ph.sb("mv", [E_N, TOP, 2])
        rstd = ph.sb("rstd", [E_N, TOP])
        pooled = ph.sb("pooled", [E_N, C])
        pooledt = ph.sb("pooledt", [P, E_N])
        pre = ph.sb("pre", [P, 2, GROUP, HB])
        hid = ph.sb("hid", [P, 2, GROUP, HB])
        outt = ph.sb("outt", [P, E_N])
        out = ph.sb("out", [E_N, C])
        ones = ph.sb("ones", [E_N, E_N])
        diag = ph.sb("diag", [E_N, TOP, E_N])
        row = ph.sb("row", [E_N, FLAT])
        mask = ph.sb("mask", [E_N, FLAT])
        count = ph.sb("count", [E_N, TOP])
        share = ph.sb("share", [E_N, FLAT])
        new = ph.sb("new", [E_N, TOP, C])
        misc_ps = ph.banks("misc_ps")
        hid_ps = ph.banks("hid_ps", 2)
        outt_ps = ph.banks("outt_ps")
        row_ps = ph.banks("row_ps")
        new_ps = ph.banks("new_ps", 2)
        bias_in = ph.sem("bias_in")
        w_in = ph.sems("w_in", 2)
        consts = ph.sem("consts")
        dve_done = ph.sem("dve_done")
        act_done = ph.sem("act_done")
        pool_done = ph.sem("pool_done")
        pe_done = ph.sem("pe_done")
        gathered = K.by_pool.pop()
        scattered = K.by_pool.pop()
        hid_pre = ph.sem("hid_pre")
        hid_add = ph.sem("hid_add")
        hid_ready = ph.sem("hid_ready")
        group_done = ph.sem("group_done")
        block = ph.block()
        EXP_IN, IDX_READY, STATS_READY, POOLED, ROW_IN, SHARE, OUTT, OUT, NEW_READY = 6, 15, 21, 30, 32, 67, 68, 69, 71

        @block.sync
        def _(sp):
            sp.dma_start(b1_sb[:, :], w1[:, P, :]).then_inc(bias_in, DMA)
            sp.dma_start(b2_sb[:, :], w2[:, HID, :]).then_inc(bias_in, DMA)
            for g in range(GROUPS):
                if g >= 2:
                    sp.wait_ge(group_done, g - 1)
                e = slice(g * GROUP, (g + 1) * GROUP)
                sp.dma_start(w1_sb[:, g % 2], w1[e, 0:P, :].rearrange("e d h -> d e h")).then_inc(w_in[g % 2], DMA)
                for k in range(HB):
                    sp.dma_start(w2_sb[:, g % 2, :, k, :],
                                 w2[e, k * P:(k + 1) * P, :].rearrange("e h o -> h e o")).then_inc(w_in[g % 2], DMA)

        @block.gpsimd
        def _(pool):
            nc.gpsimd.iota(order_i[:, :], pattern=[[1, NC]], base=0, channel_multiplier=0).then_inc(consts, 1)
            nc.gpsimd.iota(base_i[:, :, :], pattern=[[STEP, PAIRS * 2], [0, TOP]], base=0,
                           channel_multiplier=0).then_inc(consts, 1)
            nc.gpsimd.iota(own_i[:, :], pattern=[[E_N, TOP]], base=0, channel_multiplier=1).then_inc(consts, 1)
            nc.gpsimd.memset(ones[:, :], 1.0).then_inc(consts, 1)
            pool.wait_ge(dve_done, IDX_READY)
            for k in range(TOP):
                pool.indirect_dma_start(out=xg[:, k, :], out_offset=None, in_=x,
                                        in_offset=bass.IndirectOffsetOnAxis(ap=idx_u[:, k:k + 1], axis=0))\
                    .then_inc(gathered, DMA)
            pool.wait_ge(dve_done, STATS_READY)
            nc.gpsimd.tensor_scalar(rstd[:, :], mv[:, :, 1], 1.0, 1e-5, ALU.mult, ALU.add).then_inc(pool_done, 1)
            pool.wait_ge(pool_done, 1)
            nc.gpsimd.tensor_tensor(rstd[:, :], rstd[:, :], K.minus_half[0:E_N, 0:TOP], ALU.pow).then_inc(pool_done, 1)
            pool.wait_ge(dve_done, NEW_READY)
            for k in range(TOP):
                pool.indirect_dma_start(out=x, out_offset=bass.IndirectOffsetOnAxis(ap=to_u[:, k:k + 1], axis=0),
                                        in_=new[:, k, :], in_offset=None, bounds_check=N - 1,
                                        oob_is_err=False).then_inc(scattered, DMA)
            pool.wait_ge(scattered, TOP * DMA)

        flat_v = cand_v[:, :, :, :].rearrange("p q a k -> p (q a k)")
        flat_i = cand_i[:, :, :, :].rearrange("p q a k -> p (q a k)")

        @block.vector
        def _(dve):
            chain = Chain(dve, dve_done)
            link = chain.link
            dve.wait_ge(consts, 4)
            nc.vector.tensor_copy(order[:, :], order_i[:, :])
            nc.vector.tensor_copy(own[:, :], own_i[:, :])
            link(nc.vector.tensor_copy(base[:, :, :], base_i[:, :, :]))
            link(nc.vector.tensor_tensor(flat_i, flat_i, base[:, :, :].rearrange("p a k -> p (a k)"), ALU.add))
            link(nc.vector.max(top[:, :], flat_v))
            link(nc.vector.max_index(place[:, :], top[:, :], flat_v))
            link(nc.vector.tensor_copy(placef[:, :], place[:, :]))
            link(nc.vector.tensor_scalar(neg[:, :], top[:, 0:1], -1.0, None, ALU.mult))
            assert chain.n == EXP_IN
            for k in range(TOP):
                link(nc.vector.scalar_tensor_tensor(junk[:, :], order[:, :], placef[:, k:k + 1], flat_i,
                                                    ALU.is_equal, ALU.mult, accum_out=idx[:, k:k + 1]))
            link(nc.vector.tensor_copy(idx_u[:, :], idx[:, :]))
            assert chain.n == IDX_READY
            dve.wait_ge(act_done, 2)
            sums = cand_s[:, :, :].rearrange("p a q -> p (a q)")
            link(nc.vector.tensor_tensor(scale[:, :], scale[:, :], sums, ALU.mult))
            link(nc.vector.reduce_sum(total[:, :], scale[:, :], AX.X))
            link(nc.vector.reciprocal(total[:, :], total[:, :]))
            link(nc.vector.tensor_scalar(prob[:, :], prob[:, :], total[:, 0:1], None, ALU.mult))
            dve.wait_ge(gathered, TOP * DMA)
            for k in range(TOP):
                last = nc.vector.bn_stats(stats[:, k, :], xg[:, k, :])
            link(last)
            for k in range(TOP):
                last = nc.vector.bn_aggr(mv[:, k, :], stats[:, k, :])
            link(last)
            assert chain.n == STATS_READY
            dve.wait_ge(pool_done, 2)
            for k in range(TOP):
                last = nc.vector.tensor_scalar(zg[:, k, :], xg[:, k, :], mv[:, k, 0:1], rstd[:, k:k + 1],
                                               ALU.subtract, ALU.mult)
            link(last)
            link(nc.vector.tensor_scalar(pooled[:, :], zg[:, 0, :], prob[:, 0:1], None, ALU.mult))
            for k in range(1, TOP):
                link(nc.vector.scalar_tensor_tensor(pooled[:, :], zg[:, k, :], prob[:, k:k + 1], pooled[:, :],
                                                    ALU.mult, ALU.add))
            link(nc.vector.tensor_tensor(diag[:, :, :], repeat_rows(K.ident[0:E_N, 0:E_N], TOP),
                                         spread(idx[:, :], E_N), ALU.mult))
            assert chain.n == POOLED + 1
            dve.wait_ge(pe_done, 1)
            link(nc.vector.tensor_copy(pooledt[:, :], misc_ps[:, 0, 0:E_N]))
            assert chain.n == ROW_IN
            dve.wait_ge(pe_done, 2)
            nc.vector.tensor_copy(row[:, :], row_ps[0:E_N, 0, :])
            dve.wait_ge(pe_done, 3)
            link(nc.vector.tensor_copy(b1t[:, :, :].rearrange("p k e -> p (k e)"), misc_ps[:, 0, E_N:E_N + HB * E_N]))
            link(nc.vector.tensor_scalar(share[:, :], row[:, :], idx[:, 0:1], prob[:, 0:1], ALU.is_equal, ALU.mult))
            for k in range(1, TOP):
                link(nc.vector.tensor_scalar(mask[:, :], row[:, :], idx[:, k:k + 1], prob[:, k:k + 1],
                                             ALU.is_equal, ALU.mult))
                link(nc.vector.tensor_tensor(share[:, :], share[:, :], mask[:, :], ALU.add))
            for k in range(TOP):
                link(nc.vector.tensor_scalar(mask[:, :], order[:, 0:FLAT], own[:, k:k + 1], None, ALU.is_lt))
                link(nc.vector.scalar_tensor_tensor(junk[:, 0:FLAT], row[:, :], idx[:, k:k + 1], mask[:, :],
                                                    ALU.is_equal, ALU.mult, accum_out=count[:, k:k + 1]))
            link(nc.vector.tensor_scalar(count[:, :], count[:, :], float(2 * N), None, ALU.mult))
            link(nc.vector.tensor_tensor(to[:, :], count[:, :], idx[:, :], ALU.add))
            link(nc.vector.tensor_copy(to_u[:, :], to[:, :]))
            assert chain.n == SHARE, chain.n
            for g in range(GROUPS):
                dve.wait_ge(hid_pre, g + 1)
                e = slice(g * GROUP, (g + 1) * GROUP)
                if g >= 2:
                    dve.wait_ge(hid_ready, g - 1)
                nc.vector.tensor_tensor(pre[:, g % 2], hid_ps[:, g % 2, 0:GROUP * HB].rearrange("p (e k) -> p e k", k=HB),
                                        b1t[:, :, e].rearrange("p k e -> p e k"), ALU.add).then_inc(hid_add, 1)
            dve.wait_ge(group_done, GROUPS)
            link(nc.vector.tensor_copy(outt[:, :], outt_ps[:, 0, 0:E_N]))
            assert chain.n == OUTT
            dve.wait_ge(pe_done, 4)
            link(nc.vector.tensor_tensor(out[:, :], misc_ps[0:E_N, 0, 0:C], b2_sb[:, :], ALU.add))
            assert chain.n == OUT
            dve.wait_ge(pe_done, 5)
            for i in range(2):
                k = slice(i * TOP // 2, (i + 1) * TOP // 2)
                link(nc.vector.tensor_tensor(new[:, k, :].rearrange("p k c -> p (k c)"), new_ps[0:E_N, i, :],
                                             xg[:, k, :].rearrange("p k c -> p (k c)"), ALU.add))
            assert chain.n == NEW_READY

        @block.scalar
        def _(act):
            act.wait_ge(dve_done, EXP_IN)
            nc.scalar.activation(scale[:, :].rearrange("p (a q) -> p a q", a=2),
                                 cand_v[:, :, :, 0].rearrange("p q a -> p a q"), ACT.Exp,
                                 bias=neg[:, 0:1]).then_inc(act_done, 1)
            nc.scalar.activation(prob[:, :], top[:, :], ACT.Exp, bias=neg[:, 0:1]).then_inc(act_done, 1)
            for g in range(GROUPS):
                act.wait_ge(hid_add, g + 1)
                if g >= 2:
                    act.wait_ge(group_done, g - 1)
                nc.scalar.activation(hid[:, g % 2], pre[:, g % 2], ACT.Gelu).then_inc(hid_ready, 1)

        @block.tensor
        def _(pe):
            pe.wait_ge(dve_done, POOLED)
            nc.tensor.transpose(misc_ps[:, 0, 0:E_N], pooled[:, :], K.ident[0:E_N, 0:E_N]).then_inc(pe_done, 1)
            pe.wait_ge(consts, 4)
            pe.wait_ge(dve_done, POOLED + 1)
            nc.tensor.matmul(row_ps[0:E_N, 0, :], ones[:, :], diag[:, :, :].rearrange("p k e -> p (k e)"),
                             start=True, stop=True).then_inc(pe_done, 1)
            pe.wait_ge(dve_done, ROW_IN)
            pe.wait_ge(bias_in, 2 * DMA)
            for k in range(HB):
                last = nc.tensor.transpose(misc_ps[:, 0, (k + 1) * E_N:(k + 2) * E_N], b1_sb[:, k * P:(k + 1) * P],
                                           K.ident[0:E_N, 0:E_N])
            last.then_inc(pe_done, 1)
            for g in range(GROUPS + 1):
                if g < GROUPS:
                    pe.wait_ge(w_in[g % 2], (1 + HB) * DMA * (g // 2 + 1))
                    if g >= 2:
                        pe.wait_ge(hid_add, g - 1)
                    for e in range(GROUP):
                        for k in range(HB):
                            last = nc.tensor.matmul(hid_ps[:, g % 2, e * HB + k:e * HB + k + 1],
                                                    w1_sb[:, g % 2, e, k * P:(k + 1) * P],
                                                    pooledt[:, g * GROUP + e:g * GROUP + e + 1],
                                                    start=True, stop=True)
                    last.then_inc(hid_pre, 1)
                if g:
                    pe.wait_ge(hid_ready, g)
                    for e in range(GROUP):
                        n = (g - 1) * GROUP + e
                        for k in range(HB):
                            last = nc.tensor.matmul(outt_ps[:, 0, n:n + 1], w2_sb[:, (g - 1) % 2, e, k, :],
                                                    hid[:, (g - 1) % 2, e, k:k + 1],
                                                    start=(k == 0), stop=(k == HB - 1))
                    last.then_inc(group_done, 1)
            pe.wait_ge(dve_done, OUTT)
            nc.tensor.transpose(misc_ps[0:E_N, 0, 0:C], outt[:, :], K.ident[:, :]).then_inc(pe_done, 1)
            pe.wait_ge(dve_done, OUT)
            for k in range(TOP):
                last = nc.tensor.matmul(new_ps[0:E_N, k // 4, (k % 4) * C:(k % 4 + 1) * C],
                                        share[:, k * E_N:(k + 1) * E_N], out[:, :], start=True, stop=True)
            last.then_inc(pe_done, 1)


LONG = 8


def start_counts(eng, sems, n=LONG):
    for s in sems:
        eng.nop().then_inc(s, n)


def of_step(t, s, n=LONG):
    return n * t + (s + 1 + n)


def column(v):
    return v.rearrange("(c a) -> c a", a=1)


def on_all(v, n=P):
    return bass.AP(v.tensor, v.offset, [[0, n]] + [list(d) for d in v.ap])


SEQ_BLOCK = 64
SEQ_BLOCKS = W // SEQ_BLOCK


def of_rows(a, u):
    return a[:, :, bass.ds(2 * u, 2), :]


def row_order(a):
    return a.rearrange("c (k r j) -> c r k j", r=2, k=SEQ_BLOCKS)


def ema_conv(nc, K, x, w_exp_t, b_exp, w_con_t, b_con, w_t, x_out, wx_out, wx_mv):
    with ExitStack() as ctx:
        ph = Phase(nc, ctx, "ema")
        xin = ph.sb("xin", [P, LONG, TILES, C])
        xo = ph.sb("xo", [P, LONG, TILES, C])
        stats = ph.sb("stats", [P, 2, TILES, 6])
        mv = ph.sb("mv", [P, 2, TILES, 2])
        rstd = ph.sb("rstd", [P, 2, TILES])
        stats2 = ph.sb("stats2", [P, 2, TILES, 6])
        mv2 = ph.sb("mv2", [P, 2, TILES, 2])
        rstd2 = ph.sb("rstd2", [P, 2, TILES])
        z = ph.sb("z", [P, 2, TILES, C])
        zt = ph.sb("zt", [P, 2, STEP])
        z2 = ph.sb("z2", [P, 2, TILES, C])
        z2t = ph.sb("z2t", [P, 2, STEP])
        gin = ph.sb("gin", [P, 2, STEP])
        state = ph.sb("state", [P, 2, STEP])
        gate = ph.sb("gate", [P, 2, STEP])
        prod = ph.sb("prod", [P, 2, STEP])
        wx = ph.sb("wx", [P, 2, STEP])
        wx_stats = ph.sb("wx_stats", [P, STEPS, 6])
        w_exp = ph.sb("w_exp", [P, 2 * C])
        w_con = ph.sb("w_con", [P, C])
        w_sb = ph.sb("w_sb", [P, C])
        b_pg = ph.sb("b_pg", [P, 2])
        b_con_sb = ph.sb("b_con", [P, C])
        zt_ps = ph.banks("zt_ps")
        p_ps = ph.banks("p_ps", 2)
        g_ps = ph.banks("g_ps")
        out_ps = ph.banks("out_ps")
        z2t_ps = ph.banks("z2t_ps")
        wx_ps = ph.banks("wx_ps")
        loaded = ph.sems("loaded", LONG)
        stored = ph.sems("stored", LONG)
        wx_stored = ph.sems("wx_stored", 2)
        weights = ph.sem("weights")
        begun = ph.sem("begun")
        d_names = "mv_ready mv2_ready z_ready state_ready prod_ready xo_ready z2_ready wx_read"
        a_names = "zt_ready gin_ready gate_ready z2t_ready wx_ready"
        e_names = "ztp gp outp z2tp wxp"
        p_names = "rstd_ready xb_ready rstd2_ready"
        S = {n: ph.sem(n) for n in f"{d_names} {a_names} {e_names} {p_names}".split()}
        chain_d = ph.sem("chain_d")
        chain_p = ph.sem("chain_p")
        passed_d = ph.sem("passed_d")
        passed_p = ph.sem("passed_p")
        block = ph.block()
        NW = 6

        @block.sync
        def _(sp):
            for dst, src in ((w_exp[:, :], w_exp_t), (w_con[:, :], w_con_t), (w_sb[:, :], w_t),
                             (b_pg[:, 0:1], column(b_exp[0:C])), (b_pg[:, 1:2], column(b_exp[C:2 * C])),
                             (b_con_sb[:, :], on_all(b_con))):
                sp.dma_start(dst, src).then_inc(weights, DMA)

            def load(t, b):
                sp.dma_start(xin[:, b], token_tiles(x, LONG * t + b)).then_inc(loaded[b], DMA)

            def store(t, b):
                sp.wait_ge(S["z2_ready"], of_step(t, b))
                sp.dma_start(token_tiles(x_out, LONG * t + b), xo[:, b]).then_inc(stored[b], DMA)

            for b in range(LONG):
                sp.nop().then_inc(stored[b], DMA)
                load(0, b)
            with sp.Fori(0, STEPS // LONG - 1) as t:
                for b in range(LONG):
                    store(t, b)
                    load(t + 1, b)
            for b in range(LONG):
                store(STEPS // LONG - 1, b)
            for b in range(LONG):
                sp.wait_ge(stored[b], DMA * (STEPS // LONG + 1))

        @block.vector
        def _(dve):
            start_counts(dve, [S[n] for n in d_names.split()])
            dve.wait_ge(weights, NW * DMA)
            nc.vector.tensor_scalar(b_pg[:, 1:2], b_pg[:, 1:2], 0.1, None, ALU.mult).then_inc(begun, 1)
            nc.vector.memset(state[:, :, :], 0.0).then_inc(begun, 1)
            dve.wait_ge(begun, 2)
            with dve.Fori(0, STEPS // LONG) as t:
                chain = Chain(dve, chain_d, 3 * LONG * t, passed_d)
                for s in range(LONG + 4):
                    if s < LONG:
                        dve.wait_ge(loaded[s], DMA * t + DMA)
                        dve.wait_ge(S["rstd_ready"], of_step(t, s - 2))
                        column_stats(nc, chain, xin[:, s], stats[:, s % 2], mv[:, s % 2]).then_inc(S["mv_ready"], 1)
                    if 0 <= s - 1 < LONG:
                        b = s - 1
                        dve.wait_ge(S["rstd_ready"], of_step(t, b))
                        dve.wait_ge(S["ztp"], of_step(t, b - 2))
                        normalize(nc, xin[:, b], mv[:, b % 2], rstd[:, b % 2], z[:, b % 2]).then_inc(S["z_ready"], 1)
                    if 0 <= s - 2 < LONG:
                        b = s - 2
                        dve.wait_ge(S["gin_ready"], of_step(t, b))
                        dve.wait_ge(S["gate_ready"], of_step(t, b - 2))
                        dve.wait_ge(S["state_ready"], of_step(t, b - 1))
                        chain.link(nc.vector.scalar_tensor_tensor(
                            state[:, b % 2, 0:W], state[:, (b + 1) % 2, W:2 * W], 0.9, gin[:, b % 2, 0:W],
                            ALU.mult, ALU.add))
                        nc.vector.scalar_tensor_tensor(
                            state[:, b % 2, W:2 * W], state[:, b % 2, 0:W], 0.9, gin[:, b % 2, W:2 * W],
                            ALU.mult, ALU.add).then_inc(S["state_ready"], 1)
                    if 0 <= s - 3 < LONG:
                        b = s - 3
                        dve.wait_ge(S["outp"], of_step(t, b))
                        dve.wait_ge(S["xb_ready"], of_step(t, b))
                        dve.wait_ge(stored[b], DMA * t + DMA)
                        dve.wait_ge(S["rstd2_ready"], of_step(t, b - 2))
                        nc.vector.tensor_tensor(xo[:, b].rearrange("p j c -> p (j c)"), out_ps[:, 0, :],
                                                xin[:, b].rearrange("p j c -> p (j c)"), ALU.add)\
                            .then_inc(S["xo_ready"], 1)
                        wait_alone(dve, S["xo_ready"], of_step(t, b), passed_d)
                        column_stats(nc, chain, xo[:, b], stats2[:, b % 2], mv2[:, b % 2])\
                            .then_inc(S["mv2_ready"], 1)
                    if 0 <= s - 2 < LONG:
                        b = s - 2
                        dve.wait_ge(S["gate_ready"], of_step(t, b))
                        dve.wait_ge(S["outp"], of_step(t, b - 2))
                        nc.vector.scalar_tensor_tensor(prod[:, b % 2, :], p_ps[:, b % 2, :], b_pg[:, 0:1],
                                                       gate[:, b % 2, :], ALU.add, ALU.mult)\
                            .then_inc(S["prod_ready"], 1)
                    if 0 <= s - 3 < LONG:
                        b = s - 3
                        dve.wait_ge(S["rstd2_ready"], of_step(t, b))
                        dve.wait_ge(S["z2tp"], of_step(t, b - 2))
                        normalize(nc, xo[:, b], mv2[:, b % 2], rstd2[:, b % 2], z2[:, b % 2])\
                            .then_inc(S["z2_ready"], 1)
                    if 0 <= s - 4 < LONG:
                        b = s - 4
                        dve.wait_ge(S["wx_ready"], of_step(t, b))
                        nc.vector.bn_stats(wx_stats[:, LONG * t + b, :], wx[:, b % 2, :])\
                            .then_inc(S["wx_read"], 1)
                assert chain.n == 3 * LONG
            dve.wait_ge(S["wx_read"], STEPS + LONG)
            nc.vector.bn_aggr(wx_mv[:, :], wx_stats[:, :, :].rearrange("p s k -> p (s k)")).then_inc(begun, 1)
            dve.wait_ge(begun, 3)

        @block.gpsimd
        def _(pool):
            start_counts(pool, [S[n] for n in p_names.split()])
            pool.wait_ge(weights, NW * DMA)
            with pool.Fori(0, STEPS // LONG) as t:
                chain = Chain(pool, chain_p, 2 * LONG * t)
                for s in range(LONG + 3):
                    if s < LONG:
                        wait_alone(pool, S["mv_ready"], of_step(t, s), passed_p)
                        wait_alone(pool, S["z_ready"], of_step(t, s - 2), passed_p)
                        inverse_root(nc, pool, chain, mv[:, s % 2], K.minus_half[:, 0:TILES], rstd[:, s % 2],
                                     1.0, 1e-6).then_inc(S["rstd_ready"], 1)
                    if 0 <= s - 1 < LONG:
                        b = s - 1
                        pool.wait_ge(S["z_ready"], of_step(t, b))
                        nc.gpsimd.tensor_tensor(xin[:, b], xin[:, b], repeat_rows(b_con_sb[:, :], TILES), ALU.add)\
                            .then_inc(S["xb_ready"], 1)
                    if 0 <= s - 3 < LONG:
                        b = s - 3
                        wait_alone(pool, S["mv2_ready"], of_step(t, b), passed_p)
                        wait_alone(pool, S["z2_ready"], of_step(t, b - 2), passed_p)
                        inverse_root(nc, pool, chain, mv2[:, b % 2], K.minus_half[:, 0:TILES], rstd2[:, b % 2],
                                     1.0, 1e-5).then_inc(S["rstd2_ready"], 1)
                assert chain.n == 2 * LONG

        @block.tensor
        def _(pe):
            start_counts(pe, [S[n] for n in e_names.split()])
            pe.wait_ge(weights, NW * DMA)
            with pe.Fori(0, STEPS // LONG) as t:
                for s in range(LONG + 3):
                    if 0 <= s < LONG:
                        b = s
                        pe.wait_ge(S["z_ready"], of_step(t, b))
                        pe.wait_ge(S["zt_ready"], of_step(t, b - 1))
                        transpose_tiles(nc, zt_ps[:, 0], z[:, b % 2], K.ident).then_inc(S["ztp"], 1)
                        pe.wait_ge(S["zt_ready"], of_step(t, b))
                        pe.wait_ge(S["gin_ready"], of_step(t, b - 1))
                        pe.wait_ge(S["prod_ready"], of_step(t, b - 2))
                        nc.tensor.matmul(g_ps[:, 0, :], w_exp[:, C:2 * C], zt[:, b % 2, :], start=True, stop=True)
                        nc.tensor.matmul(p_ps[:, b % 2, :], w_exp[:, 0:C], zt[:, b % 2, :], start=True, stop=True)\
                            .then_inc(S["gp"], 1)
                    if 0 <= s - 1 < LONG:
                        b = s - 1
                        pe.wait_ge(S["prod_ready"], of_step(t, b))
                        pe.wait_ge(S["xo_ready"], of_step(t, b - 1))
                        for j in range(TILES):
                            last = nc.tensor.matmul(out_ps[:, 0, j * P:(j + 1) * P], prod[:, b % 2, j * P:(j + 1) * P],
                                                    w_con[:, :], start=True, stop=True)
                        last.then_inc(S["outp"], 1)
                    if 0 <= s - 2 < LONG:
                        b = s - 2
                        pe.wait_ge(S["z2_ready"], of_step(t, b))
                        pe.wait_ge(S["z2t_ready"], of_step(t, b - 1))
                        transpose_tiles(nc, z2t_ps[:, 0], z2[:, b % 2], K.ident).then_inc(S["z2tp"], 1)
                        pe.wait_ge(S["z2t_ready"], of_step(t, b))
                        pe.wait_ge(S["wx_ready"], of_step(t, b - 1))
                        nc.tensor.matmul(wx_ps[:, 0, :], w_sb[:, :], z2t[:, b % 2, :], start=True, stop=True)\
                            .then_inc(S["wxp"], 1)

        @block.scalar
        def _(act):
            start_counts(act, [S[n] for n in a_names.split()])
            for i in range(2):
                act.nop().then_inc(wx_stored[i], DMA)
            act.wait_ge(begun, 1)
            with act.Fori(0, STEPS // LONG) as t:
                for s in range(LONG + 3):
                    if 0 <= s < LONG:
                        b = s
                        act.wait_ge(S["ztp"], of_step(t, b))
                        act.wait_ge(S["gp"], of_step(t, b - 2))
                        nc.scalar.activation(zt[:, b % 2, :], zt_ps[:, 0, :], ACT.Copy).then_inc(S["zt_ready"], 1)
                    if 0 <= s - 1 < LONG:
                        b = s - 1
                        act.wait_ge(S["state_ready"], of_step(t, b))
                        act.wait_ge(S["prod_ready"], of_step(t, b - 2))
                        nc.scalar.activation(gate[:, b % 2, :], state[:, b % 2, :], ACT.Sigmoid)\
                            .then_inc(S["gate_ready"], 1)
                    if 0 <= s < LONG:
                        b = s
                        act.wait_ge(S["gp"], of_step(t, b))
                        act.wait_ge(S["state_ready"], of_step(t, b - 2))
                        nc.scalar.activation(gin[:, b % 2, :], g_ps[:, 0, :], ACT.Identity,
                                             bias=b_pg[:, 1:2], scale=0.1).then_inc(S["gin_ready"], 1)
                    if 0 <= s - 2 < LONG:
                        b = s - 2
                        act.wait_ge(S["z2tp"], of_step(t, b))
                        act.wait_ge(S["wxp"], of_step(t, b - 2))
                        nc.scalar.activation(z2t[:, b % 2, :], z2t_ps[:, 0, :], ACT.Copy).then_inc(S["z2t_ready"], 1)
                        act.wait_ge(S["wxp"], of_step(t, b))
                        act.wait_ge(S["wx_read"], of_step(t, b - 2))
                        act.wait_ge(wx_stored[b % 2], DMA * (LONG // 2 * t + b // 2 + 1))
                        nc.scalar.activation(row_order(wx[:, b % 2, :]),
                                             wx_ps[:, 0, :].rearrange("c (r k j) -> c r k j", r=2, k=SEQ_BLOCKS),
                                             ACT.Copy).then_inc(S["wx_ready"], 1)
                        act.wait_ge(S["wx_ready"], of_step(t, b))
                        act.dma_start(of_rows(wx_out, LONG * t + b), wx[:, b % 2, :].rearrange("c (k r j) -> c k r j", r=2, k=SEQ_BLOCKS))\
                            .then_inc(wx_stored[b % 2], DMA)
            for i in range(2):
                act.wait_ge(wx_stored[i], DMA * (STEPS // 2 + 1))


WARM = 32


def recur(nc, K, name, wx, seq, state, first, count, y_out, save):
    size = min(count, SEQ_BLOCK)
    blocks = count // size
    with ExitStack() as ctx:
        ph = Phase(nc, ctx, name)
        blk, pre_ps = seq.blk, seq.pre_ps
        loaded = ph.sems("loaded", 2)
        stored = ph.sems("stored", 2)
        pre_ready = ph.sem("pre_ready")
        y_ready = ph.sem("y_ready")
        copied = ph.sem("copied")
        saved = ph.sem("saved")
        block = ph.block()

        def columns(a, k):
            k0, at = divmod(first + k * size, SEQ_BLOCK)
            return a[:, k0, :, at:at + size]

        @block.sync
        def _(sp):
            def load(k):
                sp.dma_start(blk[:, k % 2, :, 0:size], columns(wx, k)).then_inc(loaded[k % 2], DMA)

            load(0)
            for k in range(blocks):
                if k + 1 < blocks:
                    if k >= 1 and y_out is not None:
                        sp.wait_ge(stored[(k + 1) % 2], DMA * ((k + 1) // 2))
                        if save:
                            sp.wait_ge(saved, 1)
                    load(k + 1)
                if y_out is not None:
                    sp.wait_ge(copied, (k + 1) * size + 2)
                    sp.dma_start(columns(y_out, k), blk[:, k % 2])\
                        .then_inc(stored[k % 2], DMA)
            if y_out is not None:
                for k in range(min(2, blocks)):
                    sp.wait_ge(stored[k], DMA * ((blocks + 1 - k) // 2))

        @block.tensor
        def _(pe):
            for k in range(blocks):
                pe.wait_ge(loaded[k % 2], DMA * (k // 2 + 1))
                with pe.Fori(0, size // 2) as t:
                    for b in range(2):
                        n = 2 * t + (k * size + b)
                        pe.wait_ge(y_ready, n + 1)
                        nc.tensor.matmul(pre_ps[:, b, 0:H], seq.diag[:, :],
                                         blk[:, k % 2, :, bass.ds(2 * t + b, 1)].rearrange("c h a -> c (h a)"),
                                         start=True, stop=False)
                        pe.wait_ge(y_ready, n + 2)
                        nc.tensor.matmul(pre_ps[:, b, 0:H], seq.vt[:, :], state[:, 1 - b, :],
                                         start=False, stop=True).then_inc(pre_ready, 1)

        @block.scalar
        def _(act):
            nc.scalar.activation(state[:, 1, :], seq.start[:, :], ACT.Copy).then_inc(y_ready, 2)
            with act.Fori(0, count // 2) as t:
                for b in range(2):
                    act.wait_ge(pre_ready, 2 * t + b + 1)
                    act.wait_ge(copied, 2 * t + b + 1)
                    nc.scalar.activation(state[:, b, :], pre_ps[:, b, 0:H], ACT.Sigmoid, bias=seq.shift[:, 0:1])\
                        .then_inc(y_ready, 1)

        @block.vector
        def _(dve):
            nc.vector.engine_nop().then_inc(copied, 2)
            for k in range(blocks):
                with dve.Fori(0, size // 2) as t:
                    for b in range(2):
                        dve.wait_ge(y_ready, 2 * t + (k * size + b + 3))
                        nc.vector.tensor_copy(blk[:, k % 2, :, bass.ds(2 * t + b, 1)].rearrange("c h a -> c (h a)"),
                                              state[:, b, :]).then_inc(copied, 1)
                if k == 0 and save:
                    dve.wait_ge(copied, size + 2)
                    nc.vector.tensor_copy(seq.early[:, :], blk[:, 0, :, size - 1]).then_inc(saved, 1)



def settle(nc, K, name, seq, state, compare):
    with ExitStack() as ctx:
        ph = Phase(nc, ctx, name)
        d = ph.sem("d")
        e = ph.sem("e")
        block = ph.block()

        @block.vector
        def _(dve):
            chain = Chain(dve, d)
            if compare:
                nc.vector.memset(seq.most[:, 1:2], 1.0)
                chain.link(nc.vector.tensor_tensor(seq.changed[:, :], state[:, 1, :], seq.early[:, :], ALU.not_equal))
                chain.link(nc.vector.reduce_max(seq.most[:, 0:1], seq.changed[:, :], AX.X))
                dve.wait_ge(e, 1)
                chain.link(nc.vector.tensor_copy(seq.again[0:1, 0:1], seq.sum_ps[0:1, 0, 0:1]))
            else:
                chain.link(nc.vector.tensor_copy(seq.start[:, 1:H], state[:, 1, 0:H - 1]))

        if compare:
            @block.tensor
            def _(pe):
                pe.wait_ge(d, 2)
                nc.tensor.matmul(seq.sum_ps[0:1, 0, 0:1], seq.most[:, 0:1], seq.most[:, 1:2],
                                 start=True, stop=True).then_inc(e, 1)



def recurrence(nc, K, wx, wx_mv, gamma, beta, vt, y_out):
    with ExitStack() as ctx:
        keep = Phase(nc, ctx, "seq")
        seq = Namespace()
        seq.diag = keep.sb("diag", [P, P])
        seq.vt = keep.sb("vt", [P, P])
        seq.shift = keep.sb("shift", [P, 1])
        seq.start = keep.sb("start", [P, H])
        seq.again = keep.sb("again", [1, 1], i32)
        state = keep.sb("state", [P, 2, H])
        seq.blk = keep.sb("blk", [P, 2, H, SEQ_BLOCK])
        seq.pre_ps = keep.banks("pre_ps", 2)
        seq.changed = keep.sb("changed", [P, H])
        seq.early = keep.sb("early", [P, H])
        seq.most = keep.sb("most", [P, 2])
        seq.sum_ps = keep.banks("sum_ps")
        with ExitStack() as inner:
            ph = Phase(nc, inner, "seqw")
            gb = ph.sb("gb", [P, 2])
            scale = ph.sb("scale", [P, 1])
            w = ph.sem("w")
            p = ph.sem("p")
            d = ph.sem("d")
            block = ph.block()

            @block.sync
            def _(sp):
                sp.dma_start(gb[:, 0:1], column(gamma)).then_inc(w, DMA)
                sp.dma_start(gb[:, 1:2], column(beta)).then_inc(w, DMA)
                sp.dma_start(seq.vt[:, :], vt).then_inc(w, DMA)

            @block.gpsimd
            def _(pool):
                nc.gpsimd.tensor_scalar(scale[:, :], wx_mv[:, 1:2], 1.0, 1e-5, ALU.mult, ALU.add).then_inc(p, 1)
                pool.wait_ge(p, 1)
                nc.gpsimd.tensor_tensor(scale[:, :], scale[:, :], K.minus_half[:, 0:1], ALU.pow).then_inc(p, 1)

            @block.vector
            def _(dve):
                chain = Chain(dve, d)
                chain.link(nc.vector.memset(seq.start[:, :], 0.0))
                chain.link(nc.vector.memset(seq.again[:, :], 1))
                dve.wait_ge(w, 3 * DMA)
                dve.wait_ge(p, 2)
                chain.link(nc.vector.tensor_tensor(scale[:, :], scale[:, :], gb[:, 0:1], ALU.mult))
                chain.link(nc.vector.tensor_scalar(seq.diag[:, :], K.ident[:, :], scale[:, 0:1], None, ALU.mult))
                chain.link(nc.vector.tensor_tensor(seq.shift[:, :], wx_mv[:, 0:1], scale[:, :], ALU.mult))
                chain.link(nc.vector.tensor_tensor(seq.shift[:, :], gb[:, 1:2], seq.shift[:, :], ALU.subtract))

        recur(nc, K, "seqg", wx, seq, state, W - WARM, WARM, None, False)
        settle(nc, K, "seqh", seq, state, False)
        with nc.Fori(0, 16):
            nc.all_engine_barrier()
            outer = nc.values_load(seq.again[0:1, 0:1])
            with nc.If(outer > 0):
                with nc.Fori(0, H // 16):
                    nc.all_engine_barrier()
                    again = nc.values_load(seq.again[0:1, 0:1])
                    with nc.If(again > 0):
                        recur(nc, K, "seqr", wx, seq, state, 0, W, y_out, True)
                        settle(nc, K, "seqs", seq, state, False)
                        recur(nc, K, "seqf", wx, seq, state, 0, SEQ_BLOCK, y_out, False)
                        settle(nc, K, "seqt", seq, state, True)
                    with nc.Else():
                        for eng in (nc.sync, nc.tensor, nc.vector, nc.scalar, nc.gpsimd):
                            eng.nop()
            with nc.Else():
                for eng in (nc.sync, nc.tensor, nc.vector, nc.scalar, nc.gpsimd):
                    eng.nop()
        nc.all_engine_barrier()


LEVELS = 3
RB = 8
CHUNK = RB * W
BLOCKS = H // RB
CB = CHUNK // 512
RING = H + 2 * PAD


def clear_rows(nc, name, images, pad):
    with ExitStack() as ctx:
        ph = Phase(nc, ctx, name)
        zero = ph.sb("zero", [P, pad * W])
        set_ = ph.sem("set")
        stored = ph.sem("stored")
        block = ph.block()

        @block.vector
        def _(dve):
            nc.vector.memset(zero[:, :], 0.0).then_inc(set_, 1)

        @block.sync
        def _(sp):
            sp.wait_ge(set_, 1)
            for im in images:
                for at in (0, pad + H):
                    sp.dma_start(im[:, at:at + pad, :].rearrange("c h w -> c (h w)"), zero[:, :]).then_inc(stored, DMA)
            sp.wait_ge(stored, 2 * len(images) * DMA)


def focal_front(nc, K, x, y, wf, bf, x_out, q_out, ctx_out, gates_out):
    G = LEVELS + 1
    with ExitStack() as ctx:
        ph = Phase(nc, ctx, "ff")
        xin = ph.sb("xin", [P, LONG, TILES, C])
        yin = ph.sb("yin", [P, LONG, STEP])
        xo = ph.sb("xo", [P, LONG, TILES, C])
        stats = ph.sb("stats", [P, 2, TILES, 6])
        mv = ph.sb("mv", [P, 2, TILES, 2])
        rstd = ph.sb("rstd", [P, 2, TILES])
        z = ph.sb("z", [P, 2, TILES, C])
        zt = ph.sb("zt", [P, 2, STEP])
        q = ph.sb("q", [P, 2, TILES, C])
        cx = ph.sb("cx", [P, 2, STEP])
        gates = ph.sb("gates", [G, 2, STEP])
        w_sb = ph.sb("w", [P, 2 * C + G])
        bq = ph.sb("bq", [P, C])
        bc = ph.sb("bc", [P, 1])
        bg = ph.sb("bg", [G, 1])
        yt_ps = ph.banks("yt_ps", 2)
        zt_ps = ph.banks("zt_ps")
        cx_ps = ph.banks("cx_ps")
        q_ps = ph.banks("q_ps")
        g_ps = ph.banks("g_ps")
        loaded = ph.sems("loaded", LONG)
        stored = ph.sems("stored", LONG)
        q_stored = ph.sems("q_stored", 2)
        cx_stored = ph.sems("cx_stored", 2)
        weights = ph.sem("weights")
        d_names = "xo_ready mv_ready z_ready q_ready"
        a_names = "zt_ready cx_ready"
        e_names = "ytp ztp cxp qp"
        p_names = "rstd_ready"
        S = {n: ph.sem(n) for n in f"{d_names} {a_names} {e_names} {p_names}".split()}
        chain_d = ph.sem("chain_d")
        chain_p = ph.sem("chain_p")
        passed_d = ph.sem("passed_d")
        passed_p = ph.sem("passed_p")
        block = ph.block()
        NW = 4

        @block.sync
        def _(sp):
            for dst, src in ((w_sb[:, :], wf), (bq[:, :], on_all(bf[0:C])), (bc[:, :], column(bf[C:2 * C])),
                             (bg[:, :], column(bf[2 * C:2 * C + G]))):
                sp.dma_start(dst, src).then_inc(weights, DMA)

            def load(t, b):
                u = LONG * t + b
                sp.dma_start(xin[:, b], token_tiles(x, u)).then_inc(loaded[b], DMA)
                for r in range(2):
                    sp.dma_start(yin[:, b, r * W:(r + 1) * W].rearrange("c (k j) -> c k j", k=SEQ_BLOCKS),
                                 y[:, :, 2 * u + r, :]).then_inc(loaded[b], DMA)

            def store(t, b):
                sp.wait_ge(S["z_ready"], of_step(t, b))
                sp.dma_start(token_tiles(x_out, LONG * t + b), xo[:, b]).then_inc(stored[b], DMA)

            for b in range(LONG):
                sp.nop().then_inc(stored[b], DMA)
                load(0, b)
            with sp.Fori(0, STEPS // LONG - 1) as t:
                for b in range(LONG):
                    store(t, b)
                    load(t + 1, b)
            for b in range(LONG):
                store(STEPS // LONG - 1, b)
            for b in range(LONG):
                sp.wait_ge(stored[b], DMA * (STEPS // LONG + 1))

        @block.vector
        def _(dve):
            start_counts(dve, [S[n] for n in d_names.split()])
            dve.wait_ge(weights, NW * DMA)
            with dve.Fori(0, STEPS // LONG) as t:
                chain = Chain(dve, chain_d, LONG * t, passed_d)
                for s in range(LONG + 2):
                    if s < LONG:
                        dve.wait_ge(loaded[s], 3 * DMA * t + 3 * DMA)
                        dve.wait_ge(S["ytp"], of_step(t, s))
                        dve.wait_ge(stored[s], DMA * t + DMA)
                        dve.wait_ge(S["rstd_ready"], of_step(t, s - 2))
                        nc.vector.tensor_tensor(xo[:, s].rearrange("p j c -> p (j c)"), yt_ps[:, s % 2, :],
                                                xin[:, s].rearrange("p j c -> p (j c)"), ALU.add)\
                            .then_inc(S["xo_ready"], 1)
                        wait_alone(dve, S["xo_ready"], of_step(t, s), passed_d)
                        column_stats(nc, chain, xo[:, s], stats[:, s % 2], mv[:, s % 2]).then_inc(S["mv_ready"], 1)
                    if 0 <= s - 2 < LONG:
                        b = s - 2
                        dve.wait_ge(S["qp"], of_step(t, b))
                        dve.wait_ge(q_stored[b % 2], DMA * (LONG // 2 * t + b // 2 + 1))
                        nc.vector.tensor_tensor(q[:, b % 2], q_ps[:, 0, :].rearrange("p (j c) -> p j c", c=C),
                                                repeat_rows(bq[:, :], TILES), ALU.add).then_inc(S["q_ready"], 1)
                    if 0 <= s - 1 < LONG:
                        b = s - 1
                        dve.wait_ge(S["rstd_ready"], of_step(t, b))
                        dve.wait_ge(S["ztp"], of_step(t, b - 2))
                        normalize(nc, xo[:, b], mv[:, b % 2], rstd[:, b % 2], z[:, b % 2]).then_inc(S["z_ready"], 1)
                assert chain.n == LONG

        @block.gpsimd
        def _(pool):
            start_counts(pool, [S[n] for n in p_names.split()])
            with pool.Fori(0, STEPS // LONG) as t:
                chain = Chain(pool, chain_p, LONG * t)
                for s in range(LONG):
                    wait_alone(pool, S["mv_ready"], of_step(t, s), passed_p)
                    wait_alone(pool, S["z_ready"], of_step(t, s - 2), passed_p)
                    inverse_root(nc, pool, chain, mv[:, s % 2], K.minus_half[:, 0:TILES], rstd[:, s % 2],
                                 1.0, 1e-6).then_inc(S["rstd_ready"], 1)

        @block.tensor
        def _(pe):
            start_counts(pe, [S[n] for n in e_names.split()])
            pe.wait_ge(weights, NW * DMA)
            with pe.Fori(0, STEPS // LONG) as t:
                for s in range(LONG + 1):
                    if s < LONG:
                        pe.wait_ge(loaded[s], 3 * DMA * t + 3 * DMA)
                        pe.wait_ge(S["xo_ready"], of_step(t, s - 2))
                        for j in range(TILES):
                            last = nc.tensor.transpose(yt_ps[:, s % 2, j * P:(j + 1) * P],
                                                       yin[:, s, j * P:(j + 1) * P], K.ident[:, :])
                        last.then_inc(S["ytp"], 1)
                    if 0 <= s - 1 < LONG:
                        b = s - 1
                        pe.wait_ge(S["z_ready"], of_step(t, b))
                        pe.wait_ge(S["zt_ready"], of_step(t, b - 1))
                        transpose_tiles(nc, zt_ps[:, 0], z[:, b % 2], K.ident).then_inc(S["ztp"], 1)
                        pe.wait_ge(S["zt_ready"], of_step(t, b))
                        pe.wait_ge(S["cx_ready"], of_step(t, b - 1))
                        nc.tensor.matmul(cx_ps[:, 0, :], w_sb[:, C:2 * C], zt[:, b % 2, :], start=True, stop=True)
                        nc.tensor.matmul(g_ps[0:G, 0, :], w_sb[:, 2 * C:2 * C + G], zt[:, b % 2, :],
                                         start=True, stop=True).then_inc(S["cxp"], 1)
                        pe.wait_ge(S["q_ready"], of_step(t, b - 1))
                        for j in range(TILES):
                            last = nc.tensor.matmul(q_ps[:, 0, j * P:(j + 1) * P], zt[:, b % 2, j * P:(j + 1) * P],
                                                    w_sb[:, 0:C], start=True, stop=True)
                        last.then_inc(S["qp"], 1)

        @block.scalar
        def _(act):
            start_counts(act, [S[n] for n in a_names.split()])
            for i in range(2):
                act.nop().then_inc(q_stored[i], DMA)
                act.nop().then_inc(cx_stored[i], 2 * DMA)
            act.wait_ge(weights, NW * DMA)
            with act.Fori(0, STEPS // LONG) as t:
                for s in range(LONG + 1):
                    if s < LONG:
                        act.wait_ge(S["ztp"], of_step(t, s))
                        act.wait_ge(S["qp"], of_step(t, s - 2))
                        nc.scalar.activation(zt[:, s % 2, :], zt_ps[:, 0, :], ACT.Copy).then_inc(S["zt_ready"], 1)
                        act.wait_ge(S["cxp"], of_step(t, s))
                        act.wait_ge(cx_stored[s % 2], 2 * DMA * (LONG // 2 * t + s // 2 + 1))
                        nc.scalar.activation(gates[:, s % 2, :], g_ps[0:G, 0, :], ACT.Identity, bias=bg[:, 0:1])
                        nc.scalar.activation(cx[:, s % 2, :], cx_ps[:, 0, :], ACT.Identity, bias=bc[:, 0:1])\
                            .then_inc(S["cx_ready"], 1)
                        act.wait_ge(S["cx_ready"], of_step(t, s))
                        u = LONG * t + s
                        act.dma_start(ctx_out[:, bass.ds(2 * u + PAD, 2), :],
                                      cx[:, s % 2, :].rearrange("c (r w) -> c r w", r=2)).then_inc(cx_stored[s % 2], DMA)
                        act.dma_start(gates_out[:, bass.ds(u * STEP, STEP)], gates[:, s % 2, :])\
                            .then_inc(cx_stored[s % 2], DMA)
                    if s:
                        b = s - 1
                        act.wait_ge(S["q_ready"], of_step(t, b))
                        act.dma_start(token_tiles(q_out, LONG * t + b), q[:, b % 2]).then_inc(q_stored[b % 2], DMA)
            for i in range(2):
                act.wait_ge(q_stored[i], DMA * (STEPS // 2 + 1))
                act.wait_ge(cx_stored[i], 2 * DMA * (STEPS // 2 + 1))


def depthwise(nc, K, name, k, pe_taps, image, kernel, gates, level, acc_in, image_out, acc_out, sums):
    R = k // 2
    WIN = RB + 2 * R
    WW = W + 2 * PAD
    taps = [(dy, dx) for dy in range(k) for dx in range(k)]
    dve_taps = taps[pe_taps:]
    TWO = 2
    n_loads = 3 if acc_in is not None else 2
    with ExitStack() as ctx:
        ph = Phase(nc, ctx, name)
        win = ph.sb("win", [P, TWO, WIN, WW])
        gate = ph.sb("gate", [P, TWO, CHUNK])
        acc = ph.sb("acc", [P, TWO, CHUNK])
        total = ph.sb("total", [P, TWO, CHUNK])
        cx = ph.sb("cx", [P, TWO, CHUNK])
        kt = ph.sb("kt", [P, k * k])
        krow = ph.sb("krow", [k * k, C])
        diag = ph.sb("diag", [P, pe_taps, P])
        conv_ps = ph.banks("conv_ps", 2 * CB)
        loaded = ph.sems("loaded", TWO)
        cx_stored = ph.sems("cx_stored", TWO)
        acc_stored = ph.sems("acc_stored", TWO)
        weights = ph.sem("weights")
        begun = ph.sem("begun")
        kt_ready = ph.sem("kt_ready")
        d_names = "conv_read total_ready"
        S = {n: ph.sem(n) for n in f"{d_names} conv_ready cx_ready acc_ready".split()}
        chain_d = ph.sem("chain_d")
        passed_p = ph.sem("passed_p")
        chain_p = ph.sem("chain_p")
        block = ph.block()

        @block.sync
        def _(sp):
            sp.dma_start(krow[:, :], kernel.rearrange("y x a c -> (y x a) c")).then_inc(weights, DMA)
            sp.wait_ge(begun, 1)

            def load(t, b):
                u = TWO * t + b
                sp.dma_start(win[:, b, :, PAD:PAD + W], image[:, bass.ds(RB * u + PAD - R, WIN), :]).then_inc(loaded[b], DMA)
                g = gates[level, bass.ds(u * CHUNK, CHUNK)]
                sp.dma_start(gate[:, b, :], bass.AP(g.tensor, g.offset, [[0, P]] + [list(d) for d in g.ap]))\
                    .then_inc(loaded[b], DMA)
                if acc_in is not None:
                    sp.dma_start(acc[:, b, :], acc_in[:, bass.ds(u * CHUNK, CHUNK)]).then_inc(loaded[b], DMA)

            def store(t, b):
                u = TWO * t + b
                sp.wait_ge(S["acc_ready"], of_step(t, b, TWO))
                sp.dma_start(acc_out[:, bass.ds(u * CHUNK, CHUNK)], acc[:, b, :]).then_inc(acc_stored[b], DMA)
                sp.wait_ge(acc_stored[b], DMA * (t + 1))

            for b in range(TWO):
                load(0, b)
            with sp.Fori(0, BLOCKS // TWO - 1) as t:
                for b in range(TWO):
                    store(t, b)
                    load(t + 1, b)
            for b in range(TWO):
                store(BLOCKS // TWO - 1, b)

        @block.vector
        def _(dve):
            start_counts(dve, [S[n] for n in d_names.split()], TWO)
            nc.vector.memset(win[:, :, :, :], 0.0).then_inc(begun, 1)
            dve.wait_ge(kt_ready, 1)
            nc.vector.tensor_copy(kt[:, :], conv_ps[:, 0, 0:k * k]).then_inc(begun, 1)
            dve.wait_ge(begun, 2)
            for i in range(pe_taps):
                last = nc.vector.tensor_scalar(diag[:, i, :], K.ident[:, :], kt[:, i:i + 1], None, ALU.mult)
            last.then_inc(begun, 1)
            dve.wait_ge(begun, 3)
            links = len(dve_taps) - 2
            with dve.Fori(0, BLOCKS // TWO) as t:
                chain = Chain(dve, chain_d, TWO * links * t)
                for b in range(TWO):
                    dve.wait_ge(loaded[b], n_loads * DMA * (t + 1))
                    dve.wait_ge(S["conv_ready"], of_step(t, b, TWO))
                    dve.wait_ge(S["cx_ready"], of_step(t, b - 2, TWO))
                    out = total[:, b, :].rearrange("p (r w) -> p r w", w=W)
                    conv = conv_ps[:, b * CB:(b + 1) * CB, :].rearrange("p n f -> p (n f)").rearrange("p (r w) -> p r w", w=W)
                    for i, (dy, dx) in enumerate(dve_taps):
                        x0 = dx + PAD - R
                        ins = nc.vector.scalar_tensor_tensor(
                            out, win[:, b, dy:dy + RB, x0:x0 + W], kt[:, pe_taps + i:pe_taps + i + 1],
                            out if i else conv, ALU.mult, ALU.add)
                        if i == 0:
                            ins.then_inc(S["conv_read"], 1)
                            dve.wait_ge(S["conv_read"], of_step(t, b, TWO))
                        elif i < len(dve_taps) - 1:
                            chain.link(ins)
                        else:
                            ins.then_inc(S["total_ready"], 1)
                assert chain.n == TWO * links

        @block.tensor
        def _(pe):
            start_counts(pe, [S["conv_ready"]], TWO)
            pe.wait_ge(weights, DMA)
            nc.tensor.transpose(conv_ps[:, 0, 0:k * k], krow[:, :], K.ident[0:k * k, 0:k * k]).then_inc(kt_ready, 1)
            pe.wait_ge(begun, 3)
            with pe.Fori(0, BLOCKS // TWO) as t:
                for b in range(TWO):
                    pe.wait_ge(loaded[b], n_loads * DMA * (t + 1))
                    pe.wait_ge(S["conv_read"], of_step(t, b - 2, TWO))
                    for i, (dy, dx) in enumerate(taps[:pe_taps]):
                        x0 = dx + PAD - R
                        for n in range(CB):
                            last = nc.tensor.matmul(conv_ps[:, b * CB + n, :], diag[:, i, :],
                                                    win[:, b, dy + 2 * n:dy + 2 * n + 2, x0:x0 + W],
                                                    start=(i == 0), stop=(i == pe_taps - 1))
                    last.then_inc(S["conv_ready"], 1)

        @block.scalar
        def _(act):
            start_counts(act, [S["cx_ready"]], TWO)
            for i in range(TWO):
                act.nop().then_inc(cx_stored[i], DMA)
            with act.Fori(0, BLOCKS // TWO) as t:
                for b in range(TWO):
                    u = TWO * t + b
                    act.wait_ge(S["total_ready"], of_step(t, b, TWO))
                    act.wait_ge(S["acc_ready"], of_step(t, b - 2, TWO))
                    if image_out is not None:
                        act.wait_ge(cx_stored[b], DMA * (t + 1))
                        nc.scalar.activation(cx[:, b, :], total[:, b, :], ACT.Gelu).then_inc(S["cx_ready"], 1)
                        act.wait_ge(S["cx_ready"], of_step(t, b, TWO))
                        act.dma_start(image_out[:, bass.ds(RB * u + PAD, RB), :],
                                      cx[:, b, :].rearrange("c (r w) -> c r w", w=W)).then_inc(cx_stored[b], DMA)
                    else:
                        nc.scalar.activation(cx[:, b, :], total[:, b, :], ACT.Gelu,
                                             accum_out=sums[:, bass.ds(u, 1)]).then_inc(S["cx_ready"], 1)
            if image_out is not None:
                for i in range(TWO):
                    act.wait_ge(cx_stored[i], DMA * (BLOCKS // TWO + 1))

        @block.gpsimd
        def _(pool):
            start_counts(pool, [S["acc_ready"]], TWO)
            with pool.Fori(0, BLOCKS // TWO) as t:
                chain = Chain(pool, chain_p, TWO * t)
                for b in range(TWO):
                    wait_alone(pool, loaded[b], n_loads * DMA * (t + 1), passed_p)
                    wait_alone(pool, S["cx_ready"], of_step(t, b, TWO), passed_p)
                    if acc_in is None:
                        nc.gpsimd.tensor_tensor(acc[:, b, :], cx[:, b, :], gate[:, b, :], ALU.mult)\
                            .then_inc(S["acc_ready"], 1)
                    else:
                        chain.link(nc.gpsimd.tensor_tensor(gate[:, b, :], cx[:, b, :], gate[:, b, :], ALU.mult))
                        nc.gpsimd.tensor_tensor(acc[:, b, :], acc[:, b, :], gate[:, b, :], ALU.add)\
                            .then_inc(S["acc_ready"], 1)


def modulate(nc, K, x, q, acc, gates, sums, wh, bh, gamma, beta, wp, bp, x_out):
    with ExitStack() as ctx:
        ph = Phase(nc, ctx, "mod")
        xin = ph.sb("xin", [P, LONG, TILES, C])
        qin = ph.sb("qin", [P, LONG, TILES, C])
        ain = ph.sb("ain", [P, LONG, STEP])
        gin = ph.sb("gin", [2, LONG, STEP])
        xo = ph.sb("xo", [P, LONG, TILES, C])
        prod = ph.sb("prod", [P, 2, TILES, C])
        stats = ph.sb("stats", [P, 2, TILES, 6])
        mv = ph.sb("mv", [P, 2, TILES, 2])
        rstd = ph.sb("rstd", [P, 2, TILES])
        z = ph.sb("z", [P, 2, TILES, C])
        zt = ph.sb("zt", [P, 2, STEP])
        w_h = ph.sb("w_h", [P, C])
        w_p = ph.sb("w_p", [P, C])
        rows = ph.sb("rows", [2, C])
        gb = ph.sb("gb", [P, 2])
        b_p = ph.sb("b_p", [P, C])
        mean = ph.sb("mean", [P, 1])
        glob = ph.sb("glob", [P, 1])
        m_ps = ph.banks("m_ps", 2)
        zt_ps = ph.banks("zt_ps")
        o_ps = ph.banks("o_ps")
        r_ps = ph.banks("r_ps")
        loaded = ph.sems("loaded", LONG)
        stored = ph.sems("stored", LONG)
        weights = ph.sem("weights")
        begun = ph.sem("begun")
        ones_set = ph.sem("ones_set")
        row_ready = ph.sem("row_ready")
        glob_ready = ph.sem("glob_ready")
        rowp = ph.sem("rowp")
        d_names = "prod_ready mv_ready z_ready xo_ready"
        a_names = "zt_ready"
        e_names = "mp ztp op"
        p_names = "rstd_ready xb_ready"
        S = {n: ph.sem(n) for n in f"{d_names} {a_names} {e_names} {p_names}".split()}
        chain_d = ph.sem("chain_d")
        chain_p = ph.sem("chain_p")
        passed_d = ph.sem("passed_d")
        passed_p = ph.sem("passed_p")
        block = ph.block()
        NW = 6

        @block.sync
        def _(sp):
            for dst, src in ((w_h[:, :], wh), (w_p[:, :], wp), (gb[:, 0:1], column(gamma)), (gb[:, 1:2], column(beta)),
                             (b_p[:, :], on_all(bp)), (rows[1:2, :], on_all(bh, 1))):
                sp.dma_start(dst, src).then_inc(weights, DMA)
            sp.wait_ge(ones_set, 1)

            def load(t, b):
                u = LONG * t + b
                sp.dma_start(ain[:, b, :], acc[:, bass.ds(u * STEP, STEP)]).then_inc(loaded[b], DMA)
                sp.dma_start(gin[0:1, b, :], gates[LEVELS:LEVELS + 1, bass.ds(u * STEP, STEP)]).then_inc(loaded[b], DMA)
                sp.dma_start(qin[:, b], token_tiles(q, u)).then_inc(loaded[b], DMA)
                sp.dma_start(xin[:, b], token_tiles(x, u)).then_inc(loaded[b], DMA)

            def store(t, b):
                sp.wait_ge(S["xo_ready"], of_step(t, b))
                sp.dma_start(token_tiles(x_out, LONG * t + b), xo[:, b]).then_inc(stored[b], DMA)

            for b in range(LONG):
                sp.nop().then_inc(stored[b], DMA)
                load(0, b)
            with sp.Fori(0, STEPS // LONG - 1) as t:
                for b in range(LONG):
                    store(t, b)
                    load(t + 1, b)
            for b in range(LONG):
                store(STEPS // LONG - 1, b)
            for b in range(LONG):
                sp.wait_ge(stored[b], DMA * (STEPS // LONG + 1))

        @block.vector
        def _(dve):
            start_counts(dve, [S[n] for n in d_names.split()])
            nc.vector.memset(gin[:, :, :], 1.0).then_inc(ones_set, 1)
            nc.vector.reduce_sum(mean[:, :], sums[:, :], AX.X).then_inc(begun, 1)
            dve.wait_ge(rowp, 1)
            nc.vector.tensor_copy(rows[0:1, :], r_ps[0:1, 0, 0:C]).then_inc(row_ready, 1)
            with dve.Fori(0, STEPS // LONG) as t:
                chain = Chain(dve, chain_d, LONG * t, passed_d)
                for s in range(LONG + 2):
                    if s < LONG:
                        dve.wait_ge(loaded[s], 4 * DMA * t + 4 * DMA)
                        dve.wait_ge(S["mp"], of_step(t, s))
                        dve.wait_ge(S["rstd_ready"], of_step(t, s - 2))
                        nc.vector.tensor_tensor(prod[:, s % 2].rearrange("p j c -> p (j c)"), m_ps[:, s % 2, :],
                                                qin[:, s].rearrange("p j c -> p (j c)"), ALU.mult)\
                            .then_inc(S["prod_ready"], 1)
                        wait_alone(dve, S["prod_ready"], of_step(t, s), passed_d)
                        column_stats(nc, chain, prod[:, s % 2], stats[:, s % 2], mv[:, s % 2])\
                            .then_inc(S["mv_ready"], 1)
                    if 0 <= s - 2 < LONG:
                        b = s - 2
                        dve.wait_ge(S["op"], of_step(t, b))
                        dve.wait_ge(S["xb_ready"], of_step(t, b))
                        dve.wait_ge(stored[b], DMA * t + DMA)
                        nc.vector.tensor_tensor(xo[:, b].rearrange("p j c -> p (j c)"), o_ps[:, 0, :],
                                                xin[:, b].rearrange("p j c -> p (j c)"), ALU.add)\
                            .then_inc(S["xo_ready"], 1)
                    if 0 <= s - 1 < LONG:
                        b = s - 1
                        dve.wait_ge(S["rstd_ready"], of_step(t, b))
                        dve.wait_ge(S["ztp"], of_step(t, b - 2))
                        normalize(nc, prod[:, b % 2], mv[:, b % 2], rstd[:, b % 2], z[:, b % 2])\
                            .then_inc(S["z_ready"], 1)
                assert chain.n == LONG

        @block.gpsimd
        def _(pool):
            start_counts(pool, [S[n] for n in p_names.split()])
            pool.wait_ge(weights, NW * DMA)
            with pool.Fori(0, STEPS // LONG) as t:
                chain = Chain(pool, chain_p, LONG * t)
                for s in range(LONG):
                    wait_alone(pool, S["mv_ready"], of_step(t, s), passed_p)
                    wait_alone(pool, S["z_ready"], of_step(t, s - 2), passed_p)
                    inverse_root(nc, pool, chain, mv[:, s % 2], K.minus_half[:, 0:TILES], rstd[:, s % 2],
                                 1.0, 1e-3).then_inc(S["rstd_ready"], 1)
                    pool.wait_ge(loaded[s], 4 * DMA * t + 4 * DMA)
                    nc.gpsimd.tensor_tensor(xin[:, s], xin[:, s], repeat_rows(b_p[:, :], TILES), ALU.add)\
                        .then_inc(S["xb_ready"], 1)

        @block.tensor
        def _(pe):
            start_counts(pe, [S[n] for n in e_names.split()])
            pe.wait_ge(weights, NW * DMA)
            pe.wait_ge(glob_ready, 1)
            nc.tensor.matmul(r_ps[0:1, 0, 0:C], glob[:, :], w_h[:, :], start=True, stop=True).then_inc(rowp, 1)
            pe.wait_ge(row_ready, 1)
            with pe.Fori(0, STEPS // LONG) as t:
                for s in range(LONG + 1):
                    if s < LONG:
                        pe.wait_ge(loaded[s], 4 * DMA * t + 4 * DMA)
                        pe.wait_ge(S["prod_ready"], of_step(t, s - 2))
                        for j in range(TILES):
                            tile = slice(j * P, (j + 1) * P)
                            nc.tensor.matmul(m_ps[:, s % 2, tile], ain[:, s, tile], w_h[:, :], start=True, stop=False)
                            last = nc.tensor.matmul(m_ps[:, s % 2, tile], gin[:, s, tile], rows[:, :],
                                                    start=False, stop=True)
                        last.then_inc(S["mp"], 1)
                    if s:
                        b = s - 1
                        pe.wait_ge(S["z_ready"], of_step(t, b))
                        pe.wait_ge(S["zt_ready"], of_step(t, b - 1))
                        transpose_tiles(nc, zt_ps[:, 0], z[:, b % 2], K.ident).then_inc(S["ztp"], 1)
                        pe.wait_ge(S["zt_ready"], of_step(t, b))
                        pe.wait_ge(S["xo_ready"], of_step(t, b - 1))
                        for j in range(TILES):
                            last = nc.tensor.matmul(o_ps[:, 0, j * P:(j + 1) * P], zt[:, b % 2, j * P:(j + 1) * P],
                                                    w_p[:, :], start=True, stop=True)
                        last.then_inc(S["op"], 1)

        @block.scalar
        def _(act):
            start_counts(act, [S[n] for n in a_names.split()])
            act.wait_ge(begun, 1)
            nc.scalar.activation(glob[:, :], mean[:, :], ACT.Gelu, scale=1.0 / N).then_inc(glob_ready, 1)
            act.wait_ge(weights, NW * DMA)
            with act.Fori(0, STEPS // LONG) as t:
                for s in range(LONG):
                    act.wait_ge(S["ztp"], of_step(t, s))
                    act.wait_ge(S["op"], of_step(t, s - 2))
                    nc.scalar.activation(zt[:, s % 2, :], zt_ps[:, 0, :], ACT.Identity, bias=gb[:, 1:2],
                                         scale=gb[:, 0:1]).then_inc(S["zt_ready"], 1)


KW = 3
TAPS = KW * KW
EDGE = 2
TAB_ROWS = H + 2 * EDGE - 1
TAB_COLS = W + 2 * EDGE
CELL = 2 * C
TAB_ROW = TAB_COLS * CELL
TABLE = TAB_ROWS * TAB_ROW


def flat_part(a, offset, dims):
    return bass.AP(a.tensor, a.offset + offset, dims)


def deform_front(nc, K, x, table, image):
    with ExitStack() as ctx:
        ph = Phase(nc, ctx, "df")
        xin = ph.sb("xin", [P, LONG, TILES, C])
        stats = ph.sb("stats", [P, 2, TILES, 6])
        mv = ph.sb("mv", [P, 2, TILES, 2])
        rstd = ph.sb("rstd", [P, 2, TILES])
        z = ph.sb("z", [P, LONG, TILES, C])
        zt = ph.sb("zt", [P, 2, STEP])
        zero = ph.sb("zero", [P, EDGE * TAB_ROW // P])
        zt_ps = ph.banks("zt_ps", 2)
        loaded = ph.sems("loaded", LONG)
        stored = ph.sems("stored", LONG)
        zt_stored = ph.sems("zt_stored", 2)
        zero_set = ph.sem("zero_set")
        edges = ph.sem("edges")
        S = {n: ph.sem(n) for n in "mv_ready z_ready zt_ready ztp rstd_ready".split()}
        chain_d = ph.sem("chain_d")
        chain_p = ph.sem("chain_p")
        passed_d = ph.sem("passed_d")
        passed_p = ph.sem("passed_p")
        block = ph.block()
        BODIES = STEPS // LONG

        @block.sync
        def _(sp):
            sp.wait_ge(zero_set, 1)
            n = 0
            for row in (0, TAB_ROWS - EDGE):
                sp.dma_start(flat_part(table, row * TAB_ROW, [[EDGE * TAB_ROW // P, P], [1, EDGE * TAB_ROW // P]]),
                             zero[:, :]).then_inc(edges, DMA)
                n += 1
            for row in range(EDGE, TAB_ROWS - EDGE, P):
                rows = min(P, TAB_ROWS - EDGE - row)
                for col in (0, TAB_COLS - EDGE):
                    sp.dma_start(flat_part(table, row * TAB_ROW + col * CELL, [[TAB_ROW, rows], [1, EDGE * CELL]]),
                                 zero[0:rows, 0:EDGE * CELL]).then_inc(edges, DMA)
                    n += 1
            sp.wait_ge(edges, n * DMA)

            def load(t, b):
                sp.dma_start(xin[:, b], token_tiles(x, LONG * t + b)).then_inc(loaded[b], DMA)

            def store(t, b):
                sp.wait_ge(S["z_ready"], of_step(t, b))
                u = LONG * t + b
                for r in range(2):
                    for part in range(2):
                        at = (EDGE + r - part) * TAB_ROW + EDGE * CELL + part * C
                        cells = bass.AP(table.tensor, u * (2 * TAB_ROW) + (table.offset + at),
                                        [[CELL, P], [P * CELL, 2], [1, C]])
                        sp.dma_start(cells, z[:, b, 2 * r:2 * r + 2, :]).then_inc(stored[b], DMA)

            for b in range(LONG):
                sp.nop().then_inc(stored[b], 4 * DMA)
                load(0, b)
            with sp.Fori(0, BODIES - 1) as t:
                for b in range(LONG):
                    store(t, b)
                    load(t + 1, b)
            for b in range(LONG):
                store(BODIES - 1, b)
            for b in range(LONG):
                sp.wait_ge(stored[b], 4 * DMA * (BODIES + 1))

        @block.vector
        def _(dve):
            nc.vector.memset(zero[:, :], 0.0).then_inc(zero_set, 1)
            start_counts(dve, [S["mv_ready"], S["z_ready"]])
            with dve.Fori(0, BODIES) as t:
                chain = Chain(dve, chain_d, LONG * t, passed_d)
                for s in range(LONG + 1):
                    if s < LONG:
                        dve.wait_ge(loaded[s], DMA * t + DMA)
                        dve.wait_ge(S["rstd_ready"], of_step(t, s - 2))
                        column_stats(nc, chain, xin[:, s], stats[:, s % 2], mv[:, s % 2]).then_inc(S["mv_ready"], 1)
                    if s:
                        b = s - 1
                        dve.wait_ge(S["rstd_ready"], of_step(t, b))
                        dve.wait_ge(stored[b], 4 * DMA * (t + 1))
                        dve.wait_ge(S["ztp"], of_step(t, b - LONG))
                        normalize(nc, xin[:, b], mv[:, b % 2], rstd[:, b % 2], z[:, b]).then_inc(S["z_ready"], 1)
                assert chain.n == LONG

        @block.gpsimd
        def _(pool):
            start_counts(pool, [S["rstd_ready"]])
            with pool.Fori(0, BODIES) as t:
                chain = Chain(pool, chain_p, LONG * t)
                for s in range(LONG):
                    wait_alone(pool, S["mv_ready"], of_step(t, s), passed_p)
                    wait_alone(pool, S["z_ready"], of_step(t, s - 2), passed_p)
                    inverse_root(nc, pool, chain, mv[:, s % 2], K.minus_half[:, 0:TILES], rstd[:, s % 2],
                                 1.0, 1e-6).then_inc(S["rstd_ready"], 1)

        @block.tensor
        def _(pe):
            start_counts(pe, [S["ztp"]])
            with pe.Fori(0, BODIES) as t:
                for s in range(LONG):
                    pe.wait_ge(S["z_ready"], of_step(t, s))
                    pe.wait_ge(S["zt_ready"], of_step(t, s - 2))
                    transpose_tiles(nc, zt_ps[:, s % 2], z[:, s], K.ident).then_inc(S["ztp"], 1)

        @block.scalar
        def _(act):
            start_counts(act, [S["zt_ready"]])
            for i in range(2):
                act.nop().then_inc(zt_stored[i], DMA)
            with act.Fori(0, BODIES) as t:
                for s in range(LONG):
                    act.wait_ge(S["ztp"], of_step(t, s))
                    act.wait_ge(zt_stored[s % 2], DMA * (LONG // 2 * t + s // 2 + 1))
                    nc.scalar.activation(zt[:, s % 2, :], zt_ps[:, s % 2, :], ACT.Copy).then_inc(S["zt_ready"], 1)
                    act.wait_ge(S["zt_ready"], of_step(t, s))
                    act.dma_start(image[:, bass.ds(2 * (LONG * t + s) + 1, 2), :],
                                  zt[:, s % 2, :].rearrange("c (r w) -> c r w", r=2)).then_inc(zt_stored[s % 2], DMA)
            for i in range(2):
                act.wait_ge(zt_stored[i], DMA * (STEPS // 2 + 1))


def deform(nc, K, x, table, image, kernel, bias, offset_w, offset_b, x_out):
    T2 = 2 * TAPS
    CORNERS = 4
    GROUPS = 3
    PER = TAPS // GROUPS
    TWO = 2
    BODIES = STEPS // TWO
    with ExitStack() as ctx:
        ph = Phase(nc, ctx, "dc")
        win = ph.sb("win", [P, TWO, 4, W + 2])
        xin = ph.sb("xin", [P, TWO, TILES, C])
        xo = ph.sb("xo", [P, TWO, TILES, C])
        grid = ph.sb("grid", [P, TILES, TAPS, 2])
        grid_i = ph.sb("grid_i", [P, TILES, TAPS, 2], i32)
        ob = ph.sb("ob", [P, T2])
        at = ph.sb("at", [P, TILES, TAPS, 2])
        low = ph.sb("low", [P, TILES, TAPS, 2])
        low_i = ph.sb("low_i", [P, TILES, TAPS, 2], i32)
        above = ph.sb("above", [P, TILES, TAPS, 2])
        frac = ph.sb("frac", [P, TILES, TAPS, 2, 2])
        cell = ph.sb("cell", [P, TILES * TAPS])
        cell_u = ph.sb("cell_u", [P, TWO, TILES * TAPS], u32)
        corner = ph.sb("corner", [P, TWO, TILES * TAPS, 2, 2])
        g = ph.sb("g", [P, TILES, TAPS, CORNERS, C])
        vt = ph.sb("vt", [P, TWO, GROUPS, PER * P])
        w_off = ph.sb("w_off", [P, TAPS, T2])
        w_k = ph.sb("w_k", [P, TAPS, C])
        b_k = ph.sb("b_k", [P, C])
        vt_ps = ph.banks("vt_ps", TWO * GROUPS)
        off_ps = ph.banks("off_ps")
        out_ps = ph.banks("out_ps")
        win_loaded = ph.sems("win_loaded", TWO)
        x_loaded = ph.sems("x_loaded", TWO)
        stored = ph.sems("stored", TWO)
        gathered = [K.by_pool.pop() for _ in range(TILES)]
        weights = ph.sem("weights")
        ready = ph.sem("ready")
        cleared = ph.sem("cleared")
        S = {n: ph.sem(n) for n in "offp off_read cell_ready xb_ready xo_ready".split()}
        Q = {n: ph.sem(n) for n in "weighted vtp vt_ready vt_used".split()}
        chain_d = ph.sem("chain_d")
        passed_p = ph.sem("passed_p")
        passed_d = ph.sem("passed_d")
        block = ph.block()
        NW = 4
        TB = TWO * TILES
        flat = flat_part(table, 0, [[1, TABLE], [1, 1]])

        def steps(t, b):
            return of_step(t, b, TWO)

        def tiles(t, b, j):
            return of_step(t, TILES * b + j, TB)

        @block.sync
        def _(sp):
            for dst, src in ((w_off[:, :, :], offset_w.rearrange("y x c o -> c (y x) o")),
                             (w_k[:, :, :], kernel.rearrange("y x c o -> c (y x) o")),
                             (ob[:, :], on_all(offset_b)), (b_k[:, :], on_all(bias))):
                sp.dma_start(dst, src).then_inc(weights, DMA)
            sp.wait_ge(cleared, 1)

            def load_window(t, b):
                sp.dma_start(win[:, b, :, 1:1 + W], image[:, bass.ds(2 * (TWO * t + b), 4), :])\
                    .then_inc(win_loaded[b], DMA)

            def load_x(t, b):
                sp.dma_start(xin[:, b], token_tiles(x, TWO * t + b)).then_inc(x_loaded[b], DMA)

            def step(t, b, more_windows, more):
                if more_windows:
                    sp.wait_ge(S["offp"], steps(t, b))
                    load_window(t + 1, b)
                sp.wait_ge(S["xo_ready"], steps(t, b))
                sp.dma_start(token_tiles(x_out, TWO * t + b), xo[:, b]).then_inc(stored[b], DMA)
                if more:
                    load_x(t + 1, b)

            for b in range(TWO):
                sp.nop().then_inc(stored[b], DMA)
                load_window(0, b)
                load_x(0, b)
            with sp.Fori(0, BODIES - 1) as t:
                for b in range(TWO):
                    step(t, b, True, True)
            for b in range(TWO):
                step(BODIES - 1, b, False, False)
            for b in range(TWO):
                sp.wait_ge(stored[b], DMA * (BODIES + 1))

        @block.gpsimd
        def _(pool):
            nc.gpsimd.iota(grid_i[:, :, :, 0], pattern=[[0, TILES], [0, TAPS]], base=0, channel_multiplier=0)\
                .then_inc(ready, 1)
            nc.gpsimd.iota(grid_i[:, :, :, 1], pattern=[[0, TILES], [0, TAPS]], base=0, channel_multiplier=1)\
                .then_inc(ready, 1)
            def step(t, b):
                for j in range(TILES):
                    if j == 0:
                        wait_alone(pool, S["cell_ready"], steps(t, b), passed_p)
                    wait_alone(pool, Q["vtp"], tiles(t, b - 1, j), passed_p)
                    for k in range(TAPS):
                        i = j * TAPS + k
                        pool.indirect_dma_start(
                            out=g[:, j, k].rearrange("p q c -> p (q c)"), out_offset=None, in_=flat,
                            in_offset=bass.IndirectOffsetOnAxis(ap=cell_u[:, b, i:i + 1], axis=0))\
                            .then_inc(gathered[j], DMA)

            with pool.Fori(0, BODIES) as t:
                for b in range(TWO):
                    step(t, b)

        @block.vector
        def _(dve):
            start_counts(dve, [S["off_read"], S["cell_ready"], S["xb_ready"], S["xo_ready"]], TWO)
            start_counts(dve, [Q["weighted"]], TB)
            nc.vector.memset(win[:, :, :, :], 0.0).then_inc(cleared, 1)
            dve.wait_ge(ready, 2)
            nc.vector.tensor_copy(grid[:, :, :, :], grid_i[:, :, :, :]).then_inc(ready, 1)
            dve.wait_ge(ready, 3)
            n = 3
            for k in range(TAPS):
                ky, kx = divmod(k, KW)
                for j in range(TILES):
                    r, h = divmod(j, 2)
                    nc.vector.tensor_scalar(grid[:, j, k, 0:1], grid[:, j, k, 0:1], float(r + ky - 1), None, ALU.add)\
                        .then_inc(ready, 1)
                    nc.vector.tensor_scalar(grid[:, j, k, 1:2], grid[:, j, k, 1:2], float(h * P + kx - 1), None, ALU.add)\
                        .then_inc(ready, 1)
                    n += 2
            dve.wait_ge(ready, n)
            dve.wait_ge(weights, NW * DMA)

            def cells(chain, t, b):
                dve.wait_ge(S["offp"], steps(t, b))
                a4 = at[:, :, :, :]
                ins = nc.vector.tensor_tensor(at[:, :, :, :].rearrange("p j k a -> p j (k a)"),
                                              off_ps[:, 0, 0:TILES * T2].rearrange("p (j o) -> p j o", o=T2),
                                              repeat_rows(ob[:, :], TILES), ALU.add)
                ins.then_inc(S["off_read"], 1)
                wait_alone(dve, S["off_read"], steps(t, b), passed_d)
                chain.link(nc.vector.tensor_tensor(a4, a4, grid[:, :, :, :], ALU.add))
                nc.vector.tensor_scalar(grid[:, :, :, 0], grid[:, :, :, 0], 2.0, None, ALU.add)
                chain.link(nc.vector.tensor_scalar(a4, a4, float(-EDGE), float(H), ALU.max, ALU.min))
                chain.link(nc.vector.tensor_copy(low_i[:, :, :, :], a4))
                chain.link(nc.vector.tensor_copy(low[:, :, :, :], low_i[:, :, :, :]))
                chain.link(nc.vector.tensor_tensor(above[:, :, :, :], low[:, :, :, :], a4, ALU.is_gt))
                chain.link(nc.vector.tensor_tensor(low[:, :, :, :], low[:, :, :, :], above[:, :, :, :], ALU.subtract))
                chain.link(nc.vector.tensor_tensor(frac[:, :, :, :, 1], a4, low[:, :, :, :], ALU.subtract))
                nc.vector.tensor_scalar(above[:, :, :, 0], low[:, :, :, 1], float(CELL),
                                        float(EDGE * TAB_ROW + EDGE * CELL), ALU.mult, ALU.add)
                chain.link(nc.vector.tensor_scalar(frac[:, :, :, :, 0], frac[:, :, :, :, 1], -1.0, 1.0,
                                                   ALU.mult, ALU.add))
                chain.link(nc.vector.scalar_tensor_tensor(
                    cell[:, :].rearrange("p (j k) -> p j k", k=TAPS), low[:, :, :, 0], float(TAB_ROW),
                    above[:, :, :, 0], ALU.mult, ALU.add))
                f = frac[:, :, :, :, :].rearrange("p j k a s -> p (j k) a s")
                xs, ys = f[:, :, 1, :], f[:, :, 0, :]
                d = [list(e) for e in ys.ap]
                ys = bass.AP(ys.tensor, ys.offset, [d[0], d[1], [0, 2], d[2]])
                nc.vector.tensor_tensor(corner[:, b], spread(xs, 2), ys, ALU.mult)
                nc.vector.tensor_copy(cell_u[:, b, :], cell[:, :]).then_inc(S["cell_ready"], 1)

            def add_bias(t, b):
                dve.wait_ge(x_loaded[b], DMA * (t + 1))
                nc.vector.tensor_tensor(xin[:, b], xin[:, b], repeat_rows(b_k[:, :], TILES), ALU.add)\
                    .then_inc(S["xb_ready"], 1)

            def result(t, b):
                dve.wait_ge(Q["vt_used"], tiles(t, b, TILES - 1))
                dve.wait_ge(S["xb_ready"], steps(t, b))
                dve.wait_ge(stored[b], DMA * (t + 1))
                nc.vector.tensor_tensor(xo[:, b].rearrange("p j c -> p (j c)"), out_ps[:, 0, :],
                                        xin[:, b].rearrange("p j c -> p (j c)"), ALU.add).then_inc(S["xo_ready"], 1)

            LINKS = 9
            first = Chain(dve, chain_d, 0, passed_d)
            cells(first, 0, 0)
            assert first.n == LINKS

            def body(t, first, more):
                chain = Chain(dve, chain_d, TWO * LINKS * t + LINKS, passed_d)
                for b in range(TWO):
                    if more or b == 0:
                        cells(chain, *((t, 1) if b == 0 else (t + 1, 0)))
                    for j in range(TILES):
                        if j == 0:
                            wait_alone(dve, S["cell_ready"], steps(t, b), passed_d)
                        dve.wait_ge(gathered[j], TAPS * DMA * (TWO * t + b + 1))
                        gj = g[:, j].rearrange("p k q c -> p (k q) c")
                        cw = corner[:, b, j * TAPS:(j + 1) * TAPS].rearrange("p k x y -> p (k x y)")
                        nc.vector.tensor_tensor(gj, gj, spread(cw, C), ALU.mult).then_inc(Q["weighted"], 1)
                        if j == 1 and not (first and b == 0):
                            result(*((t, 0) if b else (t - 1, 1)))
                    add_bias(t, b)

            body(0, True, True)
            with dve.Fori(1, BODIES - 1) as t:
                body(t, False, True)
            body(BODIES - 1, False, False)
            result(BODIES - 1, 1)

        @block.tensor
        def _(pe):
            start_counts(pe, [S["offp"]], TWO)
            start_counts(pe, [Q["vtp"]], TB)
            start_counts(pe, [Q["vt_used"]], TB)
            pe.wait_ge(weights, NW * DMA)

            def offsets(t, b):
                pe.wait_ge(win_loaded[b], DMA * (t + 1))
                pe.wait_ge(S["off_read"], steps(t, b - 1))
                for j in range(TILES):
                    r, h = divmod(j, 2)
                    for k in range(TAPS):
                        ky, kx = divmod(k, KW)
                        last = nc.tensor.matmul(off_ps[:, 0, j * T2:(j + 1) * T2],
                                                win[:, b, r + ky, h * P + kx:h * P + kx + P], w_off[:, k, :],
                                                start=(k == 0), stop=(k == TAPS - 1))
                last.then_inc(S["offp"], 1)

            def product(t, b, j):
                pe.wait_ge(Q["vt_ready"], tiles(t, b, j))
                if j == 0:
                    pe.wait_ge(S["xo_ready"], steps(t, b - 1))
                v = (TILES * b + j) % TWO
                for k in range(TAPS):
                    n, i = divmod(k, PER)
                    last = nc.tensor.matmul(out_ps[:, 0, j * C:(j + 1) * C], vt[:, v, n, i * P:(i + 1) * P],
                                            w_k[:, k, :], start=(k == 0), stop=(k == TAPS - 1))
                last.then_inc(Q["vt_used"], 1)

            def tile_sums(t, b, j):
                pe.wait_ge(Q["weighted"], tiles(t, b, j))
                pe.wait_ge(Q["vt_ready"], tiles(t, b, j - TWO))
                v = (TILES * b + j) % TWO
                for k in range(TAPS):
                    n, i = divmod(k, PER)
                    for q in range(CORNERS):
                        last = nc.tensor.matmul(vt_ps[:, v * GROUPS + n, i * P:(i + 1) * P], g[:, j, k, q, :],
                                                K.ident[:, :], start=(q == 0), stop=(q == CORNERS - 1))
                last.then_inc(Q["vtp"], 1)

            def body(t, first, more):
                for b in range(TWO):
                    if more or b == 0:
                        offsets(*((t, 1) if b == 0 else (t + 1, 0)))
                    for j in range(TILES):
                        tile_sums(t, b, j)
                        if j:
                            product(t, b, j - 1)
                        elif b:
                            product(t, 0, TILES - 1)
                        elif not first:
                            product(t - 1, 1, TILES - 1)

            offsets(0, 0)
            body(0, True, True)
            with pe.Fori(1, BODIES - 1) as t:
                body(t, False, True)
            body(BODIES - 1, False, False)
            product(BODIES - 1, 1, TILES - 1)

        @block.scalar
        def _(act):
            start_counts(act, [Q["vt_ready"]], TB)
            with act.Fori(0, BODIES) as t:
                for b in range(TWO):
                    for j in range(TILES):
                        act.wait_ge(Q["vtp"], tiles(t, b, j))
                        act.wait_ge(Q["vt_used"], tiles(t, b, j - TWO))
                        v = (TILES * b + j) % TWO
                        for n in range(GROUPS):
                            last = nc.scalar.activation(vt[:, v, n, :], vt_ps[:, v * GROUPS + n, 0:PER * P], ACT.Copy)
                        last.then_inc(Q["vt_ready"], 1)


def metaformer(nc, a, out):
    with ExitStack() as ctx:
        keep = Phase(nc, ctx, "keep")
        K = Namespace()
        K.ident = keep.sb("ident", [P, P])
        K.minus_half = keep.sb("minus_half", [P, 8])
        K.by_pool = keep.sems("by_pool", 3 * 2 + TILES)
        wx_mv = keep.sb("wx_mv", [P, 2])
        sums = keep.sb("sums", [P, BLOCKS])
        make_constants(nc, K.ident, K.minus_half)

        def dram(name, shape):
            return nc.dram_tensor(name, shape, fp32, kind="Internal").ap()

        x0 = a["x"].rearrange("a h w c -> (a h w) c")
        x_out = out.rearrange("a h w c -> (a h w) c")
        tokens_a = dram("tokens_a", [N, C])
        tokens_b = dram("tokens_b", [N, C])

        l0 = {n: a["L0_conv_" + n] for n in ("ln_gamma", "ln_beta", "Wq", "Wk", "Wv", "Wb", "Wg", "Wout")}
        zt = dram("zt", [C, N])
        att_bias = dram("l0_bias", [HEADS, N])
        attention_front(nc, K, x0, l0["ln_gamma"], l0["ln_beta"], l0["Wb"], zt, att_bias)
        attention(nc, K, x0, zt, att_bias, l0["Wq"], l0["Wk"], l0["Wv"], l0["Wg"], l0["Wout"], tokens_a)
        experts_of = [a["L0_ffn_" + n] for n in ("gate_w", "gate_b", "weight1", "weight2")]
        moe(nc, K, "m0", tokens_a, *experts_of)

        wx = dram("wx", [C, SEQ_BLOCKS, H, SEQ_BLOCK])
        ys = dram("ys", [C, SEQ_BLOCKS, H, SEQ_BLOCK])
        ema_conv(nc, K, tokens_a, a["L1_conv_W_exp"], a["L1_conv_b_exp"], a["L1_conv_W_con"], a["L1_conv_b_con"],
                 a["L1_ffn_W"], tokens_b, wx, wx_mv)
        recurrence(nc, K, wx, wx_mv, a["L1_ffn_gamma"], a["L1_ffn_beta"], a["L1_ffn_V"], ys)

        q = dram("q", [N, C])
        images = [dram(f"context{i}", [C, RING, W]) for i in range(LEVELS)]
        gates = dram("gates", [LEVELS + 1, N])
        acc = [dram(f"acc{i}", [C, N]) for i in range(LEVELS)]
        clear_rows(nc, "clr", images, PAD)
        focal_front(nc, K, tokens_b, ys, a["L2_conv_Wf"], a["L2_conv_bf"], tokens_a, q, images[0], gates)
        depthwise(nc, K, "dw0", 3, 4, images[0], a["L2_conv_k0"], gates, 0, None, images[1], acc[0], None)
        depthwise(nc, K, "dw1", 5, 10, images[1], a["L2_conv_k1"], gates, 1, acc[0], images[2], acc[1], None)
        depthwise(nc, K, "dw2", 7, 19, images[2], a["L2_conv_k2"], gates, 2, acc[1], None, acc[2], sums)
        modulate(nc, K, tokens_a, q, acc[2], gates, sums,
                 *[a["L2_conv_" + n] for n in ("Wh", "bh", "gamma", "beta", "Wp", "bp")], tokens_b)
        experts_of = [a["L2_ffn_" + n] for n in ("gate_w", "gate_b", "weight1", "weight2")]
        moe(nc, K, "m2", tokens_b, *experts_of)

        table = dram("table", [TABLE])
        image = dram("image", [C, H + 2, W])
        clear_rows(nc, "clr3", [image], 1)
        deform_front(nc, K, tokens_b, table, image)
        deform(nc, K, tokens_b, table, image,
               *[a["L3_conv_" + n] for n in ("kernel", "bias", "offset_w", "offset_b")], x_out)
        experts_of = [a["L3_ffn_" + n] for n in ("gate_w", "gate_b", "weight1", "weight2")]
        moe(nc, K, "m3", x_out, *experts_of)


_TRANSPOSED = ("L0_ffn_gate_w", "L2_ffn_gate_w", "L3_ffn_gate_w", "L1_conv_W_exp", "L1_conv_W_con", "L1_ffn_W",
               "L1_ffn_V")


def kernel(**inputs):
    import numpy as _np
    import concourse.bacc as _bacc
    from concourse import mybir as _mybir
    from concourse.bass_utils import run_bass_kernel_spmd as _run

    nc = _bacc.Bacc("TRN2", target_bir_lowering=False, num_devices=1)
    arrays, args = {}, {}
    for name in inputs:
        v = _np.asarray(inputs[name])
        v = _np.ascontiguousarray(v.T if name in _TRANSPOSED else v)
        arrays[f"in_{name}_dram"] = v
        args[name] = nc.dram_tensor(f"in_{name}_dram", v.shape, _mybir.dt.from_np(v.dtype), kind="ExternalInput").ap()
    out = nc.dram_tensor("out_0_dram", (1, H, W, C), _mybir.dt.from_np(_np.dtype("float32")), kind="ExternalOutput").ap()
    metaformer(nc, args, out)
    r = _run(nc, [arrays], core_ids=[0])
    return r.results[0]["out_0_dram"]
```

```python
import numpy as np
import concourse.bass as bass
from concourse import mybir
from contextlib import ExitStack

fp32 = mybir.dt.float32
i32 = mybir.dt.int32
u32 = mybir.dt.uint32
ACT = mybir.ActivationFunctionType
ALU = mybir.AluOpType
AX = mybir.AxisListType

P = 128
C = 128
H = W = 256
N = H * W
TILES = 4
STEP = TILES * P
STEPS = N // STEP
DMA = 16
PAD = 3


class Namespace:
    pass


class Phase:

    def __init__(self, nc, ctx, name):
        self.nc, self.ctx, self.name, self.used = nc, ctx, name, []

    def sb(self, name, shape, dt=fp32):
        return self.ctx.enter_context(self.nc.sbuf_tensor(f"{self.name}_{name}", shape, dt))

    def banks(self, name, n=1):
        return self.ctx.enter_context(self.nc.psum_tensor(f"{self.name}_{name}", [P, n, 512], fp32))

    def sem(self, name):
        s = self.ctx.enter_context(self.nc.semaphore(f"{self.name}_{name}"))
        self.used.append(s)
        return s

    def block(self):
        self.ctx.callback(self.zero)
        return self.ctx.enter_context(self.nc.Block())

    def zero(self):
        with self.nc.Block() as block:
            @block.gpsimd
            def _(pool):
                for s in self.used:
                    pool.sem_clear(s)

    def sems(self, name, n):
        return [self.sem(f"{name}{i}") for i in range(n)]


def wait_alone(eng, sem, value, passed):
    eng.wait_ge(sem, value)
    eng.sem_inc(passed, 1)


class Chain:

    def __init__(self, eng, sem, before=0, passed=None):
        self.eng, self.sem, self.before, self.passed, self.n = eng, sem, before, passed, 0

    def link(self, ins):
        self.n += 1
        ins.then_inc(self.sem, 1)
        self.eng.wait_ge(self.sem, self.before + self.n)
        if self.passed is not None:
            self.eng.sem_inc(self.passed, 1)


LONG = 8
MV = 4


def start_counts(eng, sems, n=LONG):
    for s in sems:
        eng.nop().then_inc(s, n)


def of_step(t, s, n=LONG):
    return n * t + (s + 1 + n)


def times(t, s, n=1):
    return n * DMA * t + n * DMA * (s // LONG + 1)


def of_pair(t, s, n=1):
    return n * DMA * (LONG // 2) * t + n * DMA * (s // 2 + 1)


def pipelined(eng, stages, chain=None, links=0, bodies=STEPS // LONG):
    deepest = max(lag for lag, _ in stages)
    assert deepest <= LONG
    left_out = 0

    def body(t, first, last):
        if chain is not None:
            chain.before, chain.n = (0 if first else links * LONG * t - left_out), 0
        for s in range(LONG + (deepest if last else 0)):
            for lag, stage in stages:
                if s - lag < LONG and (s >= lag or not first):
                    stage(t, s - lag)

    body(0, True, False)
    if chain is not None:
        left_out = links * LONG - chain.n
    with eng.Fori(1, bodies - 1) as t:
        body(t, False, False)
    body(bodies - 1, False, True)


def token_tiles(x, u):
    return x[bass.ds(u * STEP, STEP), :].rearrange("(j p) c -> p j c", p=P)


def column_stats(nc, chain, x4, stats, mv):
    for j in range(TILES):
        last = nc.vector.bn_stats(stats[:, j, :], x4[:, j, :])
    chain.link(last)
    for j in range(TILES):
        last = nc.vector.bn_aggr(mv[:, j, :], stats[:, j, :])
    return last


def normalize(nc, x4, mv, rstd, z4):
    for j in range(TILES):
        last = nc.vector.tensor_scalar(z4[:, j, :], x4[:, j, :], mv[:, j, 0:1], rstd[:, j:j + 1],
                                       ALU.subtract, ALU.mult)
    return last


def inverse_root(nc, pool, chain, mv, minus_half, rstd, scale, eps):
    chain.link(nc.gpsimd.tensor_scalar(rstd, mv[:, :, 1], scale, eps, ALU.mult, ALU.add))
    return nc.gpsimd.tensor_tensor(rstd, rstd, minus_half, ALU.pow)


def transpose_tiles(nc, bank, z4, ident):
    for j in range(TILES):
        last = nc.tensor.transpose(bank[:, j * P:(j + 1) * P], z4[:, j, :], ident[:, :])
    return last


def make_constants(nc, ident, minus_half):
    with ExitStack() as ctx:
        ph = Phase(nc, ctx, "const")
        done = ph.sem("done")
        block = ph.block()

        @block.gpsimd
        def _(pool):
            nc.gpsimd.memset(ident[:, :], 0.0).then_inc(done, 1)
            nc.gpsimd.memset(minus_half[:, :], -0.5).then_inc(done, 1)
            pool.wait_ge(done, 2)
            nc.gpsimd.affine_select(out=ident[:, :], in_=ident[:, :], compare_op=ALU.not_equal,
                                    fill=1.0, base=0, pattern=[[-1, P]],
                                    channel_multiplier=1).then_inc(done, 1)
            pool.wait_ge(done, 3)


def attention_front(nc, K, x, gamma, beta, wb, zt_out, bias_out):
    BODIES = STEPS // LONG
    with ExitStack() as ctx:
        ph = Phase(nc, ctx, "l0f")
        xin = ph.sb("xin", [P, LONG, TILES, C])
        stats = ph.sb("stats", [P, MV, TILES, 6])
        mv = ph.sb("mv", [P, MV, TILES, 2])
        rstd = ph.sb("rstd", [P, MV, TILES])
        z = ph.sb("z", [P, 2, TILES, C])
        zt = ph.sb("zt", [P, MV, STEP])
        bias = ph.sb("bias", [4, 2, STEP])
        gb = ph.sb("gb", [P, 2])
        wb_sb = ph.sb("wb", [P, 4])
        zt_ps = ph.banks("zt_ps", 2)
        bias_ps = ph.banks("bias_ps", 2)
        loaded = ph.sems("loaded", LONG)
        zt_stored = ph.sems("zt_stored", MV)
        bias_stored = ph.sems("bias_stored", 2)
        weights = ph.sem("weights")
        S = {n: ph.sem(n) for n in "mv_ready rstd_ready z_ready ztp zt_ready biasp bias_ready".split()}
        chain_d = ph.sem("chain_d")
        chain_p = ph.sem("chain_p")
        passed_d = ph.sem("passed_d")
        passed_p = ph.sem("passed_p")
        block = ph.block()

        @block.sync
        def _(sp):
            sp.dma_start(gb[:, 0:1], gamma.rearrange("(c a) -> c a", a=1)).then_inc(weights, DMA)
            sp.dma_start(gb[:, 1:2], beta.rearrange("(c a) -> c a", a=1)).then_inc(weights, DMA)
            sp.dma_start(wb_sb[:, :], wb).then_inc(weights, DMA)

            def load(t, b):
                sp.dma_start(xin[:, b], token_tiles(x, LONG * t + b)).then_inc(loaded[b], DMA)

            for b in range(LONG):
                load(0, b)
            with sp.Fori(0, BODIES - 1) as t:
                for b in range(LONG):
                    sp.wait_ge(S["z_ready"], of_step(t, b))
                    load(t + 1, b)

        @block.vector
        def _(dve):
            start_counts(dve, [S["mv_ready"], S["z_ready"]])
            chain = Chain(dve, chain_d, 0, passed_d)

            def moments(t, s):
                dve.wait_ge(loaded[s % LONG], times(t, s))
                dve.wait_ge(S["rstd_ready"], of_step(t, s - MV))
                dve.wait_ge(S["z_ready"], of_step(t, s - MV))
                column_stats(nc, chain, xin[:, s % LONG], stats[:, s % MV], mv[:, s % MV])\
                    .then_inc(S["mv_ready"], 1)

            def norm(t, s):
                dve.wait_ge(S["rstd_ready"], of_step(t, s))
                dve.wait_ge(S["ztp"], of_step(t, s - 2))
                normalize(nc, xin[:, s % LONG], mv[:, s % MV], rstd[:, s % MV], z[:, s % 2])\
                    .then_inc(S["z_ready"], 1)

            pipelined(dve, ((0, moments), (2, norm)), chain, 1)

        @block.gpsimd
        def _(pool):
            start_counts(pool, [S["rstd_ready"]])
            chain = Chain(pool, chain_p)

            def root(t, s):
                wait_alone(pool, S["mv_ready"], of_step(t, s), passed_p)
                wait_alone(pool, S["z_ready"], of_step(t, s - MV), passed_p)
                inverse_root(nc, pool, chain, mv[:, s % MV], K.minus_half[:, 0:TILES], rstd[:, s % MV],
                             1.0 + 1e-5, 1e-11).then_inc(S["rstd_ready"], 1)

            pipelined(pool, ((0, root),), chain, 1)

        @block.tensor
        def _(pe):
            start_counts(pe, [S["ztp"], S["biasp"]])
            pe.wait_ge(weights, 3 * DMA)

            def turn(t, s):
                pe.wait_ge(S["z_ready"], of_step(t, s))
                pe.wait_ge(S["zt_ready"], of_step(t, s - 2))
                transpose_tiles(nc, zt_ps[:, s % 2], z[:, s % 2], K.ident).then_inc(S["ztp"], 1)

            def attention_bias(t, s):
                pe.wait_ge(S["zt_ready"], of_step(t, s))
                pe.wait_ge(S["bias_ready"], of_step(t, s - 2))
                nc.tensor.matmul(bias_ps[0:4, s % 2, :], wb_sb[:, :], zt[:, s % MV, :],
                                 start=True, stop=True).then_inc(S["biasp"], 1)

            pipelined(pe, ((3, turn), (4, attention_bias)))

        @block.scalar
        def _(act):
            start_counts(act, [S["zt_ready"], S["bias_ready"]])
            for i in range(MV):
                act.nop().then_inc(zt_stored[i], DMA)
            for i in range(2):
                act.nop().then_inc(bias_stored[i], DMA)
            act.wait_ge(weights, 3 * DMA)

            def keep_zt(t, s):
                act.wait_ge(S["ztp"], of_step(t, s))
                act.wait_ge(zt_stored[s % MV], DMA * (LONG // MV) * t + DMA * (s // MV + 1))
                act.wait_ge(S["biasp"], of_step(t, s - MV))
                nc.scalar.activation(zt[:, s % MV, :], zt_ps[:, s % 2, :], ACT.Identity,
                                     bias=gb[:, 1:2], scale=gb[:, 0:1]).then_inc(S["zt_ready"], 1)

            def store_zt(t, s):
                act.wait_ge(S["zt_ready"], of_step(t, s))
                act.dma_start(zt_out[:, bass.ds((LONG * t + s) * STEP, STEP)], zt[:, s % MV, :])\
                    .then_inc(zt_stored[s % MV], DMA)

            def keep_bias(t, s):
                act.wait_ge(S["biasp"], of_step(t, s))
                act.wait_ge(bias_stored[s % 2], of_pair(t, s))
                nc.scalar.activation(bias[:, s % 2, :], bias_ps[0:4, s % 2, :], ACT.Copy)\
                    .then_inc(S["bias_ready"], 1)
                act.wait_ge(S["bias_ready"], of_step(t, s))
                act.dma_start(bias_out[:, bass.ds((LONG * t + s) * STEP, STEP)], bias[:, s % 2, :])\
                    .then_inc(bias_stored[s % 2], DMA)

            pipelined(act, ((3, keep_zt), (5, keep_bias), (3, store_zt)))
            for i in range(MV):
                act.wait_ge(zt_stored[i], DMA * (STEPS // MV + 1))
            for i in range(2):
                act.wait_ge(bias_stored[i], DMA * (STEPS // 2 + 1))


HEADS, HDIM = 4, 32


def spread(ap, n):
    return bass.AP(ap.tensor, ap.offset, [list(d) for d in ap.ap] + [[0, n]])


def attention(nc, K, x, zt, bias, wq, wk, wv, wg, wout, x_out):
    BODIES = H // LONG
    LIVE = 4
    TR = 4
    with ExitStack() as ctx:
        ph = Phase(nc, ctx, "att")
        zrow = ph.sb("zrow", [P, LONG, W])
        xrow = ph.sb("xrow", [P, LONG, 2, C])
        w_qk = ph.sb("w_qk", [P, 2 * C])
        w_vg = ph.sb("w_vg", [P, 2 * C])
        w_out = ph.sb("w_out", [P, C])
        bias_sb = ph.sb("bias", [P, 2, HEADS, W])
        qk = ph.sb("qk", [P, 2, 2 * W])
        v = ph.sb("v", [P, LIVE, 2, C])
        gate = ph.sb("gate", [P, LIVE, 2, C])
        prob = ph.sb("prob", [P, 2, 2, HEADS, W])
        most = ph.sb("most", [P, 2, 8])
        neg = ph.sb("neg", [P, 2, 8])
        total = ph.sb("total", [P, LIVE, 8])
        inv = ph.sb("inv", [P, 2, 8])
        probt = ph.sb("probt", [P, 2, TR, HEADS * P])
        o = ph.sb("o", [P, 2, 2 * C])
        ot = ph.sb("ot", [P, 2, W])
        y = ph.sb("y", [P, LONG, 2, C])
        qk_ps = ph.banks("qk_ps")
        vg_ps = ph.banks("vg_ps")
        s_ps = ph.banks("s_ps", HEADS)
        b_ps = ph.banks("b_ps", 2)
        loaded = ph.sems("loaded", LONG)
        stored = ph.sems("stored", LONG)
        weights = ph.sem("weights")
        scaled = ph.sem("scaled")
        names = "proj scores avp otp yp qk_ready vg_ready exp_ready neg_ready o_ready ot_ready y_ready"
        S = {n: ph.sem(n) for n in names.split()}
        trp = ph.sem("trp")
        tr_ready = ph.sem("tr_ready")
        chain_d = ph.sem("chain_d")
        passed_d = ph.sem("passed_d")
        block = ph.block()
        NW = 8 + 5

        def of_block(t, s, k):
            return TR * LONG * t + TR * (s + LONG) + k + 1

        def there(t, s):
            return s < LONG or not isinstance(t, int) or t < BODIES - 1

        def bank(s, lag, n):
            return b_ps[:, (7 * (s + lag) + n) % 2, :]

        @block.sync
        def _(sp):
            sp.dma_start(w_qk[:, 0:C], wq).then_inc(weights, DMA)
            sp.dma_start(w_qk[:, C:2 * C], wk).then_inc(weights, DMA)
            sp.dma_start(w_vg[:, 0:C], wv).then_inc(weights, DMA)
            sp.dma_start(w_vg[:, C:2 * C], wg).then_inc(weights, DMA)
            sp.dma_start(w_out[:, :], wout).then_inc(weights, DMA)
            for j in range(2):
                for h in range(HEADS):
                    sp.dma_start(bias_sb[:, j, h, :],
                                 bias[h, j * P * W:(j + 1) * P * W].rearrange("(p k) -> p k", k=W))\
                        .then_inc(weights, DMA)

            def load(t, b):
                i = LONG * t + b
                sp.dma_start(zrow[:, b, :], zt[:, bass.ds(i * W, W)]).then_inc(loaded[b], DMA)
                sp.dma_start(xrow[:, b], x[bass.ds(i * W, W), :].rearrange("(j p) c -> p j c", p=P))\
                    .then_inc(loaded[b], DMA)

            def store(t, b):
                i = LONG * t + b
                sp.wait_ge(S["y_ready"], of_step(t, b))
                sp.dma_start(x_out[bass.ds(i * W, W), :].rearrange("(j p) c -> p j c", p=P), y[:, b])\
                    .then_inc(stored[b], DMA)

            for b in range(LONG):
                sp.nop().then_inc(stored[b], DMA)
                load(0, b)
            with sp.Fori(0, BODIES - 1) as t:
                for b in range(LONG):
                    store(t, b)
                    load(t + 1, b)
            for b in range(LONG):
                store(BODIES - 1, b)
            for b in range(LONG):
                sp.wait_ge(stored[b], DMA * (BODIES + 1))

        @block.tensor
        def _(pe):
            start_counts(pe, [S[n] for n in "proj scores avp otp yp".split()])
            start_counts(pe, [trp], TR * LONG)
            pe.wait_ge(weights, NW * DMA)
            pe.wait_ge(scaled, 1)

            def project(t, s):
                pe.wait_ge(loaded[s % LONG], times(t, s, 2))
                pe.wait_ge(S["vg_ready"], of_step(t, s - 1))
                for a in range(2):
                    nc.tensor.matmul(qk_ps[:, 0, a * W:(a + 1) * W], w_qk[:, a * C:(a + 1) * C],
                                     zrow[:, s % LONG, :], start=True, stop=True)
                for j in range(2):
                    last = nc.tensor.matmul(vg_ps[:, 0, j * W:(j + 1) * W], zrow[:, s % LONG, j * P:(j + 1) * P],
                                            w_vg[:, :], start=True, stop=True)
                last.then_inc(S["proj"], 1)

            def score(t, s):
                pe.wait_ge(S["qk_ready"], of_step(t, s))
                pe.wait_ge(S["neg_ready"], of_step(t, s - 1))
                for j in range(2):
                    for h in range(HEADS):
                        part = slice(h * HDIM, (h + 1) * HDIM)
                        last = nc.tensor.matmul(s_ps[:, h, j * W:(j + 1) * W],
                                                qk[part, s % 2, j * P:(j + 1) * P],
                                                qk[part, s % 2, W:2 * W], start=True, stop=True)
                last.then_inc(S["scores"], 1)

            def turn(t, s, blk, into):
                j, k = divmod(blk, 2)
                for h in range(HEADS):
                    last = nc.tensor.transpose(into[:, h * P:(h + 1) * P],
                                               prob[:, s % 2, j, h, k * P:(k + 1) * P], K.ident[:, :])
                last.then_inc(trp, 1)

            def turn_first(t, s):
                pe.wait_ge(S["exp_ready"], of_step(t, s))
                pe.wait_ge(tr_ready, of_block(t, s - 1, TR - 1))
                pe.wait_ge(S["ot_ready"], of_step(t, s - 2))
                turn(t, s, 0, bank(s, 2, 0))
                pe.wait_ge(S["y_ready"], of_step(t, s - 3))
                turn(t, s, 1, bank(s, 2, 1))

            def values(t, s):
                if there(t, s + 1):
                    pe.wait_ge(tr_ready, of_block(t, s + 1, 0))
                else:
                    pe.wait_ge(tr_ready, of_block(t, s, TR - 1))
                pe.wait_ge(S["ot_ready"], of_step(t, s - 1))
                into = bank(s, 3, 2)
                for j in range(2):
                    for h in range(HEADS):
                        for k in range(2):
                            last = nc.tensor.matmul(into[:, j * C + h * HDIM:j * C + (h + 1) * HDIM],
                                                    probt[:, s % 2, 2 * j + k, h * P:(h + 1) * P],
                                                    v[:, s % LIVE, k, h * HDIM:(h + 1) * HDIM],
                                                    start=(k == 0), stop=(k == 1))
                last.then_inc(S["avp"], 1)

            def turn_second(t, s):
                pe.wait_ge(tr_ready, of_block(t, s, 1))
                turn(t, s, 2, bank(s, 2, 3))
                pe.wait_ge(S["o_ready"], of_step(t, s - 1))
                turn(t, s, 3, bank(s, 2, 4))

            def turn_output(t, s):
                pe.wait_ge(S["o_ready"], of_step(t, s))
                if there(t, s + 1):
                    pe.wait_ge(tr_ready, of_block(t, s + 1, 2))
                pe.wait_ge(S["y_ready"], of_step(t, s - 2))
                for j in range(2):
                    last = nc.tensor.transpose(bank(s, 3, 5)[:, j * P:(j + 1) * P], o[:, s % 2, j * C:(j + 1) * C],
                                               K.ident[:, :])
                last.then_inc(S["otp"], 1)

            def result(t, s):
                pe.wait_ge(S["ot_ready"], of_step(t, s))
                if there(t, s + 2):
                    pe.wait_ge(tr_ready, of_block(t, s + 2, 3))
                if there(t, s + 1):
                    pe.wait_ge(S["o_ready"], of_step(t, s + 1))
                for j in range(2):
                    last = nc.tensor.matmul(bank(s, 4, 6)[:, j * C:(j + 1) * C], ot[:, s % 2, j * P:(j + 1) * P],
                                            w_out[:, :], start=True, stop=True)
                last.then_inc(S["yp"], 1)

            pipelined(pe, ((1, score), (2, turn_first), (0, project), (3, values), (2, turn_second),
                           (3, turn_output), (4, result)), bodies=BODIES)

        @block.scalar
        def _(act):
            start_counts(act, [S[n] for n in "qk_ready vg_ready exp_ready".split()])

            def evacuate(t, s):
                act.wait_ge(S["proj"], of_step(t, s))
                act.wait_ge(S["scores"], of_step(t, s - 2))
                nc.scalar.activation(qk[:, s % 2, :], qk_ps[:, 0, :], ACT.Copy).then_inc(S["qk_ready"], 1)
                act.wait_ge(S["o_ready"], of_step(t, s - LIVE))
                vg = vg_ps[:, 0, :].rearrange("p (j c) -> p j c", j=2)
                nc.scalar.activation(v[:, s % LIVE], vg[:, :, 0:C], ACT.Copy)
                nc.scalar.activation(gate[:, s % LIVE], vg[:, :, C:2 * C], ACT.Tanh, scale=0.5)\
                    .then_inc(S["vg_ready"], 1)

            def exponentials(t, s):
                act.wait_ge(S["neg_ready"], of_step(t, s))
                act.wait_ge(S["o_ready"], of_step(t, s - LIVE))
                for j in range(2):
                    for h in range(HEADS):
                        m = j * HEADS + h
                        last = nc.scalar.activation(prob[:, s % 2, j, h, :], prob[:, s % 2, j, h, :], ACT.Exp,
                                                    bias=neg[:, s % 2, m:m + 1],
                                                    accum_out=total[:, s % LIVE, m:m + 1])
                last.then_inc(S["exp_ready"], 1)

            pipelined(act, ((0, evacuate), (1, exponentials)), bodies=BODIES)

        @block.vector
        def _(dve):
            start_counts(dve, [S[n] for n in "neg_ready o_ready ot_ready y_ready".split()])
            start_counts(dve, [tr_ready], TR * LONG)
            dve.wait_ge(weights, NW * DMA)
            nc.vector.tensor_scalar(w_qk[:, 0:C], w_qk[:, 0:C], float(HDIM) ** -0.5, None, ALU.mult)\
                .then_inc(scaled, 1)
            chain = Chain(dve, chain_d, 0, passed_d)

            def maxima(t, s):
                wait_alone(dve, trp, of_block(t, s - 2, TR - 1), passed_d)
                wait_alone(dve, S["scores"], of_step(t, s), passed_d)
                for j in range(2):
                    for h in range(HEADS):
                        m = j * HEADS + h
                        last = nc.vector.tensor_tensor_reduce(
                            out=prob[:, s % 2, j, h, :], in0=s_ps[:, h, j * W:(j + 1) * W],
                            in1=bias_sb[:, j, h, :], scale=1.0, scalar=-3.0e38, op0=ALU.add, op1=ALU.max,
                            accum_out=most[:, s % 2, m:m + 1])
                chain.link(last)
                nc.vector.tensor_scalar(neg[:, s % 2, :], most[:, s % 2, :], -1.0, None, ALU.mult)\
                    .then_inc(S["neg_ready"], 1)

            def keep_turned(t, s, blk, bank):
                dve.wait_ge(trp, of_block(t, s, blk))
                nc.vector.tensor_copy(probt[:, s % 2, blk, :], bank).then_inc(tr_ready, 1)

            def keep_first(t, s):
                dve.wait_ge(S["avp"], of_step(t, s - 2))
                keep_turned(t, s, 0, bank(s, 2, 0))
                keep_turned(t, s, 1, bank(s, 2, 1))

            def keep_second(t, s):
                keep_turned(t, s, 2, bank(s, 2, 3))
                keep_turned(t, s, 3, bank(s, 2, 4))

            def gated(t, s):
                dve.wait_ge(S["exp_ready"], of_step(t, s))
                iv = inv[:, s % 2, :]
                chain.link(nc.vector.tensor_scalar(iv, total[:, s % LIVE, :], 2.0, None, ALU.mult))
                nc.vector.reciprocal(iv, iv)
                dve.wait_ge(S["avp"], of_step(t, s))
                dve.wait_ge(S["vg_ready"], of_step(t, s))
                dve.wait_ge(S["otp"], of_step(t, s - 2))
                chain.link(nc.vector.scalar_tensor_tensor(
                    o[:, s % 2, :], gate[:, s % LIVE].rearrange("p j c -> p (j c)"), 1.0,
                    bank(s, 3, 2)[:, 0:2 * C], ALU.add, ALU.mult))
                heads = o[:, s % 2, :].rearrange("p (m d) -> p m d", d=HDIM)
                nc.vector.tensor_tensor(heads, heads, spread(iv, HDIM), ALU.mult).then_inc(S["o_ready"], 1)

            def keep_output(t, s):
                dve.wait_ge(S["otp"], of_step(t, s))
                dve.wait_ge(S["yp"], of_step(t, s - 2))
                nc.vector.tensor_copy(ot[:, s % 2, :], bank(s, 3, 5)[:, 0:W]).then_inc(S["ot_ready"], 1)

            def add(t, s):
                b = s % LONG
                dve.wait_ge(S["yp"], of_step(t, s))
                dve.wait_ge(stored[b], times(t, s))
                nc.vector.tensor_tensor(y[:, b].rearrange("p j c -> p (j c)"), bank(s, 4, 6)[:, 0:2 * C],
                                        xrow[:, b].rearrange("p j c -> p (j c)"), ALU.add).then_inc(S["y_ready"], 1)

            pipelined(dve, ((1, maxima), (2, keep_first), (3, gated), (2, keep_second), (3, keep_output),
                            (4, add)), chain, 3, BODIES)


E_N = 64
TOP = 8
HID = 512
HB = HID // P
PAIRS = STEPS // 2
GROUP = 8
GROUPS = E_N // GROUP


def repeat_rows(ap, n):
    d = [list(x) for x in ap.ap]
    return bass.AP(ap.tensor, ap.offset, [d[0], [0, n]] + d[1:])


def moe(nc, K, name, x, gate_wt, gate_b, w1, w2):
    with ExitStack() as ctx:
        keep = Phase(nc, ctx, name)
        cand_v = keep.sb("cand_v", [E_N, PAIRS, 2, TOP])
        cand_i = keep.sb("cand_i", [E_N, PAIRS, 2, TOP])
        cand_s = keep.sb("cand_s", [E_N, 2, PAIRS])
        route(nc, K, name + "r", x, gate_wt, gate_b, cand_v, cand_i, cand_s)
        experts(nc, K, name + "e", x, w1, w2, cand_v, cand_i, cand_s)


def route(nc, K, name, x, gate_wt, gate_b, cand_v, cand_i, cand_s):
    HALF = LONG // 2
    BODIES = STEPS // LONG
    with ExitStack() as ctx:
        ph = Phase(nc, ctx, name)
        xin = ph.sb("xin", [P, LONG, TILES, C])
        stats = ph.sb("stats", [P, MV, TILES, 6])
        mv = ph.sb("mv", [P, MV, TILES, 2])
        rstd = ph.sb("rstd", [P, MV, TILES])
        z = ph.sb("z", [P, 2, TILES, C])
        zt = ph.sb("zt", [P, 2, STEP])
        gw = ph.sb("gw", [P, E_N])
        gb = ph.sb("gb", [P, 1])
        logit = ph.sb("logit", [P, 2, STEP])
        junk = ph.sb("junk", [P, STEP])
        best = ph.sb("best", [P, 2, TOP])
        place = ph.sb("place", [P, 2, TOP], u32)
        neg = ph.sb("neg", [P, 2, 1])
        all_v = ph.sb("all_v", [P, PAIRS, TOP])
        all_i = ph.sb("all_i", [P, PAIRS, TOP])
        all_s = ph.sb("all_s", [P, PAIRS])
        zt_ps = ph.banks("zt_ps", 2)
        lg_ps = ph.banks("lg_ps", 2)
        loaded = ph.sems("loaded", LONG)
        weights = ph.sem("weights")
        S = {n: ph.sem(n) for n in "mv_ready rstd_ready z_ready ztp zt_ready lgp".split()}
        Q = {n: ph.sem(n) for n in "logit_ready best_ready sum_ready".split()}
        moved = ph.sem("moved")
        chain_d = ph.sem("chain_d")
        chain_p = ph.sem("chain_p")
        passed_d = ph.sem("passed_d")
        passed_p = ph.sem("passed_p")
        block = ph.block()

        def pair(t, s):
            return of_step(t, s // 2, HALF)

        @block.sync
        def _(sp):
            sp.dma_start(gw[:, :], gate_wt).then_inc(weights, DMA)
            for i in range(2):
                sp.dma_start(gb[i * E_N:(i + 1) * E_N, :], gate_b.rearrange("(c a) -> c a", a=1))\
                    .then_inc(weights, DMA)

            def load(t, b):
                sp.dma_start(xin[:, b], token_tiles(x, LONG * t + b)).then_inc(loaded[b], DMA)

            for b in range(LONG):
                load(0, b)
            with sp.Fori(0, BODIES - 1) as t:
                for b in range(LONG):
                    sp.wait_ge(S["z_ready"], of_step(t, b))
                    load(t + 1, b)
            sp.wait_ge(Q["sum_ready"], PAIRS + HALF)
            sp.wait_ge(Q["best_ready"], PAIRS + HALF)
            for i in range(2):
                part = slice(i * E_N, (i + 1) * E_N)
                sp.dma_start(cand_v[:, :, i, :], all_v[part]).then_inc(moved, DMA)
                sp.dma_start(cand_i[:, :, i, :], all_i[part]).then_inc(moved, DMA)
                sp.dma_start(cand_s[:, i, :], all_s[part, :]).then_inc(moved, DMA)
            sp.wait_ge(moved, 6 * DMA)

        @block.vector
        def _(dve):
            start_counts(dve, [S["mv_ready"], S["z_ready"]])
            start_counts(dve, [Q["best_ready"]], HALF)
            chain = Chain(dve, chain_d, 0, passed_d)

            def norm(t, s):
                dve.wait_ge(S["rstd_ready"], of_step(t, s))
                dve.wait_ge(S["ztp"], of_step(t, s - 2))
                normalize(nc, xin[:, s % LONG], mv[:, s % MV], rstd[:, s % MV], z[:, s % 2]).then_inc(S["z_ready"], 1)

            def moments(t, s):
                dve.wait_ge(loaded[s % LONG], times(t, s))
                dve.wait_ge(S["rstd_ready"], of_step(t, s - MV))
                dve.wait_ge(S["z_ready"], of_step(t, s - MV))
                column_stats(nc, chain, xin[:, s % LONG], stats[:, s % MV], mv[:, s % MV]).then_inc(S["mv_ready"], 1)

            def candidates(t, s):
                if s % 2 == 0:
                    return
                n = HALF * t + s // 2
                q = (s // 2) % 2
                wait_alone(dve, Q["logit_ready"], pair(t, s), passed_d)
                chain.link(nc.vector.max(best[:, q, :], logit[:, q, :]))
                nc.vector.max_index(place[:, q, :], best[:, q, :], logit[:, q, :])
                nc.vector.tensor_copy(all_v[:, bass.ds(n, 1), :], best[:, q:q + 1, :])
                wait_alone(dve, Q["sum_ready"], pair(t, s - 4), passed_d)
                chain.link(nc.vector.tensor_scalar(neg[:, q, :], best[:, q, 0:1], -1.0, None, ALU.mult))
                nc.vector.tensor_copy(all_i[:, bass.ds(n, 1), :], place[:, q:q + 1, :]).then_inc(Q["best_ready"], 1)

            pipelined(dve, ((0, moments), (2, norm), (6, candidates)), chain, 2)

        @block.gpsimd
        def _(pool):
            start_counts(pool, [S["rstd_ready"]])
            chain = Chain(pool, chain_p)

            def root(t, s):
                wait_alone(pool, S["mv_ready"], of_step(t, s), passed_p)
                wait_alone(pool, S["z_ready"], of_step(t, s - MV), passed_p)
                inverse_root(nc, pool, chain, mv[:, s % MV], K.minus_half[:, 0:TILES], rstd[:, s % MV],
                             1.0, 1e-5).then_inc(S["rstd_ready"], 1)

            pipelined(pool, ((0, root),), chain, 1)

        @block.tensor
        def _(pe):
            start_counts(pe, [S["ztp"], S["lgp"]])
            pe.wait_ge(weights, 3 * DMA)

            def turn(t, s):
                pe.wait_ge(S["z_ready"], of_step(t, s))
                pe.wait_ge(S["zt_ready"], of_step(t, s - 2))
                transpose_tiles(nc, zt_ps[:, s % 2], z[:, s % 2], K.ident).then_inc(S["ztp"], 1)

            def logits(t, s):
                pe.wait_ge(S["zt_ready"], of_step(t, s))
                pe.wait_ge(Q["logit_ready"], pair(t, s - 4))
                half = (s % 2) * E_N
                nc.tensor.matmul(lg_ps[half:half + E_N, (s // 2) % 2, :], gw[:, :], zt[:, s % 2, :],
                                 start=True, stop=True).then_inc(S["lgp"], 1)

            pipelined(pe, ((3, turn), (4, logits)))

        @block.scalar
        def _(act):
            start_counts(act, [S["zt_ready"]])
            start_counts(act, [Q["logit_ready"], Q["sum_ready"]], HALF)
            act.wait_ge(weights, 3 * DMA)

            def keep_zt(t, s):
                act.wait_ge(S["ztp"], of_step(t, s))
                act.wait_ge(S["lgp"], of_step(t, s - 2))
                nc.scalar.activation(zt[:, s % 2, :], zt_ps[:, s % 2, :], ACT.Copy).then_inc(S["zt_ready"], 1)

            def keep_logits(t, s):
                if s % 2 == 0:
                    return
                q = (s // 2) % 2
                act.wait_ge(S["lgp"], of_step(t, s))
                act.wait_ge(Q["best_ready"], pair(t, s - 4))
                act.wait_ge(Q["sum_ready"], pair(t, s - 4))
                nc.scalar.activation(logit[:, q, :], lg_ps[:, q, :], ACT.Identity, bias=gb[:, 0:1])\
                    .then_inc(Q["logit_ready"], 1)

            def exponentials(t, s):
                if s % 2 == 0:
                    return
                q = (s // 2) % 2
                act.wait_ge(Q["best_ready"], pair(t, s))
                act.wait_ge(Q["sum_ready"], pair(t, s - 2))
                nc.scalar.activation(junk[:, :], logit[:, q, :], ACT.Exp, bias=neg[:, q, :],
                                     accum_out=all_s[:, bass.ds(HALF * t + s // 2, 1)]).then_inc(Q["sum_ready"], 1)

            pipelined(act, ((3, keep_zt), (5, keep_logits), (7, exponentials)))


def experts(nc, K, name, x, w1, w2, cand_v, cand_i, cand_s):
    NC = PAIRS * 2 * TOP
    FLAT = TOP * E_N
    with ExitStack() as ctx:
        ph = Phase(nc, ctx, name)
        w1_sb = ph.sb("w1", [P, 2, GROUP, HID])
        w2_sb = ph.sb("w2", [P, 2, GROUP, HB, C])
        b1_sb = ph.sb("b1", [E_N, HID])
        b1t = ph.sb("b1t", [P, HB, E_N])
        b2_sb = ph.sb("b2", [E_N, C])
        top = ph.sb("top", [E_N, TOP])
        place = ph.sb("place", [E_N, TOP], u32)
        placef = ph.sb("placef", [E_N, TOP])
        order_i = ph.sb("order_i", [E_N, NC], i32)
        order = ph.sb("order", [E_N, NC])
        base_i = ph.sb("base_i", [E_N, PAIRS * 2, TOP], i32)
        base = ph.sb("base", [E_N, PAIRS * 2, TOP])
        own_i = ph.sb("own_i", [E_N, TOP], i32)
        own = ph.sb("own", [E_N, TOP])
        junk = ph.sb("junk", [E_N, NC])
        idx = ph.sb("idx", [E_N, TOP])
        idx_u = ph.sb("idx_u", [E_N, TOP], u32)
        to = ph.sb("to", [E_N, TOP])
        to_u = ph.sb("to_u", [E_N, TOP], u32)
        neg = ph.sb("neg", [E_N, 1])
        scale = ph.sb("scale", [E_N, PAIRS * 2])
        total = ph.sb("total", [E_N, 1])
        prob = ph.sb("prob", [E_N, TOP])
        xg = ph.sb("xg", [E_N, TOP, C])
        zg = ph.sb("zg", [E_N, TOP, C])
        stats = ph.sb("stats", [E_N, TOP, 6])
        mv = ph.sb("mv", [E_N, TOP, 2])
        rstd = ph.sb("rstd", [E_N, TOP])
        pooled = ph.sb("pooled", [E_N, C])
        pooledt = ph.sb("pooledt", [P, E_N])
        pre = ph.sb("pre", [P, 2, GROUP, HB])
        hid = ph.sb("hid", [P, 2, GROUP, HB])
        outt = ph.sb("outt", [P, E_N])
        out = ph.sb("out", [E_N, C])
        ones = ph.sb("ones", [E_N, E_N])
        diag = ph.sb("diag", [E_N, TOP, E_N])
        row = ph.sb("row", [E_N, FLAT])
        mask = ph.sb("mask", [E_N, FLAT])
        count = ph.sb("count", [E_N, TOP])
        share = ph.sb("share", [E_N, FLAT])
        new = ph.sb("new", [E_N, TOP, C])
        misc_ps = ph.banks("misc_ps")
        hid_ps = ph.banks("hid_ps", 2)
        outt_ps = ph.banks("outt_ps")
        row_ps = ph.banks("row_ps")
        new_ps = ph.banks("new_ps", 2)
        bias_in = ph.sem("bias_in")
        w_in = ph.sems("w_in", 2)
        consts = ph.sem("consts")
        dve_done = ph.sem("dve_done")
        act_done = ph.sem("act_done")
        pool_done = ph.sem("pool_done")
        pe_done = ph.sem("pe_done")
        gathered = K.by_pool.pop()
        scattered = K.by_pool.pop()
        hid_pre = ph.sem("hid_pre")
        hid_add = ph.sem("hid_add")
        hid_ready = ph.sem("hid_ready")
        group_done = ph.sem("group_done")
        block = ph.block()
        EXP_IN, IDX_READY, STATS_READY, POOLED, ROW_IN, SHARE, OUTT, OUT, NEW_READY = 6, 15, 21, 30, 32, 67, 68, 69, 71

        @block.sync
        def _(sp):
            sp.dma_start(b1_sb[:, :], w1[:, P, :]).then_inc(bias_in, DMA)
            sp.dma_start(b2_sb[:, :], w2[:, HID, :]).then_inc(bias_in, DMA)
            for g in range(GROUPS):
                if g >= 2:
                    sp.wait_ge(group_done, g - 1)
                e = slice(g * GROUP, (g + 1) * GROUP)
                sp.dma_start(w1_sb[:, g % 2], w1[e, 0:P, :].rearrange("e d h -> d e h")).then_inc(w_in[g % 2], DMA)
                for k in range(HB):
                    sp.dma_start(w2_sb[:, g % 2, :, k, :],
                                 w2[e, k * P:(k + 1) * P, :].rearrange("e h o -> h e o")).then_inc(w_in[g % 2], DMA)

        @block.gpsimd
        def _(pool):
            nc.gpsimd.iota(order_i[:, :], pattern=[[1, NC]], base=0, channel_multiplier=0).then_inc(consts, 1)
            nc.gpsimd.iota(base_i[:, :, :], pattern=[[STEP, PAIRS * 2], [0, TOP]], base=0,
                           channel_multiplier=0).then_inc(consts, 1)
            nc.gpsimd.iota(own_i[:, :], pattern=[[E_N, TOP]], base=0, channel_multiplier=1).then_inc(consts, 1)
            nc.gpsimd.memset(ones[:, :], 1.0).then_inc(consts, 1)
            pool.wait_ge(dve_done, IDX_READY)
            for k in range(TOP):
                pool.indirect_dma_start(out=xg[:, k, :], out_offset=None, in_=x,
                                        in_offset=bass.IndirectOffsetOnAxis(ap=idx_u[:, k:k + 1], axis=0))\
                    .then_inc(gathered, DMA)
            pool.wait_ge(dve_done, STATS_READY)
            nc.gpsimd.tensor_scalar(rstd[:, :], mv[:, :, 1], 1.0, 1e-5, ALU.mult, ALU.add).then_inc(pool_done, 1)
            pool.wait_ge(pool_done, 1)
            nc.gpsimd.tensor_tensor(rstd[:, :], rstd[:, :], K.minus_half[0:E_N, 0:TOP], ALU.pow).then_inc(pool_done, 1)
            pool.wait_ge(dve_done, NEW_READY)
            for k in range(TOP):
                pool.indirect_dma_start(out=x, out_offset=bass.IndirectOffsetOnAxis(ap=to_u[:, k:k + 1], axis=0),
                                        in_=new[:, k, :], in_offset=None, bounds_check=N - 1,
                                        oob_is_err=False).then_inc(scattered, DMA)
            pool.wait_ge(scattered, TOP * DMA)

        flat_v = cand_v[:, :, :, :].rearrange("p q a k -> p (q a k)")
        flat_i = cand_i[:, :, :, :].rearrange("p q a k -> p (q a k)")

        @block.vector
        def _(dve):
            chain = Chain(dve, dve_done)
            link = chain.link
            dve.wait_ge(consts, 4)
            nc.vector.tensor_copy(order[:, :], order_i[:, :])
            nc.vector.tensor_copy(own[:, :], own_i[:, :])
            link(nc.vector.tensor_copy(base[:, :, :], base_i[:, :, :]))
            link(nc.vector.tensor_tensor(flat_i, flat_i, base[:, :, :].rearrange("p a k -> p (a k)"), ALU.add))
            link(nc.vector.max(top[:, :], flat_v))
            link(nc.vector.max_index(place[:, :], top[:, :], flat_v))
            link(nc.vector.tensor_copy(placef[:, :], place[:, :]))
            link(nc.vector.tensor_scalar(neg[:, :], top[:, 0:1], -1.0, None, ALU.mult))
            assert chain.n == EXP_IN
            for k in range(TOP):
                link(nc.vector.scalar_tensor_tensor(junk[:, :], order[:, :], placef[:, k:k + 1], flat_i,
                                                    ALU.is_equal, ALU.mult, accum_out=idx[:, k:k + 1]))
            link(nc.vector.tensor_copy(idx_u[:, :], idx[:, :]))
            assert chain.n == IDX_READY
            dve.wait_ge(act_done, 2)
            sums = cand_s[:, :, :].rearrange("p a q -> p (a q)")
            link(nc.vector.tensor_tensor(scale[:, :], scale[:, :], sums, ALU.mult))
            link(nc.vector.reduce_sum(total[:, :], scale[:, :], AX.X))
            link(nc.vector.reciprocal(total[:, :], total[:, :]))
            link(nc.vector.tensor_scalar(prob[:, :], prob[:, :], total[:, 0:1], None, ALU.mult))
            dve.wait_ge(gathered, TOP * DMA)
            for k in range(TOP):
                last = nc.vector.bn_stats(stats[:, k, :], xg[:, k, :])
            link(last)
            for k in range(TOP):
                last = nc.vector.bn_aggr(mv[:, k, :], stats[:, k, :])
            link(last)
            assert chain.n == STATS_READY
            dve.wait_ge(pool_done, 2)
            for k in range(TOP):
                last = nc.vector.tensor_scalar(zg[:, k, :], xg[:, k, :], mv[:, k, 0:1], rstd[:, k:k + 1],
                                               ALU.subtract, ALU.mult)
            link(last)
            link(nc.vector.tensor_scalar(pooled[:, :], zg[:, 0, :], prob[:, 0:1], None, ALU.mult))
            for k in range(1, TOP):
                link(nc.vector.scalar_tensor_tensor(pooled[:, :], zg[:, k, :], prob[:, k:k + 1], pooled[:, :],
                                                    ALU.mult, ALU.add))
            link(nc.vector.tensor_tensor(diag[:, :, :], repeat_rows(K.ident[0:E_N, 0:E_N], TOP),
                                         spread(idx[:, :], E_N), ALU.mult))
            assert chain.n == POOLED + 1
            dve.wait_ge(pe_done, 1)
            link(nc.vector.tensor_copy(pooledt[:, :], misc_ps[:, 0, 0:E_N]))
            assert chain.n == ROW_IN
            dve.wait_ge(pe_done, 2)
            nc.vector.tensor_copy(row[:, :], row_ps[0:E_N, 0, :])
            dve.wait_ge(pe_done, 3)
            link(nc.vector.tensor_copy(b1t[:, :, :].rearrange("p k e -> p (k e)"), misc_ps[:, 0, E_N:E_N + HB * E_N]))
            link(nc.vector.tensor_scalar(share[:, :], row[:, :], idx[:, 0:1], prob[:, 0:1], ALU.is_equal, ALU.mult))
            for k in range(1, TOP):
                link(nc.vector.tensor_scalar(mask[:, :], row[:, :], idx[:, k:k + 1], prob[:, k:k + 1],
                                             ALU.is_equal, ALU.mult))
                link(nc.vector.tensor_tensor(share[:, :], share[:, :], mask[:, :], ALU.add))
            for k in range(TOP):
                link(nc.vector.tensor_scalar(mask[:, :], order[:, 0:FLAT], own[:, k:k + 1], None, ALU.is_lt))
                link(nc.vector.scalar_tensor_tensor(junk[:, 0:FLAT], row[:, :], idx[:, k:k + 1], mask[:, :],
                                                    ALU.is_equal, ALU.mult, accum_out=count[:, k:k + 1]))
            link(nc.vector.tensor_scalar(count[:, :], count[:, :], float(2 * N), None, ALU.mult))
            link(nc.vector.tensor_tensor(to[:, :], count[:, :], idx[:, :], ALU.add))
            link(nc.vector.tensor_copy(to_u[:, :], to[:, :]))
            assert chain.n == SHARE, chain.n
            for g in range(GROUPS):
                dve.wait_ge(hid_pre, g + 1)
                e = slice(g * GROUP, (g + 1) * GROUP)
                if g >= 2:
                    dve.wait_ge(hid_ready, g - 1)
                nc.vector.tensor_tensor(pre[:, g % 2], hid_ps[:, g % 2, 0:GROUP * HB].rearrange("p (e k) -> p e k", k=HB),
                                        b1t[:, :, e].rearrange("p k e -> p e k"), ALU.add).then_inc(hid_add, 1)
            dve.wait_ge(group_done, GROUPS)
            link(nc.vector.tensor_copy(outt[:, :], outt_ps[:, 0, 0:E_N]))
            assert chain.n == OUTT
            dve.wait_ge(pe_done, 4)
            link(nc.vector.tensor_tensor(out[:, :], misc_ps[0:E_N, 0, 0:C], b2_sb[:, :], ALU.add))
            assert chain.n == OUT
            dve.wait_ge(pe_done, 5)
            for i in range(2):
                k = slice(i * TOP // 2, (i + 1) * TOP // 2)
                link(nc.vector.tensor_tensor(new[:, k, :].rearrange("p k c -> p (k c)"), new_ps[0:E_N, i, :],
                                             xg[:, k, :].rearrange("p k c -> p (k c)"), ALU.add))
            assert chain.n == NEW_READY

        @block.scalar
        def _(act):
            act.wait_ge(dve_done, EXP_IN)
            nc.scalar.activation(scale[:, :].rearrange("p (a q) -> p a q", a=2),
                                 cand_v[:, :, :, 0].rearrange("p q a -> p a q"), ACT.Exp,
                                 bias=neg[:, 0:1]).then_inc(act_done, 1)
            nc.scalar.activation(prob[:, :], top[:, :], ACT.Exp, bias=neg[:, 0:1]).then_inc(act_done, 1)
            for g in range(GROUPS):
                act.wait_ge(hid_add, g + 1)
                if g >= 2:
                    act.wait_ge(group_done, g - 1)
                nc.scalar.activation(hid[:, g % 2], pre[:, g % 2], ACT.Gelu).then_inc(hid_ready, 1)

        @block.tensor
        def _(pe):
            pe.wait_ge(dve_done, POOLED)
            nc.tensor.transpose(misc_ps[:, 0, 0:E_N], pooled[:, :], K.ident[0:E_N, 0:E_N]).then_inc(pe_done, 1)
            pe.wait_ge(consts, 4)
            pe.wait_ge(dve_done, POOLED + 1)
            nc.tensor.matmul(row_ps[0:E_N, 0, :], ones[:, :], diag[:, :, :].rearrange("p k e -> p (k e)"),
                             start=True, stop=True).then_inc(pe_done, 1)
            pe.wait_ge(dve_done, ROW_IN)
            pe.wait_ge(bias_in, 2 * DMA)
            for k in range(HB):
                last = nc.tensor.transpose(misc_ps[:, 0, (k + 1) * E_N:(k + 2) * E_N], b1_sb[:, k * P:(k + 1) * P],
                                           K.ident[0:E_N, 0:E_N])
            last.then_inc(pe_done, 1)
            for g in range(GROUPS + 1):
                if g < GROUPS:
                    pe.wait_ge(w_in[g % 2], (1 + HB) * DMA * (g // 2 + 1))
                    if g >= 2:
                        pe.wait_ge(hid_add, g - 1)
                    for e in range(GROUP):
                        for k in range(HB):
                            last = nc.tensor.matmul(hid_ps[:, g % 2, e * HB + k:e * HB + k + 1],
                                                    w1_sb[:, g % 2, e, k * P:(k + 1) * P],
                                                    pooledt[:, g * GROUP + e:g * GROUP + e + 1],
                                                    start=True, stop=True)
                    last.then_inc(hid_pre, 1)
                if g:
                    pe.wait_ge(hid_ready, g)
                    for e in range(GROUP):
                        n = (g - 1) * GROUP + e
                        for k in range(HB):
                            last = nc.tensor.matmul(outt_ps[:, 0, n:n + 1], w2_sb[:, (g - 1) % 2, e, k, :],
                                                    hid[:, (g - 1) % 2, e, k:k + 1],
                                                    start=(k == 0), stop=(k == HB - 1))
                    last.then_inc(group_done, 1)
            pe.wait_ge(dve_done, OUTT)
            nc.tensor.transpose(misc_ps[0:E_N, 0, 0:C], outt[:, :], K.ident[:, :]).then_inc(pe_done, 1)
            pe.wait_ge(dve_done, OUT)
            for k in range(TOP):
                last = nc.tensor.matmul(new_ps[0:E_N, k // 4, (k % 4) * C:(k % 4 + 1) * C],
                                        share[:, k * E_N:(k + 1) * E_N], out[:, :], start=True, stop=True)
            last.then_inc(pe_done, 1)


def column(v):
    return v.rearrange("(c a) -> c a", a=1)


def on_all(v, n=P):
    return bass.AP(v.tensor, v.offset, [[0, n]] + [list(d) for d in v.ap])


SEQ_BLOCK = 64
SEQ_BLOCKS = W // SEQ_BLOCK


def of_rows(a, u):
    return a[:, :, bass.ds(2 * u, 2), :]


def row_order(a):
    return a.rearrange("c (k r j) -> c r k j", r=2, k=SEQ_BLOCKS)


def ema_conv(nc, K, x, w_exp_t, b_exp, w_con_t, b_con, w_t, x_out, wx_out, wx_mv):
    with ExitStack() as ctx:
        ph = Phase(nc, ctx, "ema")
        xin = ph.sb("xin", [P, LONG, TILES, C])
        xo = ph.sb("xo", [P, LONG, TILES, C])
        stats = ph.sb("stats", [P, 2, TILES, 6])
        mv = ph.sb("mv", [P, 2, TILES, 2])
        rstd = ph.sb("rstd", [P, 2, TILES])
        stats2 = ph.sb("stats2", [P, 2, TILES, 6])
        mv2 = ph.sb("mv2", [P, 2, TILES, 2])
        rstd2 = ph.sb("rstd2", [P, 2, TILES])
        z = ph.sb("z", [P, 2, TILES, C])
        zt = ph.sb("zt", [P, 2, STEP])
        z2 = ph.sb("z2", [P, 2, TILES, C])
        z2t = ph.sb("z2t", [P, 2, STEP])
        gin = ph.sb("gin", [P, 2, STEP])
        state = ph.sb("state", [P, 2, STEP])
        gate = ph.sb("gate", [P, 2, STEP])
        prod = ph.sb("prod", [P, 2, STEP])
        wx = ph.sb("wx", [P, 2, STEP])
        wx_stats = ph.sb("wx_stats", [P, STEPS, 6])
        w_exp = ph.sb("w_exp", [P, 2 * C])
        w_con = ph.sb("w_con", [P, C])
        w_sb = ph.sb("w_sb", [P, C])
        b_pg = ph.sb("b_pg", [P, 2])
        b_con_sb = ph.sb("b_con", [P, C])
        zt_ps = ph.banks("zt_ps")
        p_ps = ph.banks("p_ps", 2)
        g_ps = ph.banks("g_ps")
        out_ps = ph.banks("out_ps")
        z2t_ps = ph.banks("z2t_ps")
        wx_ps = ph.banks("wx_ps")
        loaded = ph.sems("loaded", LONG)
        stored = ph.sems("stored", LONG)
        wx_stored = ph.sems("wx_stored", 2)
        weights = ph.sem("weights")
        begun = ph.sem("begun")
        d_names = "mv_ready mv2_ready z_ready state_ready prod_ready xo_ready z2_ready wx_read"
        a_names = "zt_ready gin_ready gate_ready z2t_ready wx_ready"
        e_names = "ztp gp outp z2tp wxp"
        p_names = "rstd_ready xb_ready rstd2_ready"
        S = {n: ph.sem(n) for n in f"{d_names} {a_names} {e_names} {p_names}".split()}
        chain_d = ph.sem("chain_d")
        chain_p = ph.sem("chain_p")
        passed_d = ph.sem("passed_d")
        passed_p = ph.sem("passed_p")
        block = ph.block()
        NW = 6

        @block.sync
        def _(sp):
            for dst, src in ((w_exp[:, :], w_exp_t), (w_con[:, :], w_con_t), (w_sb[:, :], w_t),
                             (b_pg[:, 0:1], column(b_exp[0:C])), (b_pg[:, 1:2], column(b_exp[C:2 * C])),
                             (b_con_sb[:, :], on_all(b_con))):
                sp.dma_start(dst, src).then_inc(weights, DMA)

            def load(t, b):
                sp.dma_start(xin[:, b], token_tiles(x, LONG * t + b)).then_inc(loaded[b], DMA)

            def store(t, s):
                sp.wait_ge(S["z2_ready"], of_step(t, s))
                sp.dma_start(token_tiles(x_out, LONG * t + s), xo[:, s % LONG]).then_inc(stored[s % LONG], DMA)

            def load_next(t, s):
                sp.wait_ge(S["xo_ready"], of_step(t, s))
                load(t + 1, s)

            for b in range(LONG):
                sp.nop().then_inc(stored[b], DMA)
                load(0, b)
            bodies = STEPS // LONG
            for b in range(LONG):
                load_next(0, b)
                if b:
                    store(0, b - 1)
            with sp.Fori(1, bodies - 1) as t:
                for b in range(LONG):
                    load_next(t, b)
                    store(t, b - 1)
            for b in range(LONG + 1):
                store(bodies - 1, b - 1)
            for b in range(LONG):
                sp.wait_ge(stored[b], DMA * (bodies + 1))

        @block.vector
        def _(dve):
            start_counts(dve, [S[n] for n in d_names.split()])
            dve.wait_ge(weights, NW * DMA)
            nc.vector.tensor_scalar(b_pg[:, 1:2], b_pg[:, 1:2], 0.1, None, ALU.mult).then_inc(begun, 1)
            nc.vector.memset(state[:, :, :], 0.0).then_inc(begun, 1)
            dve.wait_ge(begun, 2)
            chain = Chain(dve, chain_d, 0, passed_d)

            def gated(t, s):
                dve.wait_ge(S["gate_ready"], of_step(t, s))
                dve.wait_ge(S["outp"], of_step(t, s - 2))
                nc.vector.scalar_tensor_tensor(prod[:, s % 2, :], p_ps[:, s % 2, :], b_pg[:, 0:1],
                                               gate[:, s % 2, :], ALU.add, ALU.mult).then_inc(S["prod_ready"], 1)

            def average(t, s):
                dve.wait_ge(S["gin_ready"], of_step(t, s))
                dve.wait_ge(S["gate_ready"], of_step(t, s - 2))
                dve.wait_ge(S["state_ready"], of_step(t, s - 1))
                chain.link(nc.vector.scalar_tensor_tensor(
                    state[:, s % 2, 0:W], state[:, (s + 1) % 2, W:2 * W], 0.9, gin[:, s % 2, 0:W],
                    ALU.mult, ALU.add))
                nc.vector.scalar_tensor_tensor(
                    state[:, s % 2, W:2 * W], state[:, s % 2, 0:W], 0.9, gin[:, s % 2, W:2 * W],
                    ALU.mult, ALU.add).then_inc(S["state_ready"], 1)

            def add(t, s):
                b = s % LONG
                dve.wait_ge(S["outp"], of_step(t, s))
                dve.wait_ge(S["xb_ready"], of_step(t, s))
                dve.wait_ge(stored[b], times(t, s))
                dve.wait_ge(S["rstd2_ready"], of_step(t, s - 2))
                nc.vector.tensor_tensor(xo[:, b].rearrange("p j c -> p (j c)"), out_ps[:, 0, :],
                                        xin[:, b].rearrange("p j c -> p (j c)"), ALU.add).then_inc(S["xo_ready"], 1)
                wait_alone(dve, S["xo_ready"], of_step(t, s), passed_d)
                column_stats(nc, chain, xo[:, b], stats2[:, s % 2], mv2[:, s % 2]).then_inc(S["mv2_ready"], 1)

            def moments(t, s):
                dve.wait_ge(loaded[s % LONG], times(t, s))
                dve.wait_ge(S["rstd_ready"], of_step(t, s - 2))
                dve.wait_ge(S["z_ready"], of_step(t, s - 2))
                column_stats(nc, chain, xin[:, s % LONG], stats[:, s % 2], mv[:, s % 2]).then_inc(S["mv_ready"], 1)

            def norm2(t, s):
                dve.wait_ge(S["rstd2_ready"], of_step(t, s))
                dve.wait_ge(S["z2tp"], of_step(t, s - 2))
                normalize(nc, xo[:, s % LONG], mv2[:, s % 2], rstd2[:, s % 2], z2[:, s % 2])\
                    .then_inc(S["z2_ready"], 1)

            def norm(t, s):
                dve.wait_ge(S["rstd_ready"], of_step(t, s))
                dve.wait_ge(S["ztp"], of_step(t, s - 2))
                normalize(nc, xin[:, s % LONG], mv[:, s % 2], rstd[:, s % 2], z[:, s % 2]).then_inc(S["z_ready"], 1)

            def moments_of_wx(t, s):
                dve.wait_ge(S["wx_ready"], of_step(t, s))
                nc.vector.bn_stats(wx_stats[:, LONG * t + s, :], wx[:, s % 2, :]).then_inc(S["wx_read"], 1)

            pipelined(dve, ((1, norm), (4, gated), (3, average), (5, add), (0, moments), (6, norm2),
                            (8, moments_of_wx)), chain, 3)
            dve.wait_ge(S["wx_read"], STEPS + LONG)
            nc.vector.bn_aggr(wx_mv[:, :], wx_stats[:, :, :].rearrange("p s k -> p (s k)")).then_inc(begun, 1)
            dve.wait_ge(begun, 3)

        @block.gpsimd
        def _(pool):
            start_counts(pool, [S[n] for n in p_names.split()])
            pool.wait_ge(weights, NW * DMA)
            chain = Chain(pool, chain_p)

            def root2(t, s):
                wait_alone(pool, S["mv2_ready"], of_step(t, s), passed_p)
                wait_alone(pool, S["z2_ready"], of_step(t, s - 2), passed_p)
                inverse_root(nc, pool, chain, mv2[:, s % 2], K.minus_half[:, 0:TILES], rstd2[:, s % 2],
                             1.0, 1e-5).then_inc(S["rstd2_ready"], 1)

            def root(t, s):
                wait_alone(pool, S["mv_ready"], of_step(t, s), passed_p)
                wait_alone(pool, S["z_ready"], of_step(t, s - 2), passed_p)
                inverse_root(nc, pool, chain, mv[:, s % 2], K.minus_half[:, 0:TILES], rstd[:, s % 2],
                             1.0, 1e-6).then_inc(S["rstd_ready"], 1)

            def add_bias(t, s):
                b = s % LONG
                pool.wait_ge(S["z_ready"], of_step(t, s))
                nc.gpsimd.tensor_tensor(xin[:, b], xin[:, b], repeat_rows(b_con_sb[:, :], TILES), ALU.add)\
                    .then_inc(S["xb_ready"], 1)

            pipelined(pool, ((5, root2), (0, root), (2, add_bias)), chain, 2)

        @block.tensor
        def _(pe):
            start_counts(pe, [S[n] for n in e_names.split()])
            pe.wait_ge(weights, NW * DMA)

            def contract(t, s):
                pe.wait_ge(S["prod_ready"], of_step(t, s))
                pe.wait_ge(S["xo_ready"], of_step(t, s - 1))
                for j in range(TILES):
                    last = nc.tensor.matmul(out_ps[:, 0, j * P:(j + 1) * P], prod[:, s % 2, j * P:(j + 1) * P],
                                            w_con[:, :], start=True, stop=True)
                last.then_inc(S["outp"], 1)

            def turn_z2(t, s):
                pe.wait_ge(S["z2_ready"], of_step(t, s))
                pe.wait_ge(S["z2t_ready"], of_step(t, s - 1))
                transpose_tiles(nc, z2t_ps[:, 0], z2[:, s % 2], K.ident).then_inc(S["z2tp"], 1)

            def project(t, s):
                pe.wait_ge(S["z2t_ready"], of_step(t, s))
                pe.wait_ge(S["wx_ready"], of_step(t, s - 1))
                nc.tensor.matmul(wx_ps[:, 0, :], w_sb[:, :], z2t[:, s % 2, :], start=True, stop=True)\
                    .then_inc(S["wxp"], 1)

            def expand(t, s):
                pe.wait_ge(S["zt_ready"], of_step(t, s))
                pe.wait_ge(S["gin_ready"], of_step(t, s - 1))
                pe.wait_ge(S["prod_ready"], of_step(t, s - 2))
                nc.tensor.matmul(g_ps[:, 0, :], w_exp[:, C:2 * C], zt[:, s % 2, :], start=True, stop=True)
                nc.tensor.matmul(p_ps[:, s % 2, :], w_exp[:, 0:C], zt[:, s % 2, :], start=True, stop=True)\
                    .then_inc(S["gp"], 1)

            def turn_z(t, s):
                pe.wait_ge(S["z_ready"], of_step(t, s))
                pe.wait_ge(S["zt_ready"], of_step(t, s - 1))
                transpose_tiles(nc, zt_ps[:, 0], z[:, s % 2], K.ident).then_inc(S["ztp"], 1)

            pipelined(pe, ((5, contract), (7, turn_z2), (2, expand), (1, turn_z), (7, project)))

        @block.scalar
        def _(act):
            start_counts(act, [S[n] for n in a_names.split()])
            for i in range(2):
                act.nop().then_inc(wx_stored[i], DMA)
            act.wait_ge(begun, 1)

            def keep_z2t(t, s):
                act.wait_ge(S["z2tp"], of_step(t, s))
                act.wait_ge(S["wxp"], of_step(t, s - 2))
                nc.scalar.activation(z2t[:, s % 2, :], z2t_ps[:, 0, :], ACT.Copy).then_inc(S["z2t_ready"], 1)

            def gates(t, s):
                act.wait_ge(S["state_ready"], of_step(t, s))
                act.wait_ge(S["prod_ready"], of_step(t, s - 2))
                nc.scalar.activation(gate[:, s % 2, :], state[:, s % 2, :], ACT.Sigmoid)\
                    .then_inc(S["gate_ready"], 1)

            def keep_wx(t, s):
                act.wait_ge(S["wxp"], of_step(t, s))
                act.wait_ge(S["wx_read"], of_step(t, s - 2))
                act.wait_ge(wx_stored[s % 2], of_pair(t, s))
                nc.scalar.activation(row_order(wx[:, s % 2, :]),
                                     wx_ps[:, 0, :].rearrange("c (r k j) -> c r k j", r=2, k=SEQ_BLOCKS),
                                     ACT.Copy).then_inc(S["wx_ready"], 1)
                act.wait_ge(S["wx_ready"], of_step(t, s))
                act.dma_start(of_rows(wx_out, LONG * t + s),
                              wx[:, s % 2, :].rearrange("c (k r j) -> c k r j", r=2, k=SEQ_BLOCKS))\
                    .then_inc(wx_stored[s % 2], DMA)

            def average_input(t, s):
                act.wait_ge(S["gp"], of_step(t, s))
                act.wait_ge(S["state_ready"], of_step(t, s - 2))
                nc.scalar.activation(gin[:, s % 2, :], g_ps[:, 0, :], ACT.Identity,
                                     bias=b_pg[:, 1:2], scale=0.1).then_inc(S["gin_ready"], 1)

            def keep_zt(t, s):
                act.wait_ge(S["ztp"], of_step(t, s))
                act.wait_ge(S["gp"], of_step(t, s - 2))
                nc.scalar.activation(zt[:, s % 2, :], zt_ps[:, 0, :], ACT.Copy).then_inc(S["zt_ready"], 1)

            pipelined(act, ((8, keep_wx), (7, keep_z2t), (3, gates), (2, average_input), (1, keep_zt)))
            for i in range(2):
                act.wait_ge(wx_stored[i], DMA * (STEPS // 2 + 1))


WARM = 32


def recur(nc, K, name, wx, seq, state, first, count, y_out, save):
    size = min(count, SEQ_BLOCK)
    blocks = count // size
    with ExitStack() as ctx:
        ph = Phase(nc, ctx, name)
        blk, pre_ps = seq.blk, seq.pre_ps
        loaded = ph.sems("loaded", 2)
        stored = ph.sems("stored", 2)
        pre_ready = ph.sem("pre_ready")
        y_ready = ph.sem("y_ready")
        copied = ph.sem("copied")
        saved = ph.sem("saved")
        block = ph.block()

        def columns(a, k):
            k0, at = divmod(first + k * size, SEQ_BLOCK)
            return a[:, k0, :, at:at + size]

        @block.sync
        def _(sp):
            def load(k):
                sp.dma_start(blk[:, k % 2, :, 0:size], columns(wx, k)).then_inc(loaded[k % 2], DMA)

            load(0)
            for k in range(blocks):
                if k + 1 < blocks:
                    if k >= 1 and y_out is not None:
                        sp.wait_ge(stored[(k + 1) % 2], DMA * ((k + 1) // 2))
                        if save:
                            sp.wait_ge(saved, 1)
                    load(k + 1)
                if y_out is not None:
                    sp.wait_ge(copied, (k + 1) * size + 2)
                    sp.dma_start(columns(y_out, k), blk[:, k % 2])\
                        .then_inc(stored[k % 2], DMA)
            if y_out is not None:
                for k in range(min(2, blocks)):
                    sp.wait_ge(stored[k], DMA * ((blocks + 1 - k) // 2))

        @block.tensor
        def _(pe):
            for k in range(blocks):
                pe.wait_ge(loaded[k % 2], DMA * (k // 2 + 1))
                with pe.Fori(0, size // 2) as t:
                    for b in range(2):
                        n = 2 * t + (k * size + b)
                        pe.wait_ge(y_ready, n + 1)
                        nc.tensor.matmul(pre_ps[:, b, 0:H], seq.diag[:, :],
                                         blk[:, k % 2, :, bass.ds(2 * t + b, 1)].rearrange("c h a -> c (h a)"),
                                         start=True, stop=False)
                        pe.wait_ge(y_ready, n + 2)
                        nc.tensor.matmul(pre_ps[:, b, 0:H], seq.vt[:, :], state[:, 1 - b, :],
                                         start=False, stop=True).then_inc(pre_ready, 1)

        @block.scalar
        def _(act):
            nc.scalar.activation(state[:, 1, :], seq.start[:, :], ACT.Copy).then_inc(y_ready, 2)
            with act.Fori(0, count // 2) as t:
                for b in range(2):
                    act.wait_ge(pre_ready, 2 * t + b + 1)
                    act.wait_ge(copied, 2 * t + b + 1)
                    nc.scalar.activation(state[:, b, :], pre_ps[:, b, 0:H], ACT.Sigmoid, bias=seq.shift[:, 0:1])\
                        .then_inc(y_ready, 1)

        @block.vector
        def _(dve):
            nc.vector.engine_nop().then_inc(copied, 2)
            for k in range(blocks):
                with dve.Fori(0, size // 2) as t:
                    for b in range(2):
                        dve.wait_ge(y_ready, 2 * t + (k * size + b + 3))
                        nc.vector.tensor_copy(blk[:, k % 2, :, bass.ds(2 * t + b, 1)].rearrange("c h a -> c (h a)"),
                                              state[:, b, :]).then_inc(copied, 1)
                if k == 0 and save:
                    dve.wait_ge(copied, size + 2)
                    nc.vector.tensor_copy(seq.early[:, :], blk[:, 0, :, size - 1]).then_inc(saved, 1)



def settle(nc, K, name, seq, state, compare):
    with ExitStack() as ctx:
        ph = Phase(nc, ctx, name)
        d = ph.sem("d")
        e = ph.sem("e")
        block = ph.block()

        @block.vector
        def _(dve):
            chain = Chain(dve, d)
            if compare:
                nc.vector.memset(seq.most[:, 1:2], 1.0)
                chain.link(nc.vector.tensor_tensor(seq.changed[:, :], state[:, 1, :], seq.early[:, :], ALU.not_equal))
                chain.link(nc.vector.reduce_max(seq.most[:, 0:1], seq.changed[:, :], AX.X))
                dve.wait_ge(e, 1)
                chain.link(nc.vector.tensor_copy(seq.again[0:1, 0:1], seq.sum_ps[0:1, 0, 0:1]))
            else:
                chain.link(nc.vector.tensor_copy(seq.start[:, 1:H], state[:, 1, 0:H - 1]))

        if compare:
            @block.tensor
            def _(pe):
                pe.wait_ge(d, 2)
                nc.tensor.matmul(seq.sum_ps[0:1, 0, 0:1], seq.most[:, 0:1], seq.most[:, 1:2],
                                 start=True, stop=True).then_inc(e, 1)



def recurrence(nc, K, wx, wx_mv, gamma, beta, vt, y_out):
    with ExitStack() as ctx:
        keep = Phase(nc, ctx, "seq")
        seq = Namespace()
        seq.diag = keep.sb("diag", [P, P])
        seq.vt = keep.sb("vt", [P, P])
        seq.shift = keep.sb("shift", [P, 1])
        seq.start = keep.sb("start", [P, H])
        seq.again = keep.sb("again", [1, 1], i32)
        state = keep.sb("state", [P, 2, H])
        seq.blk = keep.sb("blk", [P, 2, H, SEQ_BLOCK])
        seq.pre_ps = keep.banks("pre_ps", 2)
        seq.changed = keep.sb("changed", [P, H])
        seq.early = keep.sb("early", [P, H])
        seq.most = keep.sb("most", [P, 2])
        seq.sum_ps = keep.banks("sum_ps")
        with ExitStack() as inner:
            ph = Phase(nc, inner, "seqw")
            gb = ph.sb("gb", [P, 2])
            scale = ph.sb("scale", [P, 1])
            w = ph.sem("w")
            p = ph.sem("p")
            d = ph.sem("d")
            block = ph.block()

            @block.sync
            def _(sp):
                sp.dma_start(gb[:, 0:1], column(gamma)).then_inc(w, DMA)
                sp.dma_start(gb[:, 1:2], column(beta)).then_inc(w, DMA)
                sp.dma_start(seq.vt[:, :], vt).then_inc(w, DMA)

            @block.gpsimd
            def _(pool):
                nc.gpsimd.tensor_scalar(scale[:, :], wx_mv[:, 1:2], 1.0, 1e-5, ALU.mult, ALU.add).then_inc(p, 1)
                pool.wait_ge(p, 1)
                nc.gpsimd.tensor_tensor(scale[:, :], scale[:, :], K.minus_half[:, 0:1], ALU.pow).then_inc(p, 1)

            @block.vector
            def _(dve):
                chain = Chain(dve, d)
                chain.link(nc.vector.memset(seq.start[:, :], 0.0))
                chain.link(nc.vector.memset(seq.again[:, :], 1))
                dve.wait_ge(w, 3 * DMA)
                dve.wait_ge(p, 2)
                chain.link(nc.vector.tensor_tensor(scale[:, :], scale[:, :], gb[:, 0:1], ALU.mult))
                chain.link(nc.vector.tensor_scalar(seq.diag[:, :], K.ident[:, :], scale[:, 0:1], None, ALU.mult))
                chain.link(nc.vector.tensor_tensor(seq.shift[:, :], wx_mv[:, 0:1], scale[:, :], ALU.mult))
                chain.link(nc.vector.tensor_tensor(seq.shift[:, :], gb[:, 1:2], seq.shift[:, :], ALU.subtract))

        recur(nc, K, "seqg", wx, seq, state, W - WARM, WARM, None, False)
        settle(nc, K, "seqh", seq, state, False)
        with nc.Fori(0, 16):
            nc.all_engine_barrier()
            outer = nc.values_load(seq.again[0:1, 0:1])
            with nc.If(outer > 0):
                with nc.Fori(0, H // 16):
                    nc.all_engine_barrier()
                    again = nc.values_load(seq.again[0:1, 0:1])
                    with nc.If(again > 0):
                        recur(nc, K, "seqr", wx, seq, state, 0, W, y_out, True)
                        settle(nc, K, "seqs", seq, state, False)
                        recur(nc, K, "seqf", wx, seq, state, 0, SEQ_BLOCK, y_out, False)
                        settle(nc, K, "seqt", seq, state, True)
                    with nc.Else():
                        for eng in (nc.sync, nc.tensor, nc.vector, nc.scalar, nc.gpsimd):
                            eng.nop()
            with nc.Else():
                for eng in (nc.sync, nc.tensor, nc.vector, nc.scalar, nc.gpsimd):
                    eng.nop()
        nc.all_engine_barrier()


LEVELS = 3
RB = 8
BUFS = 4
CHUNK = RB * W
BLOCKS = H // RB
CB = CHUNK // 512
RING = H + 2 * PAD


def clear_rows(nc, name, images, pad):
    with ExitStack() as ctx:
        ph = Phase(nc, ctx, name)
        zero = ph.sb("zero", [P, pad * W])
        set_ = ph.sem("set")
        stored = ph.sem("stored")
        block = ph.block()

        @block.vector
        def _(dve):
            nc.vector.memset(zero[:, :], 0.0).then_inc(set_, 1)

        @block.sync
        def _(sp):
            sp.wait_ge(set_, 1)
            for im in images:
                for at in (0, pad + H):
                    sp.dma_start(im[:, at:at + pad, :].rearrange("c h w -> c (h w)"), zero[:, :]).then_inc(stored, DMA)
            sp.wait_ge(stored, 2 * len(images) * DMA)


def focal_front(nc, K, x, y, wf, bf, x_out, q_out, ctx_out, gates_out):
    G = LEVELS + 1
    with ExitStack() as ctx:
        ph = Phase(nc, ctx, "ff")
        xin = ph.sb("xin", [P, LONG, TILES, C])
        yin = ph.sb("yin", [P, LONG, STEP])
        xo = ph.sb("xo", [P, LONG, TILES, C])
        stats = ph.sb("stats", [P, MV, TILES, 6])
        mv = ph.sb("mv", [P, MV, TILES, 2])
        rstd = ph.sb("rstd", [P, MV, TILES])
        z = ph.sb("z", [P, 2, TILES, C])
        zt = ph.sb("zt", [P, 2, STEP])
        q = ph.sb("q", [P, 2, TILES, C])
        cx = ph.sb("cx", [P, 2, STEP])
        gates = ph.sb("gates", [G, 2, STEP])
        w_sb = ph.sb("w", [P, 2 * C + G])
        bq = ph.sb("bq", [P, C])
        bc = ph.sb("bc", [P, 1])
        bg = ph.sb("bg", [G, 1])
        yt_ps = ph.banks("yt_ps", 2)
        zt_ps = ph.banks("zt_ps", 2)
        cx_ps = ph.banks("cx_ps")
        q_ps = ph.banks("q_ps", 2)
        g_ps = ph.banks("g_ps")
        loaded = ph.sems("loaded", LONG)
        stored = ph.sems("stored", LONG)
        q_stored = ph.sems("q_stored", 2)
        cx_stored = ph.sems("cx_stored", 2)
        weights = ph.sem("weights")
        d_names = "xo_ready mv_ready z_ready q_ready"
        a_names = "zt_ready cx_ready"
        e_names = "ytp ztp cxp qp"
        p_names = "rstd_ready"
        S = {n: ph.sem(n) for n in f"{d_names} {a_names} {e_names} {p_names}".split()}
        chain_d = ph.sem("chain_d")
        chain_p = ph.sem("chain_p")
        passed_d = ph.sem("passed_d")
        passed_p = ph.sem("passed_p")
        block = ph.block()
        NW = 4

        @block.sync
        def _(sp):
            for dst, src in ((w_sb[:, :], wf), (bq[:, :], on_all(bf[0:C])), (bc[:, :], column(bf[C:2 * C])),
                             (bg[:, :], column(bf[2 * C:2 * C + G]))):
                sp.dma_start(dst, src).then_inc(weights, DMA)

            def load(t, b):
                u = LONG * t + b
                sp.dma_start(xin[:, b], token_tiles(x, u)).then_inc(loaded[b], DMA)
                for r in range(2):
                    sp.dma_start(yin[:, b, r * W:(r + 1) * W].rearrange("c (k j) -> c k j", k=SEQ_BLOCKS),
                                 y[:, :, 2 * u + r, :]).then_inc(loaded[b], DMA)

            def store(t, b):
                sp.wait_ge(S["z_ready"], of_step(t, b))
                sp.dma_start(token_tiles(x_out, LONG * t + b), xo[:, b]).then_inc(stored[b], DMA)

            for b in range(LONG):
                sp.nop().then_inc(stored[b], DMA)
                load(0, b)
            with sp.Fori(0, STEPS // LONG - 1) as t:
                for b in range(LONG):
                    store(t, b)
                    load(t + 1, b)
            for b in range(LONG):
                store(STEPS // LONG - 1, b)
            for b in range(LONG):
                sp.wait_ge(stored[b], DMA * (STEPS // LONG + 1))

        @block.vector
        def _(dve):
            start_counts(dve, [S[n] for n in d_names.split()])
            dve.wait_ge(weights, NW * DMA)
            chain = Chain(dve, chain_d, 0, passed_d)

            def add(t, s):
                b = s % LONG
                dve.wait_ge(loaded[b], times(t, s, 3))
                dve.wait_ge(S["ytp"], of_step(t, s))
                dve.wait_ge(stored[b], times(t, s))
                dve.wait_ge(S["rstd_ready"], of_step(t, s - MV))
                dve.wait_ge(S["z_ready"], of_step(t, s - MV))
                nc.vector.tensor_tensor(xo[:, b].rearrange("p j c -> p (j c)"), yt_ps[:, s % 2, :],
                                        xin[:, b].rearrange("p j c -> p (j c)"), ALU.add).then_inc(S["xo_ready"], 1)
                wait_alone(dve, S["xo_ready"], of_step(t, s), passed_d)
                column_stats(nc, chain, xo[:, b], stats[:, s % MV], mv[:, s % MV]).then_inc(S["mv_ready"], 1)

            def norm(t, s):
                dve.wait_ge(S["rstd_ready"], of_step(t, s))
                dve.wait_ge(S["ztp"], of_step(t, s - 2))
                normalize(nc, xo[:, s % LONG], mv[:, s % MV], rstd[:, s % MV], z[:, s % 2]).then_inc(S["z_ready"], 1)

            def queries(t, s):
                dve.wait_ge(S["qp"], of_step(t, s))
                dve.wait_ge(q_stored[s % 2], of_pair(t, s))
                nc.vector.tensor_tensor(q[:, s % 2], q_ps[:, s % 2, :].rearrange("p (j c) -> p j c", c=C),
                                        repeat_rows(bq[:, :], TILES), ALU.add).then_inc(S["q_ready"], 1)

            pipelined(dve, ((0, add), (5, queries), (2, norm)), chain, 1)

        @block.gpsimd
        def _(pool):
            start_counts(pool, [S[n] for n in p_names.split()])
            chain = Chain(pool, chain_p)

            def root(t, s):
                wait_alone(pool, S["mv_ready"], of_step(t, s), passed_p)
                wait_alone(pool, S["z_ready"], of_step(t, s - MV), passed_p)
                inverse_root(nc, pool, chain, mv[:, s % MV], K.minus_half[:, 0:TILES], rstd[:, s % MV],
                             1.0, 1e-6).then_inc(S["rstd_ready"], 1)

            pipelined(pool, ((0, root),), chain, 1)

        @block.tensor
        def _(pe):
            start_counts(pe, [S[n] for n in e_names.split()])
            pe.wait_ge(weights, NW * DMA)

            def turn_y(t, s):
                pe.wait_ge(loaded[s % LONG], times(t, s, 3))
                pe.wait_ge(S["xo_ready"], of_step(t, s - 2))
                for j in range(TILES):
                    last = nc.tensor.transpose(yt_ps[:, s % 2, j * P:(j + 1) * P],
                                               yin[:, s % LONG, j * P:(j + 1) * P], K.ident[:, :])
                last.then_inc(S["ytp"], 1)

            def turn_z(t, s):
                pe.wait_ge(S["z_ready"], of_step(t, s))
                pe.wait_ge(S["zt_ready"], of_step(t, s - 2))
                transpose_tiles(nc, zt_ps[:, s % 2], z[:, s % 2], K.ident).then_inc(S["ztp"], 1)

            def project(t, s):
                pe.wait_ge(S["zt_ready"], of_step(t, s))
                pe.wait_ge(S["cx_ready"], of_step(t, s - 1))
                nc.tensor.matmul(cx_ps[:, 0, :], w_sb[:, C:2 * C], zt[:, s % 2, :], start=True, stop=True)
                nc.tensor.matmul(g_ps[0:G, 0, :], w_sb[:, 2 * C:2 * C + G], zt[:, s % 2, :],
                                 start=True, stop=True).then_inc(S["cxp"], 1)
                pe.wait_ge(S["q_ready"], of_step(t, s - 2))
                for j in range(TILES):
                    last = nc.tensor.matmul(q_ps[:, s % 2, j * P:(j + 1) * P], zt[:, s % 2, j * P:(j + 1) * P],
                                            w_sb[:, 0:C], start=True, stop=True)
                last.then_inc(S["qp"], 1)

            pipelined(pe, ((0, turn_y), (3, turn_z), (4, project)))

        @block.scalar
        def _(act):
            start_counts(act, [S[n] for n in a_names.split()])
            for i in range(2):
                act.nop().then_inc(q_stored[i], DMA)
                act.nop().then_inc(cx_stored[i], 2 * DMA)
            act.wait_ge(weights, NW * DMA)

            def keep_zt(t, s):
                act.wait_ge(S["ztp"], of_step(t, s))
                act.wait_ge(S["qp"], of_step(t, s - 2))
                nc.scalar.activation(zt[:, s % 2, :], zt_ps[:, s % 2, :], ACT.Copy).then_inc(S["zt_ready"], 1)

            def context(t, s):
                act.wait_ge(S["cxp"], of_step(t, s))
                act.wait_ge(cx_stored[s % 2], of_pair(t, s, 2))
                nc.scalar.activation(gates[:, s % 2, :], g_ps[0:G, 0, :], ACT.Identity, bias=bg[:, 0:1])
                nc.scalar.activation(cx[:, s % 2, :], cx_ps[:, 0, :], ACT.Identity, bias=bc[:, 0:1])\
                    .then_inc(S["cx_ready"], 1)

            def store_all(t, s):
                u = LONG * t + s
                act.wait_ge(S["cx_ready"], of_step(t, s))
                act.dma_start(ctx_out[:, bass.ds(2 * u + PAD, 2), :],
                              cx[:, s % 2, :].rearrange("c (r w) -> c r w", r=2)).then_inc(cx_stored[s % 2], DMA)
                act.dma_start(gates_out[:, bass.ds(u * STEP, STEP)], gates[:, s % 2, :])\
                    .then_inc(cx_stored[s % 2], DMA)

            def store_q(t, s):
                act.wait_ge(S["q_ready"], of_step(t, s))
                act.dma_start(token_tiles(q_out, LONG * t + s), q[:, s % 2]).then_inc(q_stored[s % 2], DMA)

            pipelined(act, ((3, keep_zt), (4, context), (4, store_all), (6, store_q)))
            for i in range(2):
                act.wait_ge(q_stored[i], DMA * (STEPS // 2 + 1))
                act.wait_ge(cx_stored[i], 2 * DMA * (STEPS // 2 + 1))


def depthwise(nc, K, name, k, pe_taps, image, kernel, gates, level, acc_in, image_out, acc_out, sums):
    R = k // 2
    WIN = RB + 2 * R
    WW = W + 2 * PAD
    taps = [(dy, dx) for dy in range(k) for dx in range(k)]
    dve_taps = taps[pe_taps:]
    n_loads = 3 if acc_in is not None else 2
    with ExitStack() as ctx:
        ph = Phase(nc, ctx, name)
        win = ph.sb("win", [P, BUFS, WIN, WW])
        gate = ph.sb("gate", [P, BUFS, CHUNK])
        acc = ph.sb("acc", [P, BUFS, CHUNK])
        total = ph.sb("total", [P, 2, CHUNK])
        cx = ph.sb("cx", [P, 2, CHUNK])
        kt = ph.sb("kt", [P, k * k])
        krow = ph.sb("krow", [k * k, C])
        diag = ph.sb("diag", [P, pe_taps, P])
        conv_ps = ph.banks("conv_ps", 2 * CB)
        loaded = ph.sems("loaded", BUFS)
        cx_stored = ph.sems("cx_stored", 2)
        acc_stored = ph.sems("acc_stored", BUFS)
        weights = ph.sem("weights")
        begun = ph.sem("begun")
        kt_ready = ph.sem("kt_ready")
        d_names = "conv_read total_ready"
        S = {n: ph.sem(n) for n in f"{d_names} conv_ready cx_ready acc_ready".split()}
        chain_d = ph.sem("chain_d")
        passed_p = ph.sem("passed_p")
        chain_p = ph.sem("chain_p")
        block = ph.block()

        @block.sync
        def _(sp):
            sp.dma_start(krow[:, :], kernel.rearrange("y x a c -> (y x a) c")).then_inc(weights, DMA)
            sp.wait_ge(begun, 1)

            def load(t, b):
                u = BUFS * t + b
                sp.dma_start(win[:, b, :, PAD:PAD + W], image[:, bass.ds(RB * u + PAD - R, WIN), :]).then_inc(loaded[b], DMA)
                g = gates[level, bass.ds(u * CHUNK, CHUNK)]
                sp.dma_start(gate[:, b, :], bass.AP(g.tensor, g.offset, [[0, P]] + [list(d) for d in g.ap]))\
                    .then_inc(loaded[b], DMA)
                if acc_in is not None:
                    sp.dma_start(acc[:, b, :], acc_in[:, bass.ds(u * CHUNK, CHUNK)]).then_inc(loaded[b], DMA)

            def store(t, b):
                u = BUFS * t + b
                sp.wait_ge(S["acc_ready"], of_step(t, b, BUFS))
                sp.dma_start(acc_out[:, bass.ds(u * CHUNK, CHUNK)], acc[:, b, :]).then_inc(acc_stored[b], DMA)
                sp.wait_ge(acc_stored[b], DMA * (t + 1))

            for b in range(BUFS):
                load(0, b)
            with sp.Fori(0, BLOCKS // BUFS - 1) as t:
                for b in range(BUFS):
                    store(t, b)
                    load(t + 1, b)
            for b in range(BUFS):
                store(BLOCKS // BUFS - 1, b)

        @block.vector
        def _(dve):
            start_counts(dve, [S[n] for n in d_names.split()], BUFS)
            nc.vector.memset(win[:, :, :, :], 0.0).then_inc(begun, 1)
            dve.wait_ge(kt_ready, 1)
            nc.vector.tensor_copy(kt[:, :], conv_ps[:, 0, 0:k * k]).then_inc(begun, 1)
            dve.wait_ge(begun, 2)
            for i in range(pe_taps):
                last = nc.vector.tensor_scalar(diag[:, i, :], K.ident[:, :], kt[:, i:i + 1], None, ALU.mult)
            last.then_inc(begun, 1)
            dve.wait_ge(begun, 3)
            links = len(dve_taps) - 2
            with dve.Fori(0, BLOCKS // BUFS) as t:
                chain = Chain(dve, chain_d, BUFS * links * t)
                for b in range(BUFS):
                    dve.wait_ge(loaded[b], n_loads * DMA * (t + 1))
                    dve.wait_ge(S["conv_ready"], of_step(t, b, BUFS))
                    dve.wait_ge(S["cx_ready"], of_step(t, b - 2, BUFS))
                    out = total[:, b % 2, :].rearrange("p (r w) -> p r w", w=W)
                    conv = conv_ps[:, b % 2 * CB:(b % 2 + 1) * CB, :].rearrange("p n f -> p (n f)").rearrange("p (r w) -> p r w", w=W)
                    for i, (dy, dx) in enumerate(dve_taps):
                        x0 = dx + PAD - R
                        ins = nc.vector.scalar_tensor_tensor(
                            out, win[:, b, dy:dy + RB, x0:x0 + W], kt[:, pe_taps + i:pe_taps + i + 1],
                            out if i else conv, ALU.mult, ALU.add)
                        if i == 0:
                            ins.then_inc(S["conv_read"], 1)
                            dve.wait_ge(S["conv_read"], of_step(t, b, BUFS))
                        elif i < len(dve_taps) - 1:
                            chain.link(ins)
                        else:
                            ins.then_inc(S["total_ready"], 1)
                assert chain.n == BUFS * links

        @block.tensor
        def _(pe):
            start_counts(pe, [S["conv_ready"]], BUFS)
            pe.wait_ge(weights, DMA)
            nc.tensor.transpose(conv_ps[:, 0, 0:k * k], krow[:, :], K.ident[0:k * k, 0:k * k]).then_inc(kt_ready, 1)
            pe.wait_ge(begun, 3)
            with pe.Fori(0, BLOCKS // BUFS) as t:
                for b in range(BUFS):
                    pe.wait_ge(loaded[b], n_loads * DMA * (t + 1))
                    pe.wait_ge(S["conv_read"], of_step(t, b - 2, BUFS))
                    for i, (dy, dx) in enumerate(taps[:pe_taps]):
                        x0 = dx + PAD - R
                        for n in range(CB):
                            last = nc.tensor.matmul(conv_ps[:, b % 2 * CB + n, :], diag[:, i, :],
                                                    win[:, b, dy + 2 * n:dy + 2 * n + 2, x0:x0 + W],
                                                    start=(i == 0), stop=(i == pe_taps - 1))
                    last.then_inc(S["conv_ready"], 1)

        @block.scalar
        def _(act):
            start_counts(act, [S["cx_ready"]], BUFS)
            for i in range(2):
                act.nop().then_inc(cx_stored[i], DMA)
            with act.Fori(0, BLOCKS // BUFS) as t:
                for b in range(BUFS):
                    u = BUFS * t + b
                    act.wait_ge(S["total_ready"], of_step(t, b, BUFS))
                    act.wait_ge(S["acc_ready"], of_step(t, b - 2, BUFS))
                    if image_out is not None:
                        act.wait_ge(cx_stored[b % 2], DMA * (BUFS // 2) * t + DMA * (b // 2 + 1))
                        nc.scalar.activation(cx[:, b % 2, :], total[:, b % 2, :], ACT.Gelu).then_inc(S["cx_ready"], 1)
                        act.wait_ge(S["cx_ready"], of_step(t, b, BUFS))
                        act.dma_start(image_out[:, bass.ds(RB * u + PAD, RB), :],
                                      cx[:, b % 2, :].rearrange("c (r w) -> c r w", w=W)).then_inc(cx_stored[b % 2], DMA)
                    else:
                        nc.scalar.activation(cx[:, b % 2, :], total[:, b % 2, :], ACT.Gelu,
                                             accum_out=sums[:, bass.ds(u, 1)]).then_inc(S["cx_ready"], 1)
            if image_out is not None:
                for i in range(2):
                    act.wait_ge(cx_stored[i], DMA * (BLOCKS // 2 + 1))

        @block.gpsimd
        def _(pool):
            start_counts(pool, [S["acc_ready"]], BUFS)
            with pool.Fori(0, BLOCKS // BUFS) as t:
                chain = Chain(pool, chain_p, BUFS * t)
                for b in range(BUFS):
                    wait_alone(pool, loaded[b], n_loads * DMA * (t + 1), passed_p)
                    wait_alone(pool, S["cx_ready"], of_step(t, b, BUFS), passed_p)
                    if acc_in is None:
                        nc.gpsimd.tensor_tensor(acc[:, b, :], cx[:, b % 2, :], gate[:, b, :], ALU.mult)\
                            .then_inc(S["acc_ready"], 1)
                    else:
                        chain.link(nc.gpsimd.tensor_tensor(gate[:, b, :], cx[:, b % 2, :], gate[:, b, :], ALU.mult))
                        nc.gpsimd.tensor_tensor(acc[:, b, :], acc[:, b, :], gate[:, b, :], ALU.add)\
                            .then_inc(S["acc_ready"], 1)


def modulate(nc, K, x, q, acc, gates, sums, wh, bh, gamma, beta, wp, bp, x_out):
    with ExitStack() as ctx:
        ph = Phase(nc, ctx, "mod")
        xin = ph.sb("xin", [P, LONG, TILES, C])
        qin = ph.sb("qin", [P, LONG, TILES, C])
        ain = ph.sb("ain", [P, LONG, STEP])
        gin = ph.sb("gin", [2, LONG, STEP])
        xo = ph.sb("xo", [P, LONG, TILES, C])
        prod = ph.sb("prod", [P, MV, TILES, C])
        stats = ph.sb("stats", [P, MV, TILES, 6])
        mv = ph.sb("mv", [P, MV, TILES, 2])
        rstd = ph.sb("rstd", [P, MV, TILES])
        z = ph.sb("z", [P, 2, TILES, C])
        zt = ph.sb("zt", [P, 2, STEP])
        w_h = ph.sb("w_h", [P, C])
        w_p = ph.sb("w_p", [P, C])
        rows = ph.sb("rows", [2, C])
        gb = ph.sb("gb", [P, 2])
        b_p = ph.sb("b_p", [P, C])
        mean = ph.sb("mean", [P, 1])
        glob = ph.sb("glob", [P, 1])
        m_ps = ph.banks("m_ps", 2)
        zt_ps = ph.banks("zt_ps", 2)
        o_ps = ph.banks("o_ps", 2)
        r_ps = ph.banks("r_ps")
        loaded = ph.sems("loaded", LONG)
        stored = ph.sems("stored", LONG)
        weights = ph.sem("weights")
        begun = ph.sem("begun")
        ones_set = ph.sem("ones_set")
        row_ready = ph.sem("row_ready")
        glob_ready = ph.sem("glob_ready")
        rowp = ph.sem("rowp")
        d_names = "prod_ready mv_ready z_ready xo_ready"
        a_names = "zt_ready"
        e_names = "mp ztp op"
        p_names = "rstd_ready xb_ready"
        S = {n: ph.sem(n) for n in f"{d_names} {a_names} {e_names} {p_names}".split()}
        chain_d = ph.sem("chain_d")
        chain_p = ph.sem("chain_p")
        passed_d = ph.sem("passed_d")
        passed_p = ph.sem("passed_p")
        block = ph.block()
        NW = 6

        @block.sync
        def _(sp):
            for dst, src in ((w_h[:, :], wh), (w_p[:, :], wp), (gb[:, 0:1], column(gamma)), (gb[:, 1:2], column(beta)),
                             (b_p[:, :], on_all(bp)), (rows[1:2, :], on_all(bh, 1))):
                sp.dma_start(dst, src).then_inc(weights, DMA)
            sp.wait_ge(ones_set, 1)

            def load(t, b):
                u = LONG * t + b
                sp.dma_start(ain[:, b, :], acc[:, bass.ds(u * STEP, STEP)]).then_inc(loaded[b], DMA)
                sp.dma_start(gin[0:1, b, :], gates[LEVELS:LEVELS + 1, bass.ds(u * STEP, STEP)]).then_inc(loaded[b], DMA)
                sp.dma_start(qin[:, b], token_tiles(q, u)).then_inc(loaded[b], DMA)
                sp.dma_start(xin[:, b], token_tiles(x, u)).then_inc(loaded[b], DMA)

            def store(t, b):
                sp.wait_ge(S["xo_ready"], of_step(t, b))
                sp.dma_start(token_tiles(x_out, LONG * t + b), xo[:, b]).then_inc(stored[b], DMA)

            for b in range(LONG):
                sp.nop().then_inc(stored[b], DMA)
                load(0, b)
            with sp.Fori(0, STEPS // LONG - 1) as t:
                for b in range(LONG):
                    store(t, b)
                    load(t + 1, b)
            for b in range(LONG):
                store(STEPS // LONG - 1, b)
            for b in range(LONG):
                sp.wait_ge(stored[b], DMA * (STEPS // LONG + 1))

        @block.vector
        def _(dve):
            start_counts(dve, [S[n] for n in d_names.split()])
            nc.vector.memset(gin[:, :, :], 1.0).then_inc(ones_set, 1)
            nc.vector.reduce_sum(mean[:, :], sums[:, :], AX.X).then_inc(begun, 1)
            dve.wait_ge(rowp, 1)
            nc.vector.tensor_copy(rows[0:1, :], r_ps[0:1, 0, 0:C]).then_inc(row_ready, 1)
            chain = Chain(dve, chain_d, 0, passed_d)

            def product(t, s):
                dve.wait_ge(loaded[s % LONG], times(t, s, 4))
                dve.wait_ge(S["mp"], of_step(t, s))
                dve.wait_ge(S["rstd_ready"], of_step(t, s - MV))
                dve.wait_ge(S["z_ready"], of_step(t, s - MV))
                nc.vector.tensor_tensor(prod[:, s % MV].rearrange("p j c -> p (j c)"), m_ps[:, s % 2, :],
                                        qin[:, s % LONG].rearrange("p j c -> p (j c)"), ALU.mult)\
                    .then_inc(S["prod_ready"], 1)
                wait_alone(dve, S["prod_ready"], of_step(t, s), passed_d)
                column_stats(nc, chain, prod[:, s % MV], stats[:, s % MV], mv[:, s % MV]).then_inc(S["mv_ready"], 1)

            def norm(t, s):
                dve.wait_ge(S["rstd_ready"], of_step(t, s))
                dve.wait_ge(S["ztp"], of_step(t, s - 2))
                normalize(nc, prod[:, s % MV], mv[:, s % MV], rstd[:, s % MV], z[:, s % 2]).then_inc(S["z_ready"], 1)

            def result(t, s):
                b = s % LONG
                dve.wait_ge(S["op"], of_step(t, s))
                dve.wait_ge(S["xb_ready"], of_step(t, s))
                dve.wait_ge(stored[b], times(t, s))
                nc.vector.tensor_tensor(xo[:, b].rearrange("p j c -> p (j c)"), o_ps[:, s % 2, :],
                                        xin[:, b].rearrange("p j c -> p (j c)"), ALU.add).then_inc(S["xo_ready"], 1)

            pipelined(dve, ((0, product), (5, result), (2, norm)), chain, 1)

        @block.gpsimd
        def _(pool):
            start_counts(pool, [S[n] for n in p_names.split()])
            pool.wait_ge(weights, NW * DMA)
            chain = Chain(pool, chain_p)

            def root(t, s):
                wait_alone(pool, S["mv_ready"], of_step(t, s), passed_p)
                wait_alone(pool, S["z_ready"], of_step(t, s - MV), passed_p)
                inverse_root(nc, pool, chain, mv[:, s % MV], K.minus_half[:, 0:TILES], rstd[:, s % MV],
                             1.0, 1e-3).then_inc(S["rstd_ready"], 1)
                b = s % LONG
                pool.wait_ge(loaded[b], times(t, s, 4))
                nc.gpsimd.tensor_tensor(xin[:, b], xin[:, b], repeat_rows(b_p[:, :], TILES), ALU.add)\
                    .then_inc(S["xb_ready"], 1)

            pipelined(pool, ((0, root),), chain, 1)

        @block.tensor
        def _(pe):
            start_counts(pe, [S[n] for n in e_names.split()])
            pe.wait_ge(weights, NW * DMA)
            pe.wait_ge(glob_ready, 1)
            nc.tensor.matmul(r_ps[0:1, 0, 0:C], glob[:, :], w_h[:, :], start=True, stop=True).then_inc(rowp, 1)
            pe.wait_ge(row_ready, 1)

            def modulator(t, s):
                pe.wait_ge(loaded[s % LONG], times(t, s, 4))
                pe.wait_ge(S["prod_ready"], of_step(t, s - 2))
                for j in range(TILES):
                    tile = slice(j * P, (j + 1) * P)
                    nc.tensor.matmul(m_ps[:, s % 2, tile], ain[:, s % LONG, tile], w_h[:, :], start=True, stop=False)
                    last = nc.tensor.matmul(m_ps[:, s % 2, tile], gin[:, s % LONG, tile], rows[:, :],
                                            start=False, stop=True)
                last.then_inc(S["mp"], 1)

            def turn_z(t, s):
                pe.wait_ge(S["z_ready"], of_step(t, s))
                pe.wait_ge(S["zt_ready"], of_step(t, s - 2))
                transpose_tiles(nc, zt_ps[:, s % 2], z[:, s % 2], K.ident).then_inc(S["ztp"], 1)

            def project(t, s):
                pe.wait_ge(S["zt_ready"], of_step(t, s))
                pe.wait_ge(S["xo_ready"], of_step(t, s - 2))
                for j in range(TILES):
                    last = nc.tensor.matmul(o_ps[:, s % 2, j * P:(j + 1) * P], zt[:, s % 2, j * P:(j + 1) * P],
                                            w_p[:, :], start=True, stop=True)
                last.then_inc(S["op"], 1)

            pipelined(pe, ((0, modulator), (3, turn_z), (4, project)))

        @block.scalar
        def _(act):
            start_counts(act, [S[n] for n in a_names.split()])
            act.wait_ge(begun, 1)
            nc.scalar.activation(glob[:, :], mean[:, :], ACT.Gelu, scale=1.0 / N).then_inc(glob_ready, 1)
            act.wait_ge(weights, NW * DMA)

            def keep_zt(t, s):
                act.wait_ge(S["ztp"], of_step(t, s))
                act.wait_ge(S["op"], of_step(t, s - 2))
                nc.scalar.activation(zt[:, s % 2, :], zt_ps[:, s % 2, :], ACT.Identity, bias=gb[:, 1:2],
                                     scale=gb[:, 0:1]).then_inc(S["zt_ready"], 1)

            pipelined(act, ((3, keep_zt),))


KW = 3
TAPS = KW * KW
EDGE = 2
TAB_ROWS = H + 2 * EDGE - 1
TAB_COLS = W + 2 * EDGE
CELL = 2 * C
TAB_ROW = TAB_COLS * CELL
TABLE = TAB_ROWS * TAB_ROW


def flat_part(a, offset, dims):
    return bass.AP(a.tensor, a.offset + offset, dims)


def deform_front(nc, K, x, table, image):
    with ExitStack() as ctx:
        ph = Phase(nc, ctx, "df")
        xin = ph.sb("xin", [P, LONG, TILES, C])
        stats = ph.sb("stats", [P, MV, TILES, 6])
        mv = ph.sb("mv", [P, MV, TILES, 2])
        rstd = ph.sb("rstd", [P, MV, TILES])
        z = ph.sb("z", [P, LONG, TILES, C])
        zt = ph.sb("zt", [P, 2, STEP])
        zero = ph.sb("zero", [P, EDGE * TAB_ROW // P])
        zt_ps = ph.banks("zt_ps", 2)
        loaded = ph.sems("loaded", LONG)
        stored = ph.sems("stored", LONG)
        zt_stored = ph.sems("zt_stored", 2)
        zero_set = ph.sem("zero_set")
        edges = ph.sem("edges")
        S = {n: ph.sem(n) for n in "mv_ready z_ready zt_ready ztp rstd_ready".split()}
        chain_d = ph.sem("chain_d")
        chain_p = ph.sem("chain_p")
        passed_d = ph.sem("passed_d")
        passed_p = ph.sem("passed_p")
        block = ph.block()
        BODIES = STEPS // LONG

        @block.sync
        def _(sp):
            sp.wait_ge(zero_set, 1)
            n = 0
            for row in (0, TAB_ROWS - EDGE):
                sp.dma_start(flat_part(table, row * TAB_ROW, [[EDGE * TAB_ROW // P, P], [1, EDGE * TAB_ROW // P]]),
                             zero[:, :]).then_inc(edges, DMA)
                n += 1
            for row in range(EDGE, TAB_ROWS - EDGE, P):
                rows = min(P, TAB_ROWS - EDGE - row)
                for col in (0, TAB_COLS - EDGE):
                    sp.dma_start(flat_part(table, row * TAB_ROW + col * CELL, [[TAB_ROW, rows], [1, EDGE * CELL]]),
                                 zero[0:rows, 0:EDGE * CELL]).then_inc(edges, DMA)
                    n += 1
            sp.wait_ge(edges, n * DMA)

            def load(t, b):
                sp.dma_start(xin[:, b], token_tiles(x, LONG * t + b)).then_inc(loaded[b], DMA)

            def store(t, b):
                sp.wait_ge(S["z_ready"], of_step(t, b))
                u = LONG * t + b
                for r in range(2):
                    for part in range(2):
                        at = (EDGE + r - part) * TAB_ROW + EDGE * CELL + part * C
                        cells = bass.AP(table.tensor, u * (2 * TAB_ROW) + (table.offset + at),
                                        [[CELL, P], [P * CELL, 2], [1, C]])
                        sp.dma_start(cells, z[:, b, 2 * r:2 * r + 2, :]).then_inc(stored[b], DMA)

            for b in range(LONG):
                sp.nop().then_inc(stored[b], 4 * DMA)
                load(0, b)
            with sp.Fori(0, BODIES - 1) as t:
                for b in range(LONG):
                    store(t, b)
                    load(t + 1, b)
            for b in range(LONG):
                store(BODIES - 1, b)
            for b in range(LONG):
                sp.wait_ge(stored[b], 4 * DMA * (BODIES + 1))

        @block.vector
        def _(dve):
            nc.vector.memset(zero[:, :], 0.0).then_inc(zero_set, 1)
            start_counts(dve, [S["mv_ready"], S["z_ready"]])
            chain = Chain(dve, chain_d, 0, passed_d)

            def moments(t, s):
                dve.wait_ge(loaded[s % LONG], times(t, s))
                dve.wait_ge(S["rstd_ready"], of_step(t, s - MV))
                dve.wait_ge(S["z_ready"], of_step(t, s - MV))
                column_stats(nc, chain, xin[:, s % LONG], stats[:, s % MV], mv[:, s % MV])\
                    .then_inc(S["mv_ready"], 1)

            def norm(t, s):
                b = s % LONG
                dve.wait_ge(S["rstd_ready"], of_step(t, s))
                dve.wait_ge(stored[b], times(t, s, 4))
                dve.wait_ge(S["ztp"], of_step(t, s - LONG))
                normalize(nc, xin[:, b], mv[:, s % MV], rstd[:, s % MV], z[:, b]).then_inc(S["z_ready"], 1)

            pipelined(dve, ((0, moments), (2, norm)), chain, 1)

        @block.gpsimd
        def _(pool):
            start_counts(pool, [S["rstd_ready"]])
            chain = Chain(pool, chain_p)

            def root(t, s):
                wait_alone(pool, S["mv_ready"], of_step(t, s), passed_p)
                wait_alone(pool, S["z_ready"], of_step(t, s - MV), passed_p)
                inverse_root(nc, pool, chain, mv[:, s % MV], K.minus_half[:, 0:TILES], rstd[:, s % MV],
                             1.0, 1e-6).then_inc(S["rstd_ready"], 1)

            pipelined(pool, ((0, root),), chain, 1)

        @block.tensor
        def _(pe):
            start_counts(pe, [S["ztp"]])

            def turn(t, s):
                pe.wait_ge(S["z_ready"], of_step(t, s))
                pe.wait_ge(S["zt_ready"], of_step(t, s - 2))
                transpose_tiles(nc, zt_ps[:, s % 2], z[:, s % LONG], K.ident).then_inc(S["ztp"], 1)

            pipelined(pe, ((3, turn),))

        @block.scalar
        def _(act):
            start_counts(act, [S["zt_ready"]])
            for i in range(2):
                act.nop().then_inc(zt_stored[i], DMA)

            def keep_zt(t, s):
                act.wait_ge(S["ztp"], of_step(t, s))
                act.wait_ge(zt_stored[s % 2], of_pair(t, s))
                nc.scalar.activation(zt[:, s % 2, :], zt_ps[:, s % 2, :], ACT.Copy).then_inc(S["zt_ready"], 1)
                act.wait_ge(S["zt_ready"], of_step(t, s))
                act.dma_start(image[:, bass.ds(2 * (LONG * t + s) + 1, 2), :],
                              zt[:, s % 2, :].rearrange("c (r w) -> c r w", r=2)).then_inc(zt_stored[s % 2], DMA)

            pipelined(act, ((3, keep_zt),))
            for i in range(2):
                act.wait_ge(zt_stored[i], DMA * (STEPS // 2 + 1))


def deform(nc, K, x, table, image, kernel, bias, offset_w, offset_b, x_out):
    T2 = 2 * TAPS
    CORNERS = 4
    GROUPS = 3
    PER = TAPS // GROUPS
    TWO = 2
    BODIES = STEPS // TWO
    with ExitStack() as ctx:
        ph = Phase(nc, ctx, "dc")
        win = ph.sb("win", [P, TWO, 4, W + 2])
        xin = ph.sb("xin", [P, TWO, TILES, C])
        xo = ph.sb("xo", [P, TWO, TILES, C])
        grid = ph.sb("grid", [P, TILES, TAPS, 2])
        grid_i = ph.sb("grid_i", [P, TILES, TAPS, 2], i32)
        ob = ph.sb("ob", [P, T2])
        at = ph.sb("at", [P, TILES, TAPS, 2])
        low = ph.sb("low", [P, TILES, TAPS, 2])
        low_i = ph.sb("low_i", [P, TILES, TAPS, 2], i32)
        above = ph.sb("above", [P, TILES, TAPS, 2])
        frac = ph.sb("frac", [P, TILES, TAPS, 2, 2])
        cell = ph.sb("cell", [P, TILES * TAPS])
        cell_u = ph.sb("cell_u", [P, TWO, TILES * TAPS], u32)
        corner = ph.sb("corner", [P, TWO, TILES * TAPS, 2, 2])
        g = ph.sb("g", [P, TILES, TAPS, CORNERS, C])
        vt = ph.sb("vt", [P, TWO, GROUPS, PER * P])
        w_off = ph.sb("w_off", [P, TAPS, T2])
        w_k = ph.sb("w_k", [P, TAPS, C])
        b_k = ph.sb("b_k", [P, C])
        vt_ps = ph.banks("vt_ps", TWO * GROUPS)
        off_ps = ph.banks("off_ps")
        out_ps = ph.banks("out_ps")
        win_loaded = ph.sems("win_loaded", TWO)
        x_loaded = ph.sems("x_loaded", TWO)
        stored = ph.sems("stored", TWO)
        gathered = [K.by_pool.pop() for _ in range(TILES)]
        weights = ph.sem("weights")
        ready = ph.sem("ready")
        cleared = ph.sem("cleared")
        S = {n: ph.sem(n) for n in "offp off_read cell_ready xb_ready xo_ready".split()}
        Q = {n: ph.sem(n) for n in "weighted vtp vt_ready vt_used".split()}
        chain_d = ph.sem("chain_d")
        passed_p = ph.sem("passed_p")
        passed_d = ph.sem("passed_d")
        block = ph.block()
        NW = 4
        TB = TWO * TILES
        flat = flat_part(table, 0, [[1, TABLE], [1, 1]])

        def steps(t, b):
            return of_step(t, b, TWO)

        def tiles(t, b, j):
            return of_step(t, TILES * b + j, TB)

        @block.sync
        def _(sp):
            for dst, src in ((w_off[:, :, :], offset_w.rearrange("y x c o -> c (y x) o")),
                             (w_k[:, :, :], kernel.rearrange("y x c o -> c (y x) o")),
                             (ob[:, :], on_all(offset_b)), (b_k[:, :], on_all(bias))):
                sp.dma_start(dst, src).then_inc(weights, DMA)
            sp.wait_ge(cleared, 1)

            def load_window(t, b):
                sp.dma_start(win[:, b, :, 1:1 + W], image[:, bass.ds(2 * (TWO * t + b), 4), :])\
                    .then_inc(win_loaded[b], DMA)

            def load_x(t, b):
                sp.dma_start(xin[:, b], token_tiles(x, TWO * t + b)).then_inc(x_loaded[b], DMA)

            def step(t, b, more_windows, more):
                if more_windows:
                    nt, nb = (t, 1) if b == 0 else (t + 1, 0)
                    sp.wait_ge(S["offp"], steps(nt, nb))
                    load_window(nt + 1, nb)
                sp.wait_ge(S["xo_ready"], steps(t, b))
                sp.dma_start(token_tiles(x_out, TWO * t + b), xo[:, b]).then_inc(stored[b], DMA)
                if more:
                    load_x(t + 1, b)

            for b in range(TWO):
                sp.nop().then_inc(stored[b], DMA)
                load_window(0, b)
                load_x(0, b)
            sp.wait_ge(S["offp"], steps(0, 0))
            load_window(1, 0)
            with sp.Fori(0, BODIES - 2) as t:
                for b in range(TWO):
                    step(t, b, True, True)
            step(BODIES - 2, 0, True, True)
            step(BODIES - 2, 1, False, True)
            for b in range(TWO):
                step(BODIES - 1, b, False, False)
            for b in range(TWO):
                sp.wait_ge(stored[b], DMA * (BODIES + 1))

        @block.gpsimd
        def _(pool):
            nc.gpsimd.iota(grid_i[:, :, :, 0], pattern=[[0, TILES], [0, TAPS]], base=0, channel_multiplier=0)\
                .then_inc(ready, 1)
            nc.gpsimd.iota(grid_i[:, :, :, 1], pattern=[[0, TILES], [0, TAPS]], base=0, channel_multiplier=1)\
                .then_inc(ready, 1)
            def step(t, b):
                for j in range(TILES):
                    if j == 0:
                        wait_alone(pool, S["cell_ready"], steps(t, b), passed_p)
                    wait_alone(pool, Q["vtp"], tiles(t, b - 1, j), passed_p)
                    for k in range(TAPS):
                        i = j * TAPS + k
                        pool.indirect_dma_start(
                            out=g[:, j, k].rearrange("p q c -> p (q c)"), out_offset=None, in_=flat,
                            in_offset=bass.IndirectOffsetOnAxis(ap=cell_u[:, b, i:i + 1], axis=0))\
                            .then_inc(gathered[j], DMA)

            with pool.Fori(0, BODIES) as t:
                for b in range(TWO):
                    step(t, b)

        @block.vector
        def _(dve):
            start_counts(dve, [S["off_read"], S["cell_ready"], S["xb_ready"], S["xo_ready"]], TWO)
            start_counts(dve, [Q["weighted"]], TB)
            nc.vector.memset(win[:, :, :, :], 0.0).then_inc(cleared, 1)
            dve.wait_ge(ready, 2)
            nc.vector.tensor_copy(grid[:, :, :, :], grid_i[:, :, :, :]).then_inc(ready, 1)
            dve.wait_ge(ready, 3)
            n = 3
            for k in range(TAPS):
                ky, kx = divmod(k, KW)
                for j in range(TILES):
                    r, h = divmod(j, 2)
                    nc.vector.tensor_scalar(grid[:, j, k, 0:1], grid[:, j, k, 0:1], float(r + ky - 1), None, ALU.add)\
                        .then_inc(ready, 1)
                    nc.vector.tensor_scalar(grid[:, j, k, 1:2], grid[:, j, k, 1:2], float(h * P + kx - 1), None, ALU.add)\
                        .then_inc(ready, 1)
                    n += 2
            dve.wait_ge(ready, n)
            dve.wait_ge(weights, NW * DMA)

            def cells(chain, t, b):
                dve.wait_ge(S["offp"], steps(t, b))
                a4 = at[:, :, :, :]
                ins = nc.vector.tensor_tensor(at[:, :, :, :].rearrange("p j k a -> p j (k a)"),
                                              off_ps[:, 0, 0:TILES * T2].rearrange("p (j o) -> p j o", o=T2),
                                              repeat_rows(ob[:, :], TILES), ALU.add)
                ins.then_inc(S["off_read"], 1)
                wait_alone(dve, S["off_read"], steps(t, b), passed_d)
                chain.link(nc.vector.tensor_tensor(a4, a4, grid[:, :, :, :], ALU.add))
                nc.vector.tensor_scalar(grid[:, :, :, 0], grid[:, :, :, 0], 2.0, None, ALU.add)
                chain.link(nc.vector.tensor_scalar(a4, a4, float(-EDGE), float(H), ALU.max, ALU.min))
                chain.link(nc.vector.tensor_copy(low_i[:, :, :, :], a4))
                chain.link(nc.vector.tensor_copy(low[:, :, :, :], low_i[:, :, :, :]))
                chain.link(nc.vector.tensor_tensor(above[:, :, :, :], low[:, :, :, :], a4, ALU.is_gt))
                chain.link(nc.vector.tensor_tensor(low[:, :, :, :], low[:, :, :, :], above[:, :, :, :], ALU.subtract))
                chain.link(nc.vector.tensor_tensor(frac[:, :, :, :, 1], a4, low[:, :, :, :], ALU.subtract))
                nc.vector.tensor_scalar(above[:, :, :, 0], low[:, :, :, 1], float(CELL),
                                        float(EDGE * TAB_ROW + EDGE * CELL), ALU.mult, ALU.add)
                chain.link(nc.vector.tensor_scalar(frac[:, :, :, :, 0], frac[:, :, :, :, 1], -1.0, 1.0,
                                                   ALU.mult, ALU.add))
                chain.link(nc.vector.scalar_tensor_tensor(
                    cell[:, :].rearrange("p (j k) -> p j k", k=TAPS), low[:, :, :, 0], float(TAB_ROW),
                    above[:, :, :, 0], ALU.mult, ALU.add))
                f = frac[:, :, :, :, :].rearrange("p j k a s -> p (j k) a s")
                xs, ys = f[:, :, 1, :], f[:, :, 0, :]
                d = [list(e) for e in ys.ap]
                ys = bass.AP(ys.tensor, ys.offset, [d[0], d[1], [0, 2], d[2]])
                nc.vector.tensor_tensor(corner[:, b], spread(xs, 2), ys, ALU.mult)
                nc.vector.tensor_copy(cell_u[:, b, :], cell[:, :]).then_inc(S["cell_ready"], 1)

            def add_bias(t, b):
                dve.wait_ge(x_loaded[b], DMA * (t + 1))
                nc.vector.tensor_tensor(xin[:, b], xin[:, b], repeat_rows(b_k[:, :], TILES), ALU.add)\
                    .then_inc(S["xb_ready"], 1)

            def result(t, b):
                dve.wait_ge(Q["vt_used"], tiles(t, b, TILES - 1))
                dve.wait_ge(S["xb_ready"], steps(t, b))
                dve.wait_ge(stored[b], DMA * (t + 1))
                nc.vector.tensor_tensor(xo[:, b].rearrange("p j c -> p (j c)"), out_ps[:, 0, :],
                                        xin[:, b].rearrange("p j c -> p (j c)"), ALU.add).then_inc(S["xo_ready"], 1)

            LINKS = 9
            first = Chain(dve, chain_d, 0, passed_d)
            cells(first, 0, 0)
            assert first.n == LINKS

            def body(t, first, more):
                chain = Chain(dve, chain_d, (TWO * LINKS + TB) * t + LINKS, passed_d)
                for b in range(TWO):
                    if more or b == 0:
                        cells(chain, *((t, 1) if b == 0 else (t + 1, 0)))
                    for j in range(TILES):
                        if j == 0:
                            wait_alone(dve, S["cell_ready"], steps(t, b), passed_d)
                        dve.wait_ge(gathered[j], TAPS * DMA * (TWO * t + b + 1))
                        gj = g[:, j].rearrange("p k q c -> p (k q) c")
                        cw = corner[:, b, j * TAPS:(j + 1) * TAPS].rearrange("p k x y -> p (k x y)")
                        chain.link(nc.vector.tensor_tensor(gj, gj, spread(cw, C), ALU.mult))
                        nc.vector.tensor_tensor(g[:, j, :, 0:2, :], g[:, j, :, 0:2, :], g[:, j, :, 2:4, :], ALU.add)\
                            .then_inc(Q["weighted"], 1)
                        if j == 1 and not (first and b == 0):
                            result(*((t, 0) if b else (t - 1, 1)))
                    add_bias(t, b)

            body(0, True, True)
            with dve.Fori(1, BODIES - 1) as t:
                body(t, False, True)
            body(BODIES - 1, False, False)
            result(BODIES - 1, 1)

        @block.tensor
        def _(pe):
            start_counts(pe, [S["offp"]], TWO)
            start_counts(pe, [Q["vtp"]], TB)
            start_counts(pe, [Q["vt_used"]], TB)
            pe.wait_ge(weights, NW * DMA)

            def offsets(t, b):
                pe.wait_ge(win_loaded[b], DMA * (t + 1))
                pe.wait_ge(S["off_read"], steps(t, b - 1))
                for j in range(TILES):
                    r, h = divmod(j, 2)
                    for k in range(TAPS):
                        ky, kx = divmod(k, KW)
                        last = nc.tensor.matmul(off_ps[:, 0, j * T2:(j + 1) * T2],
                                                win[:, b, r + ky, h * P + kx:h * P + kx + P], w_off[:, k, :],
                                                start=(k == 0), stop=(k == TAPS - 1))
                last.then_inc(S["offp"], 1)

            def product(t, b, j):
                pe.wait_ge(Q["vt_ready"], tiles(t, b, j))
                if j == 0:
                    pe.wait_ge(S["xo_ready"], steps(t, b - 1))
                v = (TILES * b + j) % TWO
                for k in range(TAPS):
                    n, i = divmod(k, PER)
                    last = nc.tensor.matmul(out_ps[:, 0, j * C:(j + 1) * C], vt[:, v, n, i * P:(i + 1) * P],
                                            w_k[:, k, :], start=(k == 0), stop=(k == TAPS - 1))
                last.then_inc(Q["vt_used"], 1)

            def tile_sums(t, b, j):
                pe.wait_ge(Q["weighted"], tiles(t, b, j))
                pe.wait_ge(Q["vt_ready"], tiles(t, b, j - TWO))
                v = (TILES * b + j) % TWO
                for k in range(TAPS):
                    n, i = divmod(k, PER)
                    for q in range(2):
                        last = nc.tensor.matmul(vt_ps[:, v * GROUPS + n, i * P:(i + 1) * P], g[:, j, k, q, :],
                                                K.ident[:, :], start=(q == 0), stop=(q == 1))
                last.then_inc(Q["vtp"], 1)

            def body(t, first, more):
                for b in range(TWO):
                    for j in range(TILES):
                        if j == 2 and more:
                            offsets(t + 1, b)
                        tile_sums(t, b, j)
                        if j:
                            product(t, b, j - 1)
                        elif b:
                            product(t, 0, TILES - 1)
                        elif not first:
                            product(t - 1, 1, TILES - 1)

            offsets(0, 0)
            offsets(0, 1)
            body(0, True, True)
            with pe.Fori(1, BODIES - 1) as t:
                body(t, False, True)
            body(BODIES - 1, False, False)
            product(BODIES - 1, 1, TILES - 1)

        @block.scalar
        def _(act):
            start_counts(act, [Q["vt_ready"]], TB)
            with act.Fori(0, BODIES) as t:
                for b in range(TWO):
                    for j in range(TILES):
                        act.wait_ge(Q["vtp"], tiles(t, b, j))
                        act.wait_ge(Q["vt_used"], tiles(t, b, j - TWO))
                        v = (TILES * b + j) % TWO
                        for n in range(GROUPS):
                            last = nc.scalar.activation(vt[:, v, n, :], vt_ps[:, v * GROUPS + n, 0:PER * P], ACT.Copy)
                        last.then_inc(Q["vt_ready"], 1)


def metaformer(nc, a, out):
    with ExitStack() as ctx:
        keep = Phase(nc, ctx, "keep")
        K = Namespace()
        K.ident = keep.sb("ident", [P, P])
        K.minus_half = keep.sb("minus_half", [P, 8])
        K.by_pool = keep.sems("by_pool", 3 * 2 + TILES)
        wx_mv = keep.sb("wx_mv", [P, 2])
        sums = keep.sb("sums", [P, BLOCKS])
        make_constants(nc, K.ident, K.minus_half)

        def dram(name, shape):
            return nc.dram_tensor(name, shape, fp32, kind="Internal").ap()

        x0 = a["x"].rearrange("a h w c -> (a h w) c")
        x_out = out.rearrange("a h w c -> (a h w) c")
        tokens_a = dram("tokens_a", [N, C])
        tokens_b = dram("tokens_b", [N, C])

        l0 = {n: a["L0_conv_" + n] for n in ("ln_gamma", "ln_beta", "Wq", "Wk", "Wv", "Wb", "Wg", "Wout")}
        zt = dram("zt", [C, N])
        att_bias = dram("l0_bias", [HEADS, N])
        attention_front(nc, K, x0, l0["ln_gamma"], l0["ln_beta"], l0["Wb"], zt, att_bias)
        attention(nc, K, x0, zt, att_bias, l0["Wq"], l0["Wk"], l0["Wv"], l0["Wg"], l0["Wout"], tokens_a)
        experts_of = [a["L0_ffn_" + n] for n in ("gate_w", "gate_b", "weight1", "weight2")]
        moe(nc, K, "m0", tokens_a, *experts_of)

        wx = dram("wx", [C, SEQ_BLOCKS, H, SEQ_BLOCK])
        ys = dram("ys", [C, SEQ_BLOCKS, H, SEQ_BLOCK])
        ema_conv(nc, K, tokens_a, a["L1_conv_W_exp"], a["L1_conv_b_exp"], a["L1_conv_W_con"], a["L1_conv_b_con"],
                 a["L1_ffn_W"], tokens_b, wx, wx_mv)
        recurrence(nc, K, wx, wx_mv, a["L1_ffn_gamma"], a["L1_ffn_beta"], a["L1_ffn_V"], ys)

        q = dram("q", [N, C])
        images = [dram(f"context{i}", [C, RING, W]) for i in range(LEVELS)]
        gates = dram("gates", [LEVELS + 1, N])
        acc = [dram(f"acc{i}", [C, N]) for i in range(LEVELS)]
        clear_rows(nc, "clr", images, PAD)
        focal_front(nc, K, tokens_b, ys, a["L2_conv_Wf"], a["L2_conv_bf"], tokens_a, q, images[0], gates)
        depthwise(nc, K, "dw0", 3, 4, images[0], a["L2_conv_k0"], gates, 0, None, images[1], acc[0], None)
        depthwise(nc, K, "dw1", 5, 10, images[1], a["L2_conv_k1"], gates, 1, acc[0], images[2], acc[1], None)
        depthwise(nc, K, "dw2", 7, 20, images[2], a["L2_conv_k2"], gates, 2, acc[1], None, acc[2], sums)
        modulate(nc, K, tokens_a, q, acc[2], gates, sums,
                 *[a["L2_conv_" + n] for n in ("Wh", "bh", "gamma", "beta", "Wp", "bp")], tokens_b)
        experts_of = [a["L2_ffn_" + n] for n in ("gate_w", "gate_b", "weight1", "weight2")]
        moe(nc, K, "m2", tokens_b, *experts_of)

        table = dram("table", [TABLE])
        image = dram("image", [C, H + 2, W])
        clear_rows(nc, "clr3", [image], 1)
        deform_front(nc, K, tokens_b, table, image)
        deform(nc, K, tokens_b, table, image,
               *[a["L3_conv_" + n] for n in ("kernel", "bias", "offset_w", "offset_b")], x_out)
        experts_of = [a["L3_ffn_" + n] for n in ("gate_w", "gate_b", "weight1", "weight2")]
        moe(nc, K, "m3", x_out, *experts_of)


_TRANSPOSED = ("L0_ffn_gate_w", "L2_ffn_gate_w", "L3_ffn_gate_w", "L1_conv_W_exp", "L1_conv_W_con", "L1_ffn_W",
               "L1_ffn_V")


def kernel(**inputs):
    import numpy as _np
    import concourse.bacc as _bacc
    from concourse import mybir as _mybir
    from concourse.bass_utils import run_bass_kernel_spmd as _run

    nc = _bacc.Bacc("TRN2", target_bir_lowering=False, num_devices=1)
    arrays, args = {}, {}
    for name in inputs:
        v = _np.asarray(inputs[name])
        v = _np.ascontiguousarray(v.T if name in _TRANSPOSED else v)
        arrays[f"in_{name}_dram"] = v
        args[name] = nc.dram_tensor(f"in_{name}_dram", v.shape, _mybir.dt.from_np(v.dtype), kind="ExternalInput").ap()
    out = nc.dram_tensor("out_0_dram", (1, H, W, C), _mybir.dt.from_np(_np.dtype("float32")), kind="ExternalOutput").ap()
    metaformer(nc, args, out)
    r = _run(nc, [arrays], core_ids=[0])
    return r.results[0]["out_0_dram"]
```
